# Optimizing a Trainium2 kernel written in Bass

```python
import numpy as np
import jax
import jax.numpy as jnp

def _softmax(x, axis=-1):
    return jax.nn.softmax(x, axis=axis)

def _gelu(x):
    return jax.nn.gelu(x, approximate=True)

def _silu(x):
    return jax.nn.silu(x)

def _sigmoid(x):
    return jax.nn.sigmoid(x)

def _layernorm(x, axis=-1, eps=1e-05):
    m = jnp.mean(x, axis=axis, keepdims=True)
    v = jnp.var(x, axis=axis, keepdims=True)
    return (x - m) / jnp.sqrt(v + eps)

def _scatter_add(tgt, idx, src, axis=0):
    return tgt.at[idx].add(src)

def _segment_sum(src, seg, n):
    return jax.ops.segment_sum(src, seg, n)
kernel_name = 'mk_vit_tower_cls_d2_tok_img768_r4_ee7c51'

def setup_inputs(seed: int=0):
    np.random.seed(seed)
    _w = jnp.asarray

    def _rec_inputs():
        import jax
        import jax.numpy as jnp
        _rk = jax.random.key(seed)
        x = 7.57192e-06 + 1.00007 * jax.random.normal(jax.random.fold_in(_rk, 1), (32, 3, 96, 96), jnp.float32)
        cls_tok = 0.02 * jax.random.normal(jax.random.fold_in(_rk, 5), (1, 1, 192), jnp.float32)
        return (x, cls_tok)
    x, cls_tok = _rec_inputs()

    def _L0_tok_setup():
        import jax, jax.numpy as jnp
        import numpy as np
        PATCH = 16

        def _shift2d(x, shift):
            l, r, t, b = shift
            H, W = (x.shape[2], x.shape[3])
            xp = jnp.pad(x, ((0, 0), (0, 0), (max(t, 0), max(b, 0)), (max(l, 0), max(r, 0))))
            h0 = max(-t, 0)
            w0 = max(-l, 0)
            return xp[:, :, h0:h0 + H, w0:w0 + W]
        key = jax.random.key(seed)
        k1, k2 = jax.random.split(key)
        B, C, H, W = (64, 3, 224, 224)
        dim = 192
        patch_dim = PATCH * PATCH * 5 * C
        x = jax.random.normal(k1, (B, C, H, W), dtype=jnp.float32)
        ln_weight = jnp.ones((patch_dim,), dtype=jnp.float32)
        ln_bias = jnp.zeros((patch_dim,), dtype=jnp.float32)
        proj_weight = jax.random.normal(k2, (dim, patch_dim), dtype=jnp.float32) * patch_dim ** (-0.5)
        proj_bias = jnp.zeros((dim,), dtype=jnp.float32)
        return {'x': x, 'ln_weight': ln_weight, 'ln_bias': ln_bias, 'proj_weight': proj_weight, 'proj_bias': proj_bias}
    _L0_tok_all = _L0_tok_setup()
    _L0_tok_in = {k: v for k, v in _L0_tok_all.items() if k in ('ln_weight', 'ln_bias', 'proj_weight', 'proj_bias')}
    del _L0_tok_all

    def _L0_attn_setup():
        import jax, jax.numpy as jnp
        import numpy as np
        EMBED_DIM = 192
        SEQ_LEN = 256
        BATCH = 32
        ALPHA = 0.99

        def _decay_mask(sl: int, alpha: float) -> jnp.ndarray:
            i = jnp.arange(sl, dtype=jnp.float32)
            diff = i[:, None] - i[None, :]
            return jnp.where(diff >= 0, jnp.float32(alpha) ** diff, 0.0)
        key = jax.random.key(seed)
        k1, k2 = jax.random.split(key)
        x = jax.random.normal(k1, (BATCH, SEQ_LEN, EMBED_DIM), dtype=jnp.float32)
        W_qkv = jax.random.normal(k2, (EMBED_DIM, 3 * EMBED_DIM), dtype=jnp.float32) * EMBED_DIM ** (-0.5)
        b_qkv = jnp.zeros((3 * EMBED_DIM,), dtype=jnp.float32)
        return {'x': x, 'W_qkv': W_qkv, 'b_qkv': b_qkv}
    _L0_attn_all = _L0_attn_setup()
    _L0_attn_in = {k: v for k, v in _L0_attn_all.items() if k in ('W_qkv', 'b_qkv')}
    del _L0_attn_all

    def _L0_ffn_setup():
        import jax, jax.numpy as jnp
        import numpy as np
        DIM = 192
        HEADS = 12
        EXPERTS = 8
        HID = 768
        TOP_K = 2
        LN_EPS = 1e-05

        def _layer_norm(x, g, b):
            mu = x.mean(-1, keepdims=True)
            var = ((x - mu) ** 2).mean(-1, keepdims=True)
            return (x - mu) * jax.lax.rsqrt(var + LN_EPS) * g + b

        def _attention(x, qkv_w, qkv_b, proj_w, proj_b):
            B, N, C = x.shape
            hd = C // HEADS
            qkv = (x @ qkv_w + qkv_b).reshape(B, N, 3, HEADS, hd).transpose(2, 0, 3, 1, 4)
            q, k, v = (qkv[0], qkv[1], qkv[2])
            attn = jax.nn.softmax(jnp.einsum('bhnd,bhmd->bhnm', q, k) * hd ** (-0.5), axis=-1)
            o = jnp.einsum('bhnm,bhmd->bhnd', attn, v).transpose(0, 2, 1, 3).reshape(B, N, C)
            return o @ proj_w + proj_b

        def _moe_mlp(xn, gate_w, w1, b1, w2, b2):
            T = xn.shape[0]
            logits = xn @ gate_w
            top_logits, top_idx = jax.lax.top_k(logits, TOP_K)
            top_gates = jax.nn.softmax(top_logits, axis=-1)
            gates = jnp.zeros((T, EXPERTS), xn.dtype).at[jnp.arange(T)[:, None], top_idx].set(top_gates)
            h = jax.nn.gelu(jnp.einsum('td,edh->teh', xn, w1) + b1, approximate=False)
            y = jnp.einsum('teh,ehd->ted', h, w2) + b2
            return jnp.einsum('ted,te->td', y, gates)
        key = jax.random.key(seed)
        ks = jax.random.split(key, 16)
        s = 0.02
        return {'x': jax.random.normal(ks[0], (8, 196, DIM), jnp.float32), 'ln1_g': jnp.ones((DIM,), jnp.float32), 'ln1_b': jnp.zeros((DIM,), jnp.float32), 'qkv_w': jax.random.normal(ks[1], (DIM, 3 * DIM), jnp.float32) * s, 'qkv_b': jnp.zeros((3 * DIM,), jnp.float32), 'proj_w': jax.random.normal(ks[2], (DIM, DIM), jnp.float32) * s, 'proj_b': jnp.zeros((DIM,), jnp.float32), 'ln2_g': jnp.ones((DIM,), jnp.float32), 'ln2_b': jnp.zeros((DIM,), jnp.float32), 'gate_w': jax.random.normal(ks[3], (DIM, EXPERTS), jnp.float32) * s, 'w1': jax.random.normal(ks[4], (EXPERTS, DIM, HID), jnp.float32) * s, 'b1': jnp.zeros((EXPERTS, HID), jnp.float32), 'w2': jax.random.normal(ks[5], (EXPERTS, HID, DIM), jnp.float32) * s, 'b2': jnp.zeros((EXPERTS, DIM), jnp.float32)}
    _L0_ffn_all = _L0_ffn_setup()
    _L0_ffn_in = {k: v for k, v in _L0_ffn_all.items() if k in ('ln1_g', 'ln1_b', 'qkv_w', 'qkv_b', 'proj_w', 'proj_b', 'ln2_g', 'ln2_b', 'gate_w', 'w1', 'b1', 'w2', 'b2')}
    del _L0_ffn_all

    def _L1_attn_setup():
        import jax, jax.numpy as jnp
        import numpy as np
        N_HEAD = 12
        N_EMBD = 192
        BLOCK = 512
        THETA = 10000.0

        def _rope_tables(head_dim, end, theta=THETA):
            half = head_dim // 2
            freqs = 1.0 / theta ** (jnp.arange(0, head_dim, 2, dtype=jnp.float32) / head_dim)
            t = jnp.arange(end, dtype=jnp.float32)
            ang = jnp.outer(t, freqs)
            return (jnp.cos(ang), jnp.sin(ang))

        def _apply_rope(x, cos, sin):
            B, H, T, hd = x.shape
            xr = x.reshape(B, H, T, hd // 2, 2)
            x0, x1 = (xr[..., 0], xr[..., 1])
            c = cos[None, None, :T, :]
            s = sin[None, None, :T, :]
            o0 = x0 * c - x1 * s
            o1 = x0 * s + x1 * c
            return jnp.stack([o0, o1], axis=-1).reshape(B, H, T, hd)
        key = jax.random.key(seed)
        ks = jax.random.split(key, 9)
        B, T, C = (2, 512, N_EMBD)
        std = 0.02
        return {'x': jax.random.normal(ks[0], (B, T, C), jnp.float32), 'norm_scale': jnp.ones((C,), jnp.float32), 'norm_bias': jnp.zeros((C,), jnp.float32), 'W_attn': jax.random.normal(ks[1], (C, 3 * C), jnp.float32) * std, 'b_attn': jax.random.normal(ks[2], (3 * C,), jnp.float32) * std, 'W_proj': jax.random.normal(ks[3], (C, C), jnp.float32) * std, 'b_proj': jax.random.normal(ks[4], (C,), jnp.float32) * std, 'sinks': jax.random.normal(ks[5], (N_HEAD,), jnp.float32) * 0.5, 'rezero': jax.random.normal(ks[6], (1,), jnp.float32) * 0.1}
    _L1_attn_all = _L1_attn_setup()
    _L1_attn_in = {k: v for k, v in _L1_attn_all.items() if k in ('norm_scale', 'norm_bias', 'W_attn', 'b_attn', 'W_proj', 'b_proj', 'sinks', 'rezero')}
    del _L1_attn_all

    def _L1_ffn_setup():
        import jax, jax.numpy as jnp
        import numpy as np
        B, S, D, F, E = (4, 512, 192, 768, 8)
        key = jax.random.key(seed)
        ks = jax.random.split(key, 5)
        return {'x': jax.random.normal(ks[0], (B, S, D), dtype=jnp.float32), 'Ws': jax.random.normal(ks[1], (D, E), dtype=jnp.float32) * 0.02, 'bs': jnp.zeros((E,), dtype=jnp.float32), 'W1': jax.random.normal(ks[2], (E, D, F), dtype=jnp.float32) * 0.02, 'b1': jnp.zeros((E, F), dtype=jnp.float32), 'W2': jax.random.normal(ks[3], (E, F, D), dtype=jnp.float32) * 0.02, 'b2': jnp.zeros((E, D), dtype=jnp.float32)}
    _L1_ffn_all = _L1_ffn_setup()
    _L1_ffn_in = {k: v for k, v in _L1_ffn_all.items() if k in ('Ws', 'bs', 'W1', 'b1', 'W2', 'b2')}
    del _L1_ffn_all
    return {'x': x, 'cls_tok': cls_tok, 'L0_tok_ln_weight': _L0_tok_in['ln_weight'], 'L0_tok_ln_bias': _L0_tok_in['ln_bias'], 'L0_tok_proj_weight': _L0_tok_in['proj_weight'], 'L0_tok_proj_bias': _L0_tok_in['proj_bias'], 'L0_attn_W_qkv': _L0_attn_in['W_qkv'], 'L0_attn_b_qkv': _L0_attn_in['b_qkv'], 'L0_ffn_ln1_g': _L0_ffn_in['ln1_g'], 'L0_ffn_ln1_b': _L0_ffn_in['ln1_b'], 'L0_ffn_qkv_w': _L0_ffn_in['qkv_w'], 'L0_ffn_qkv_b': _L0_ffn_in['qkv_b'], 'L0_ffn_proj_w': _L0_ffn_in['proj_w'], 'L0_ffn_proj_b': _L0_ffn_in['proj_b'], 'L0_ffn_ln2_g': _L0_ffn_in['ln2_g'], 'L0_ffn_ln2_b': _L0_ffn_in['ln2_b'], 'L0_ffn_gate_w': _L0_ffn_in['gate_w'], 'L0_ffn_w1': _L0_ffn_in['w1'], 'L0_ffn_b1': _L0_ffn_in['b1'], 'L0_ffn_w2': _L0_ffn_in['w2'], 'L0_ffn_b2': _L0_ffn_in['b2'], 'L1_attn_norm_scale': _L1_attn_in['norm_scale'], 'L1_attn_norm_bias': _L1_attn_in['norm_bias'], 'L1_attn_W_attn': _L1_attn_in['W_attn'], 'L1_attn_b_attn': _L1_attn_in['b_attn'], 'L1_attn_W_proj': _L1_attn_in['W_proj'], 'L1_attn_b_proj': _L1_attn_in['b_proj'], 'L1_attn_sinks': _L1_attn_in['sinks'], 'L1_attn_rezero': _L1_attn_in['rezero'], 'L1_ffn_Ws': _L1_ffn_in['Ws'], 'L1_ffn_bs': _L1_ffn_in['bs'], 'L1_ffn_W1': _L1_ffn_in['W1'], 'L1_ffn_b1': _L1_ffn_in['b1'], 'L1_ffn_W2': _L1_ffn_in['W2'], 'L1_ffn_b2': _L1_ffn_in['b2']}

def reference(x, cls_tok, L0_tok_ln_weight, L0_tok_ln_bias, L0_tok_proj_weight, L0_tok_proj_bias, L0_attn_W_qkv, L0_attn_b_qkv, L0_ffn_ln1_g, L0_ffn_ln1_b, L0_ffn_qkv_w, L0_ffn_qkv_b, L0_ffn_proj_w, L0_ffn_proj_b, L0_ffn_ln2_g, L0_ffn_ln2_b, L0_ffn_gate_w, L0_ffn_w1, L0_ffn_b1, L0_ffn_w2, L0_ffn_b2, L1_attn_norm_scale, L1_attn_norm_bias, L1_attn_W_attn, L1_attn_b_attn, L1_attn_W_proj, L1_attn_b_proj, L1_attn_sinks, L1_attn_rezero, L1_ffn_Ws, L1_ffn_bs, L1_ffn_W1, L1_ffn_b1, L1_ffn_W2, L1_ffn_b2):
    import jax
    import jax.numpy as jnp

    def _L0_tok_ref(x, ln_weight, ln_bias, proj_weight, proj_bias):
        import jax, jax.numpy as jnp
        import numpy as np
        PATCH = 16

        def _shift2d(x, shift):
            l, r, t, b = shift
            H, W = (x.shape[2], x.shape[3])
            xp = jnp.pad(x, ((0, 0), (0, 0), (max(t, 0), max(b, 0)), (max(l, 0), max(r, 0))))
            h0 = max(-t, 0)
            w0 = max(-l, 0)
            return xp[:, :, h0:h0 + H, w0:w0 + W]
        shifts = ((1, -1, 0, 0), (-1, 1, 0, 0), (0, 0, 1, -1), (0, 0, -1, 1))
        xc = jnp.concatenate([x] + [_shift2d(x, s) for s in shifts], axis=1)
        B, C5, H, W = xc.shape
        p = PATCH
        h, w = (H // p, W // p)
        t = xc.reshape(B, C5, h, p, w, p)
        t = t.transpose(0, 2, 4, 3, 5, 1).reshape(B, h * w, p * p * C5)
        mu = jnp.mean(t, axis=-1, keepdims=True)
        var = jnp.mean(jnp.square(t - mu), axis=-1, keepdims=True)
        tn = (t - mu) * jax.lax.rsqrt(var + 1e-05) * ln_weight + ln_bias
        return jnp.einsum('bnk,dk->bnd', tn, proj_weight) + proj_bias

    def _L0_attn_ref(x, W_qkv, b_qkv):
        import jax, jax.numpy as jnp
        import numpy as np
        EMBED_DIM = 192
        SEQ_LEN = 256
        BATCH = 32
        ALPHA = 0.99

        def _decay_mask(sl: int, alpha: float) -> jnp.ndarray:
            i = jnp.arange(sl, dtype=jnp.float32)
            diff = i[:, None] - i[None, :]
            return jnp.where(diff >= 0, jnp.float32(alpha) ** diff, 0.0)
        bs, sl, d = x.shape
        qkv = x @ W_qkv + b_qkv
        q, k, v = jnp.split(qkv, 3, axis=-1)
        M = _decay_mask(sl, ALPHA)
        dim_sqrt = jnp.sqrt(jnp.float32(d))
        scores = jnp.einsum('bsd,btd->bst', q, k) / dim_sqrt * M
        return jnp.einsum('bst,btd->bsd', scores, v)

    def _L0_ffn_ref(x, ln1_g, ln1_b, qkv_w, qkv_b, proj_w, proj_b, ln2_g, ln2_b, gate_w, w1, b1, w2, b2):
        import jax, jax.numpy as jnp
        import numpy as np
        DIM = 192
        HEADS = 12
        EXPERTS = 8
        HID = 768
        TOP_K = 2
        LN_EPS = 1e-05

        def _layer_norm(x, g, b):
            mu = x.mean(-1, keepdims=True)
            var = ((x - mu) ** 2).mean(-1, keepdims=True)
            return (x - mu) * jax.lax.rsqrt(var + LN_EPS) * g + b

        def _attention(x, qkv_w, qkv_b, proj_w, proj_b):
            B, N, C = x.shape
            hd = C // HEADS
            qkv = (x @ qkv_w + qkv_b).reshape(B, N, 3, HEADS, hd).transpose(2, 0, 3, 1, 4)
            q, k, v = (qkv[0], qkv[1], qkv[2])
            attn = jax.nn.softmax(jnp.einsum('bhnd,bhmd->bhnm', q, k) * hd ** (-0.5), axis=-1)
            o = jnp.einsum('bhnm,bhmd->bhnd', attn, v).transpose(0, 2, 1, 3).reshape(B, N, C)
            return o @ proj_w + proj_b

        def _moe_mlp(xn, gate_w, w1, b1, w2, b2):
            T = xn.shape[0]
            logits = xn @ gate_w
            top_logits, top_idx = jax.lax.top_k(logits, TOP_K)
            top_gates = jax.nn.softmax(top_logits, axis=-1)
            gates = jnp.zeros((T, EXPERTS), xn.dtype).at[jnp.arange(T)[:, None], top_idx].set(top_gates)
            h = jax.nn.gelu(jnp.einsum('td,edh->teh', xn, w1) + b1, approximate=False)
            y = jnp.einsum('teh,ehd->ted', h, w2) + b2
            return jnp.einsum('ted,te->td', y, gates)
        B, N, C = x.shape
        x = x + _attention(_layer_norm(x, ln1_g, ln1_b), qkv_w, qkv_b, proj_w, proj_b)
        xn = _layer_norm(x, ln2_g, ln2_b).reshape(B * N, C)
        moe_out = _moe_mlp(xn, gate_w, w1, b1, w2, b2).reshape(B, N, C)
        return x + moe_out

    def _L1_attn_ref(x, norm_scale, norm_bias, W_attn, b_attn, W_proj, b_proj, sinks, rezero):
        import jax, jax.numpy as jnp
        import numpy as np
        N_HEAD = 12
        N_EMBD = 192
        BLOCK = 512
        THETA = 10000.0

        def _rope_tables(head_dim, end, theta=THETA):
            half = head_dim // 2
            freqs = 1.0 / theta ** (jnp.arange(0, head_dim, 2, dtype=jnp.float32) / head_dim)
            t = jnp.arange(end, dtype=jnp.float32)
            ang = jnp.outer(t, freqs)
            return (jnp.cos(ang), jnp.sin(ang))

        def _apply_rope(x, cos, sin):
            B, H, T, hd = x.shape
            xr = x.reshape(B, H, T, hd // 2, 2)
            x0, x1 = (xr[..., 0], xr[..., 1])
            c = cos[None, None, :T, :]
            s = sin[None, None, :T, :]
            o0 = x0 * c - x1 * s
            o1 = x0 * s + x1 * c
            return jnp.stack([o0, o1], axis=-1).reshape(B, H, T, hd)
        B, T, C = x.shape
        H = N_HEAD
        hd = C // H
        xn = norm_scale * x + norm_bias
        qkv = xn @ W_attn + b_attn
        q, k, v = jnp.split(qkv, 3, axis=-1)
        q = q.reshape(B, T, H, hd).transpose(0, 2, 1, 3)
        k = k.reshape(B, T, H, hd).transpose(0, 2, 1, 3)
        v = v.reshape(B, T, H, hd).transpose(0, 2, 1, 3)
        cos, sin = _rope_tables(hd, T)
        q = _apply_rope(q, cos, sin)
        k = _apply_rope(k, cos, sin)
        scale = 1.0 / jnp.sqrt(jnp.float32(hd))
        att = jnp.einsum('bhqd,bhkd->bhqk', q, k) * scale
        causal = jnp.tril(jnp.ones((T, T), dtype=bool))
        att = jnp.where(causal[None, None], att, -jnp.inf)
        sink_col = jnp.broadcast_to(sinks.reshape(1, H, 1, 1), (B, H, T, 1))
        att = jnp.concatenate([sink_col, att], axis=-1)
        att = jax.nn.softmax(att, axis=-1)[..., 1:]
        y = jnp.einsum('bhqk,bhkd->bhqd', att, v)
        y = y.transpose(0, 2, 1, 3).reshape(B, T, C)
        y = (y @ W_proj + b_proj) * rezero
        return y

    def _L1_ffn_ref(x, Ws, bs, W1, b1, W2, b2):
        import jax, jax.numpy as jnp
        import numpy as np
        B, S, D, F, E = (4, 512, 192, 768, 8)
        b, s, d = x.shape
        xt = x.reshape(-1, d)
        logits = xt @ Ws + bs
        probs = jax.nn.softmax(logits, axis=-1)
        routes = jnp.argmax(probs, axis=-1)
        prob_max = jnp.max(probs, axis=-1)
        h = jax.nn.gelu(jnp.einsum('td,edf->etf', xt, W1) + b1[:, None, :], approximate=False)
        y = jnp.einsum('etf,efd->etd', h, W2) + b2[:, None, :]
        out = jnp.take_along_axis(y, routes[None, :, None], axis=0)[0]
        out = out * prob_max[:, None]
        return out.reshape(b, s, d)
    h = _L0_tok_ref(x, L0_tok_ln_weight, L0_tok_ln_bias, L0_tok_proj_weight, L0_tok_proj_bias)
    h = jnp.concatenate([jnp.broadcast_to(cls_tok, (h.shape[0], 1, h.shape[2])), h], axis=1)
    h = h + _L0_attn_ref(_layernorm(h, axis=-1), L0_attn_W_qkv, L0_attn_b_qkv)
    h = h + _L0_ffn_ref(_layernorm(h, axis=-1), L0_ffn_ln1_g, L0_ffn_ln1_b, L0_ffn_qkv_w, L0_ffn_qkv_b, L0_ffn_proj_w, L0_ffn_proj_b, L0_ffn_ln2_g, L0_ffn_ln2_b, L0_ffn_gate_w, L0_ffn_w1, L0_ffn_b1, L0_ffn_w2, L0_ffn_b2)
    h = h + _L1_attn_ref(_layernorm(h, axis=-1), L1_attn_norm_scale, L1_attn_norm_bias, L1_attn_W_attn, L1_attn_b_attn, L1_attn_W_proj, L1_attn_b_proj, L1_attn_sinks, L1_attn_rezero)
    h = h + _L1_ffn_ref(_layernorm(h, axis=-1), L1_ffn_Ws, L1_ffn_bs, L1_ffn_W1, L1_ffn_b1, L1_ffn_W2, L1_ffn_b2)
    return h

_drawn_inputs = setup_inputs


def setup_inputs(seed=0):
    import zlib

    import numpy as np

    out = dict(_drawn_inputs(seed))
    spreads = {'L0_tok_ln_weight': (1.0, 0.2),
     'L0_tok_ln_bias': (0.0, 0.1),
     'L0_tok_proj_bias': (0.0, 0.1),
     'L0_attn_b_qkv': (0.0, 0.1),
     'L0_ffn_ln1_g': (1.0, 0.6),
     'L0_ffn_ln1_b': (0.0, 0.8),
     'L0_ffn_qkv_b': (0.0, 0.8),
     'L0_ffn_proj_b': (0.0, 0.401),
     'L0_ffn_ln2_g': (1.0, 0.6),
     'L0_ffn_ln2_b': (0.0, 0.8),
     'L0_ffn_b1': (0.0, 0.8),
     'L0_ffn_b2': (0.0, 0.588),
     'L1_attn_norm_scale': (1.0, 0.6),
     'L1_attn_norm_bias': (0.0, 0.8),
     'L1_ffn_bs': (0.0, 0.8),
     'L1_ffn_b1': (0.0, 0.8),
     'L1_ffn_b2': (0.0, 0.8)}
    factors = {'L0_ffn_qkv_w': 8.0,
     'L0_ffn_proj_w': 8.0,
     'L0_ffn_gate_w': 3.674,
     'L0_ffn_w1': 4.988,
     'L0_ffn_w2': 4.583,
     'L1_attn_W_attn': 8.0,
     'L1_attn_b_attn': 8.0,
     'L1_attn_W_proj': 8.0,
     'L1_attn_b_proj': 37.475,
     'L1_attn_sinks': 24.518,
     'L1_ffn_Ws': 8.0,
     'L1_ffn_W1': 8.0,
     'L1_ffn_W2': 8.0}
    for name, (base, spread) in spreads.items():
        noise = np.random.default_rng([zlib.crc32(name.encode()), seed]).standard_normal(out[name].shape)
        drawn = base * np.exp(spread * noise) if base else spread * noise
        out[name] = jnp.asarray(drawn.astype(out[name].dtype))
    for name, factor in factors.items():
        out[name] = (out[name] * factor).astype(out[name].dtype)
    return out
```

```python
from contextlib import ExitStack

import numpy as np

import concourse.bass as bass
from concourse import mybir

F32 = mybir.dt.float32
BF16 = mybir.dt.bfloat16
ALU = mybir.AluOpType
ACT = mybir.ActivationFunctionType
AX = mybir.AxisListType

B, C, IMG, PATCH = 32, 3, 96, 16
D = 192
N = (IMG // PATCH) ** 2 + 1
T = B * N
R = 3 * N
TILES = -(-T // R)
TAIL = T - (TILES - 1) * R
PAIRS = (TILES - 1) // 2
KD = 96
H, HD = 12, 16
HP = 32
HC = H * HP // 128
EXPERTS, FF = 8, 768
FB = FF // 128
SHIFTS = ((0, 0), (0, -1), (0, 1), (-1, 0), (1, 0))
HALO = PATCH + 2
SPOTS = [(i, j) for i in range(HALO) for j in range(HALO)
         if not (i in (0, HALO - 1) and j in (0, HALO - 1))]
KT = C * len(SPOTS)
TC = 8
TP = KT // TC
PD = PATCH * PATCH * 5 * C
EPS = 1e-5
CHUNK = 4
CHUNKS = [range(a, min(a + CHUNK, TILES)) for a in range(0, TILES, CHUNK)]
PER_PASS = (12, 14)


def rows(t):
    return TAIL if t == TILES - 1 else R


def build(nc, a, out):
    with ExitStack() as ctx:
        def sb(name, shape, dt=F32):
            return ctx.enter_context(nc.sbuf_tensor(name, shape, dt))

        def pb(name, shape, dt=F32):
            return ctx.enter_context(nc.psum_tensor(name, shape, dt))

        def sem(name):
            return ctx.enter_context(nc.semaphore(name))

        ident = sb("ident", [128, 128])
        identb = sb("identb", [R, R], BF16)
        blockmask = sb("blockmask", [R, 3, R], BF16)
        causal_q = sb("causal_q", [R, 3, R], BF16)
        causal_k = sb("causal_k", [R, 3, R], BF16)
        decay = sb("decay", [R, R])
        count = sb("count", [R, KT])
        rootcount = sb("rootcount", [R, KT])
        shared = sb("shared", [128, max(5 * TC * D, 2 * FB * CHUNK * R)])
        wsh = shared[0:TP, 0:5 * TC * D].rearrange("p (s c d) -> p s c d", s=5, c=TC)
        gsh = sb("gsh", [TP, 5, TC])
        bsh = sb("bsh", [TP, 5, TC])
        etok = sb("etok", [TP, TC, D])
        clsrow = sb("clsrow", [1, D])
        tokbias = sb("tokbias", [1, D])
        tokrow = sb("tokrow", [1, D])
        roles = sb("roles", [1, 2, R])
        base = sb("base", [R, D])
        w_a = sb("w_a", [KD, 2, 3 * D])
        bqk_a = sb("bqk_a", [KD, 4])
        bv_a = sb("bv_a", [R, D])
        ropecos = sb("ropecos", [R, HD])
        ropesin = sb("ropesin", [R, HD])
        W = []
        for l in range(2):
            W.append(dict(
                qkv=sb(f"qkv{l}", [KD, 2, 3 * D]), bqkv=sb(f"bqkv{l}", [R, 3 * D]),
                gain=sb(f"gain{l}", [KD, 2]), shift=sb(f"shift{l}", [KD, 2]),
                proj=sb(f"proj{l}", [KD, 2, D]), bproj=sb(f"bproj{l}", [R, D]),
                gate=sb(f"gate{l}", [KD, 2, EXPERTS]),
                b2=sb(f"b2_{l}", [EXPERTS, D]),
            ))
        gain2 = sb("gain2", [KD, 2])
        shift2 = sb("shift2", [KD, 2])
        sinks = sb("sinks", [R, H])
        rezero = sb("rezero", [R, 1])
        bs = sb("bs", [R, 2, EXPERTS])

        h = sb("h", [R, TILES, D])
        xT = sb("xT", [KD, 2, T])
        logits = sb("logits", [R, TILES, EXPERTS])
        gates = sb("gates", [R, TILES, EXPERTS])
        earlier = sb("earlier", [R, EXPERTS, EXPERTS])
        cmp = sb("cmp", [R, TILES, EXPERTS, EXPERTS])
        cmq = sb("cmq", [R, TILES, EXPERTS, EXPERTS])
        masks = cmp[:].rearrange("r t e f -> r (t e f)")[:, 0:3 * R].rearrange("r (k n) -> r k n", k=3)
        rank = sb("rank", [R, TILES, EXPERTS])
        top = sb("top", [R, TILES])
        gsum = sb("gsum", [R, TILES])
        gatesT = sb("gatesT", [EXPERTS, T])
        w1 = sb("w1", [KD, 2, 2, FF])
        w2 = sb("w2", [128, 2, FB, D])
        b1 = sb("b1", [128, 2, FB])
        hid = shared[:, 0:2 * FB * CHUNK * R].rearrange("p (k b n) -> p k b n", k=2, b=FB)
        def slots(name, shape, dt=F32):
            return [sb(f"{name}_{p}", shape, dt) for p in range(2)]

        xin = slots("xin", [R, KT])
        zin = slots("zin", [R, KT])
        yT = slots("yT", [TP, TC, R])
        small = slots("small", [R, 16])
        stats = slots("stats", [R, 6])
        minushalf = sb("minushalf", [R, 2])
        xn = slots("xn", [R, D])
        xnT = slots("xnT", [KD, 2, R])
        qkT_a = slots("qkT_a", [KD, 4, R])
        v_a = slots("v_a", [R, D])
        sT_a = slots("sT_a", [R, R])
        x1 = slots("x1", [R, D])
        x1b = slots("x1b", [R, D])
        qk = slots("qk", [R, 2 * H, HD])
        rot = slots("rot", [R, 2 * H, HD])
        rot2 = slots("rot2", [R, 2 * H, HD])
        qkpad = slots("qkpad", [R, 2, H, HP])
        vone = slots("vone", [R, H, HD + 1])
        kT = slots("kT", [128, HC, R])
        qT = slots("qT", [128, HC, R])
        qTm = slots("qTm", [128, HC, R])
        e = slots("e", [R, 4, HC, R])
        negmax = slots("negmax", [R, H])
        den = slots("den", [R, H])
        o = slots("o", [R, H, HD])
        oT = slots("oT", [KD, 2, R])

        ps = [pb(f"ps{i}", [128, 2, 512]) for i in range(2)]
        pm = [pb(f"pm{i}", [128, 2, 512]) for i in range(2)]

        tok_in = sem("tok_in")
        rest_in = sem("rest_in")
        etok_done = sem("etok_done")
        tokrow_mm, tokrow_done, base_mm, base_done = (sem(x) for x in
                                                      ("tokrow_mm", "tokrow_done", "base_mm", "base_done"))
        pads_set, masks_cast = sem("pads_set"), sem("masks_cast")
        x_in = [sem(f"x_in{p}") for p in range(2)]
        def sems(names, tag=""):
            return {n: sem(n + tag) for n in names.split()}

        A = sems("centred weighted squared tok_var tok_root stats_done var_ready root_done tok_turned tok_evac_act tok_evac_dve tok_mm h0_done normed turned "
                 "xnT_done qkv_mm qkv_done score_mm score_done out_mm h1_done", "_a")
        L = [sems("stats_done stats_done2 var_ready root_done var_ready2 root_done2 normed turned xnT_done qkv_mm qk_added swapped qk_done v_done qk_turned kT_done qT_done "
                  "score_mm max_done negmax_done sink_exp q_turned qTm_done scoreT_mm exp_done pv_mm o_done "
                  "o_turned oT_done proj_mm x1_done x1b_done y_done normed2 turned2 xnT2_done logit_mm logit_done "
                  "xT_done h_added", f"_{l}") for l in range(2)]
        M = [sems("gates_shifted gates_exp gates_done gatesT_mm gatesT_done up_mm gelu_done down_mm y_added",
                  f"_m{l}") for l in range(2)]
        w_in = [[sem(f"w_in_{l}{p}") for p in range(2)] for l in range(2)]
        dve_step = sem("dve_step")
        pool_step = sem("pool_step")
        out_done = sem("out_done")

        HID_BANKS = 4
        Y_CREDIT = 3
        DOWN_CREDIT = 4
        per_expert = TILES
        FIRST = TILES

        block = ctx.enter_context(nc.Block())

        def cols(t, n):
            return slice(t * R, t * R + n) if isinstance(t, int) else bass.ds(t * R, R)

        def hrow(t, n):
            return h[0:n, t, :] if isinstance(t, int) else h[0:n, bass.ds(t, 1), :].rearrange("p o d -> p (o d)")

        def pair(i):
            return [(0, i * 2, R, i + 1), (1, i * 2 + 1, R, i + 1)]

        LAST = [(0, TILES - 1, TAIL, PAIRS + 1)]

        class Steps:

            def __init__(self, eng, s):
                self.eng, self.s, self.base, self.n, self.i, self.per = eng, s, 0, 0, None, 0

            def enter(self, i, per):
                self.base, self.n, self.i, self.per = self.base + self.n, 0, i, per

            def leave(self, passes):
                assert self.n == self.per, (self.n, self.per)
                self.base, self.n, self.i = self.base + passes * self.per, 0, None

            def did(self, ins):
                ins.then_inc(self.s, 1)
                self.n += 1
                return self.n

            def after(self, n):
                v = self.base + n
                self.eng.wait_ge(self.s, v if self.i is None else self.i * self.per + v)

        def two(buf, bank, parts, n):
            return buf[0:parts, bank, 0:2 * R].rearrange("p (c n) -> p c n", c=2)[:, :, 0:n]

        def three(buf, bank, n, parts=128):
            return buf[0:parts, bank, 0:HC * R].rearrange("p (c n) -> p c n", c=HC)[:, :, 0:n]

        def scores(half, n):
            return ps[half][0:n, :, 0:HC * R].rearrange("p r (c n) -> p r c n", c=HC)[:, :, :, 0:n]

        tok_loads = [(count[:], a["c_count"].partition_broadcast(R)), (gsh[:], a["gsh"]), (bsh[:], a["bsh"])]
        tok_loads += [(wsh[:, s], a["wsh"][:, s]) for s in range(5)]
        tok_loads += [(rootcount[:], a["c_rootcount"].partition_broadcast(R)), (ident[:], a["c_ident"]),
                      (roles[:], a["c_roles"]), (clsrow[:], a["cls_tok"]), (tokbias[:], a["tok_bias"])]
        rest_loads = [
            (w_a[:], a["L0_attn_W_qkv"].rearrange("(c p) n -> p c n", p=KD)), (bqk_a[:], a["attn_bqk"]),
            (bv_a[:], a["attn_bv"].partition_broadcast(R)), (decay[:], a["c_decay"]), (masks[:], a["c_masks"])]
        for l in range(2):
            w = W[l]
            rest_loads += [
                (w["qkv"][:], a[f"qkv{l}"].rearrange("(c p) n -> p c n", p=KD)),
                (w["bqkv"][:], a[f"bqkv{l}"].partition_broadcast(R)), (w["gain"][:], a[f"gain{l}"]),
                (w["shift"][:], a[f"shift{l}"]), (w["proj"][:], a[f"proj{l}"].rearrange("(c p) n -> p c n", p=KD)),
                (w["bproj"][:], a[f"bproj{l}"].partition_broadcast(R)),
                (w["gate"][:], a[f"gate{l}"].rearrange("(c p) n -> p c n", p=KD)),
                (w["b2"][:], a[f"b2_{l}"])]
        rest_loads += [(gain2[:], a["gain2"]), (shift2[:], a["shift2"]), (ropecos[:], a["c_cos"]),
                       (ropesin[:], a["c_sin"]), (sinks[:], a["sinks"].partition_broadcast(R)),
                       (rezero[:], a["rezero"].partition_broadcast(R)), (bs[:], a["bs"].partition_broadcast(R)),
                       (earlier[:], a["c_earlier"].partition_broadcast(R))]
        TOK_IN, REST_IN = 16 * len(tok_loads), 16 * len(rest_loads)

        @block.sync
        def _(sp):
            for dst, src in tok_loads:
                sp.dma_start(dst, src).then_inc(tok_in, 16)
            for dst, src in rest_loads:
                sp.dma_start(dst, src).then_inc(rest_in, 16)

            def load_expert(l, p, ex):
                one = slice(ex, ex + 1) if isinstance(ex, int) else bass.ds(ex, 1)
                sp.dma_start(w1[:, p], a[f"w1_{l}"][one].rearrange("o (c p) n -> p (o c) n", p=KD)
                             ).then_inc(w_in[l][p], 16)
                sp.dma_start(w2[:, p], a[f"w2_{l}"][one].rearrange("o (b p) n -> p (o b) n", p=128)
                             ).then_inc(w_in[l][p], 16)
                sp.dma_start(b1[:, p], a[f"b1_{l}"][one].rearrange("o p b -> p (o b)")).then_inc(w_in[l][p], 16)

            for l in range(2):
                if l == 1:
                    sp.wait_ge(M[0]["down_mm"], DOWN_CREDIT + FIRST + per_expert * EXPERTS)
                for p in range(2):
                    load_expert(l, p, p)
                with sp.Fori(0, EXPERTS // 2 - 1) as i:
                    for p in range(2):
                        sp.wait_ge(M[l]["down_mm"], i * (2 * per_expert) + (DOWN_CREDIT + FIRST + (p + 1) * per_expert))
                        load_expert(l, p, i * 2 + (2 + p))
            sp.wait_ge(M[1]["y_added"], Y_CREDIT + FIRST + per_expert * EXPERTS)
            full = (TILES - 1) * R
            sp.dma_start(out[0:full, :].rearrange("(t p) d -> p t d", p=R), h[:, 0:TILES - 1, :]
                         ).then_inc(out_done, 16)
            sp.dma_start(out[full:T, :], h[0:TAIL, TILES - 1, :]).then_inc(out_done, 16)
            sp.wait_ge(out_done, 32)

        @block.scalar
        def _(act):
            def copy(dst, src):
                return nc.scalar.activation(dst, src, ACT.Copy)

            def affine(dst, src, gain, shift, n):
                for c in range(2):
                    last = nc.scalar.activation(dst[:, c, 0:n], src[:, c, 0:n], ACT.Identity,
                                                bias=shift[:, c:c + 1], scale=gain[:, c:c + 1])
                return last

            def tokens(tiles):
                for p, t, n, _ in tiles:
                    act.wait_ge(A["weighted"], t + 1)
                    nc.scalar.activation(zin[p][0:n], zin[p][0:n], ACT.Square,
                                         accum_out=small[p][0:n, 7:8]).then_inc(A["squared"], 1)
                for p, t, n, _ in tiles:
                    act.wait_ge(A["tok_turned"], t + 1)
                    copy(yT[p][:, 0:4, 0:n], pm[p][0:TP, 0, 0:4 * R].rearrange("p (c n) -> p c n", c=4)[:, :, 0:n]
                         ).then_inc(A["tok_evac_act"], 1)

            def decay_attention(tiles):
                for p, t, n, _ in tiles:
                    act.wait_ge(A["turned"], t + 1)
                    copy(xnT[p][:, :, 0:n], two(pm[p], 0, KD, n)).then_inc(A["xnT_done"], 1)

            def heads_attention(l, tiles):
                s, w = L[l], W[l]
                for p, t, n, _ in tiles:
                    act.wait_ge(s["turned"], t + 1)
                    affine(xnT[p], two(pm[p], 0, KD, n), w["gain"], w["shift"], n).then_inc(s["xnT_done"], 1)
                for p, t, n, _ in tiles:
                    act.wait_ge(s["qk_turned"], t + 1)
                    copy(kT[p][:, :, 0:n], three(pm[p], 0, n)).then_inc(s["kT_done"], 1)
                if l == 1:
                    for p, t, n, _ in tiles:
                        act.wait_ge(s["negmax_done"], t + 1)
                        nc.scalar.activation(den[p][0:n], den[p][0:n], ACT.Exp, scale=HD ** -0.5
                                             ).then_inc(s["sink_exp"], 1)
                for p, t, n, _ in tiles:
                    act.wait_ge(s["q_turned"], t + 1)
                    copy(qTm[p][:, :, 0:n], three(pm[p], 1, n)).then_inc(s["qTm_done"], 1)
                for p, t, n, _ in tiles:
                    for half in range(2):
                        act.wait_ge(s["scoreT_mm"], t * 2 + (half + 1))
                        nc.scalar.activation(e[p][0:n, 2 * half:2 * half + 2, :, 0:n], scores(half, n), ACT.Exp,
                                             scale=HD ** -0.5).then_inc(s["exp_done"], 1)
                for p, t, n, _ in tiles:
                    act.wait_ge(s["o_turned"], t + 1)
                    copy(oT[p][:, :, 0:n], two(pm[p], 1, KD, n)).then_inc(s["oT_done"], 1)
                for p, t, n, _ in tiles:
                    act.wait_ge(s["turned2"], t + 1)
                    if l == 0:
                        last = affine(xnT[p], two(pm[p], 1, KD, n), gain2, shift2, n)
                    else:
                        last = copy(xnT[p][:, :, 0:n], two(pm[p], 1, KD, n))
                    last.then_inc(s["xnT2_done"], 1)

            def experts(l):
                m = M[l]
                act.wait_ge(m["gates_shifted"], 1)
                nc.scalar.activation(gates[:], gates[:], ACT.Exp).then_inc(m["gates_exp"], 1)
                act.sem_inc(m["gelu_done"], HID_BANKS)
                with act.Fori(0, EXPERTS // 2) as i:
                    for p in range(2):
                        for k, tiles in enumerate(CHUNKS):
                            step = p * len(CHUNKS) + k
                            used = FIRST + p * per_expert + (-3, 0, 4)[k] + DOWN_CREDIT
                            act.wait_ge(m["down_mm"], i * (2 * per_expert) + used)
                            n = sum(rows(t) for t in tiles)
                            for b in range(FB):
                                u = step * FB + b
                                act.wait_ge(m["up_mm"], i * (6 * FB) + (u + 1))
                                nc.scalar.activation(hid[:, step % 2, b, 0:n], ps[u % 4 // 2][:, u % 2, 0:n],
                                                     ACT.Gelu, bias=b1[:, p, b:b + 1]
                                                     ).then_inc(m["gelu_done"], 1)

            for p in range(2):
                act.dma_start(xin[p][:], a["x"][p * R:(p + 1) * R, :]).then_inc(x_in[p], 16)
            act.wait_ge(rest_in, REST_IN)
            with act.Fori(0, PAIRS - 1) as i:
                tokens(pair(i))
                for p, t, n, _ in pair(i):
                    act.dma_start(xin[p][:], a["x"][bass.ds((t + 2) * R, R), :]).then_inc(x_in[p], 16)
                decay_attention(pair(i))
                heads_attention(0, pair(i))
            tokens(pair(PAIRS - 1))
            act.dma_start(xin[0][0:TAIL], a["x"][(TILES - 1) * R:T, :]).then_inc(x_in[0], 16)
            decay_attention(pair(PAIRS - 1))
            heads_attention(0, pair(PAIRS - 1))
            tokens(LAST)
            decay_attention(LAST)
            heads_attention(0, LAST)
            experts(0)
            with act.Fori(0, PAIRS) as i:
                heads_attention(1, pair(i))
            heads_attention(1, LAST)
            experts(1)

        @block.gpsimd
        def _(pool):
            for p in range(2):
                nc.gpsimd.memset(qkpad[p][:], 0.0).then_inc(pool_step, 1)
                nc.gpsimd.memset(vone[p][:], 1.0).then_inc(pads_set, 1)
            nc.gpsimd.memset(logits[:], 0.0).then_inc(pads_set, 1)
            nc.gpsimd.memset(minushalf[:], -0.5).then_inc(pool_step, 1)
            pool.wait_ge(pool_step, 3)
            for p in range(2):
                nc.gpsimd.memset(qkpad[p][:, 1, :, HD:HD + 1], 1.0).then_inc(pads_set, 1)
            pool.wait_ge(tok_in, TOK_IN)
            pool.wait_ge(rest_in, REST_IN)

            def root(tiles, ready, done, src, dst, k=1):
                for p, t, n, _ in tiles:
                    pool.wait_ge(ready, t + 1)
                    nc.gpsimd.tensor_tensor(small[p][0:n, dst:dst + k], small[p][0:n, src:src + k],
                                            minushalf[0:n, 0:k], ALU.pow).then_inc(done, 1)

            def tokens(tiles):
                for p, t, n, _ in tiles:
                    pool.wait_ge(A["centred"], t + 1)
                    nc.gpsimd.tensor_tensor(zin[p][0:n], xin[p][0:n], rootcount[0:n], ALU.mult
                                            ).then_inc(A["weighted"], 1)
                root(tiles, A["tok_var"], A["tok_root"], 8, 9)
                root(tiles, A["var_ready"], A["root_done"], 2, 4)

            def heads_attention(l, tiles):
                s = L[l]
                root(tiles, s["var_ready"], s["root_done"], 2, 4, 2 - l)
                if l == 0:
                    for p, t, n, _ in tiles:
                        pool.wait_ge(s["x1_done"], t + 1)
                        nc.gpsimd.tensor_tensor(x1b[p][0:n], x1[p][0:n], W[0]["bproj"][0:n], ALU.add
                                                ).then_inc(s["x1b_done"], 1)
                else:
                    for p, t, n, _ in tiles:
                        pool.wait_ge(s["qk_added"], t + 1)
                        for c in range(2):
                            last = nc.gpsimd.tensor_tensor(
                                rot2[p][0:n, :, c::2], qk[p][0:n, :, 1 - c::2],
                                ropesin[0:n, c::2].unsqueeze(1).to_broadcast((n, 2 * H, HD // 2)), ALU.mult)
                            last.then_inc(s["swapped"], 1)
                root(tiles, s["var_ready2"], s["root_done2"], 2, 4)
                if l == 0:
                    for p, t, n, _ in tiles:
                        pool.wait_ge(s["y_done"], t + 1)
                        nc.gpsimd.tensor_tensor(hrow(t, n), hrow(t, n), x1[p][0:n], ALU.add
                                                ).then_inc(s["h_added"], 1)
                for p, t, n, _ in tiles:
                    pool.wait_ge(s["xnT2_done"], t + 1)
                    nc.gpsimd.tensor_copy(xT[:, :, cols(t, n)], xnT[p][:, :, 0:n]).then_inc(s["xT_done"], 1)

            with pool.Fori(0, PAIRS) as i:
                tokens(pair(i))
                heads_attention(0, pair(i))
            tokens(LAST)
            heads_attention(0, LAST)
            with pool.Fori(0, PAIRS) as i:
                heads_attention(1, pair(i))
            heads_attention(1, LAST)

        @block.vector
        def _(dve):
            V = nc.vector
            st = Steps(dve, dve_step)

            def alone():
                dve.wait_ge(pads_set, 5)

            def row_stats(tiles, src, ready, stats_done, done):
                at = {}
                for p, t, n, _ in tiles:
                    alone()
                    dve.wait_ge(ready, t + 1)
                    V.bn_stats(stats[p][0:n], src(p, t, n)).then_inc(stats_done, 1)
                for p, t, n, _ in tiles:
                    alone()
                    dve.wait_ge(stats_done, t + 1)
                    at[p] = st.did(V.bn_aggr(small[p][0:n, 0:2], stats[p][0:n]))
                for p, t, n, _ in tiles:
                    st.after(at[p])
                    ins = V.tensor_scalar(small[p][0:n, 2:3], small[p][0:n, 1:2], EPS, None, ALU.add)
                    if done is None:
                        at[p] = st.did(ins)
                    else:
                        ins.then_inc(done, 1)
                return at

            def normalise(tiles, src, dst, ready, stats_done, var_ready, root_done, done):
                row_stats(tiles, src, ready, stats_done, var_ready)
                for p, t, n, _ in tiles:
                    dve.wait_ge(root_done, t + 1)
                    V.tensor_scalar(dst[p][0:n], src(p, t, n), small[p][0:n, 0:1], small[p][0:n, 4:5],
                                    ALU.subtract, ALU.mult).then_inc(done, 1)

            def from_h(p, t, n):
                return hrow(t, n)

            def tokens(tiles):
                at = {}
                for p, t, n, loads in tiles:
                    dve.wait_ge(x_in[p], loads * 16)
                    at[p] = st.did(V.tensor_tensor_reduce(zin[p][0:n], xin[p][0:n], count[0:n], 1.0 / PD, 0.0,
                                                          ALU.mult, ALU.add, small[p][0:n, 6:7]))
                for p, t, n, _ in tiles:
                    st.after(at[p])
                    V.tensor_scalar(xin[p][0:n], xin[p][0:n], small[p][0:n, 6:7], None, ALU.subtract
                                    ).then_inc(A["centred"], 1)
                for p, t, n, _ in tiles:
                    dve.wait_ge(A["tok_turned"], t + 1)
                    V.tensor_copy(yT[p][:, 4:8, 0:n], pm[p][0:TP, 1, 0:4 * R].rearrange(
                        "p (c n) -> p c n", c=4)[:, :, 0:n]).then_inc(A["tok_evac_dve"], 1)
                for p, t, n, _ in tiles:
                    dve.wait_ge(A["squared"], t + 1)
                    V.tensor_scalar(small[p][0:n, 8:9], small[p][0:n, 7:8], EPS, None, ALU.add
                                    ).then_inc(A["tok_var"], 1)
                for p, t, n, _ in tiles:
                    dve.wait_ge(A["tok_root"], t + 1)
                    dve.wait_ge(A["tok_mm"], t + 1)
                    V.scalar_tensor_tensor(hrow(t, n), pm[p][0:n, 0, 0:D], small[p][0:n, 9:10], base[0:n],
                                           ALU.mult, ALU.add).then_inc(A["h0_done"], 1)

            def decay_attention(tiles):
                normalise(tiles, from_h, xn, A["h0_done"], A["stats_done"], A["var_ready"], A["root_done"], A["normed"])
                for p, t, n, _ in tiles:
                    dve.wait_ge(A["qkv_mm"], t + 1)
                    V.tensor_tensor(qkT_a[p][:, :, 0:n],
                                    pm[p][0:KD, 0, 0:4 * R].rearrange("p (c n) -> p c n", c=4)[:, :, 0:n],
                                    bqk_a[:].unsqueeze(2).to_broadcast((KD, 4, n)), ALU.add
                                    ).then_inc(A["qkv_done"], 1)
                    V.tensor_tensor(v_a[p][0:n], pm[p][0:n, 1, 0:D], bv_a[0:n], ALU.add).then_inc(A["qkv_done"], 1)
                for p, t, n, _ in tiles:
                    dve.wait_ge(A["score_mm"], t + 1)
                    V.tensor_tensor(sT_a[p][0:n, 0:n], pm[p][0:n, 0, 0:n], decay[0:n, 0:n], ALU.mult
                                    ).then_inc(A["score_done"], 1)
                for p, t, n, _ in tiles:
                    dve.wait_ge(A["out_mm"], t + 1)
                    V.tensor_tensor(hrow(t, n), hrow(t, n), pm[p][0:n, 1, 0:D], ALU.add).then_inc(A["h1_done"], 1)

            def heads_attention(l, tiles):
                s, w = L[l], W[l]
                at = {}
                if l == 0:
                    at = row_stats(tiles, from_h, A["h1_done"], s["stats_done"], None)
                    for p, t, n, _ in tiles:
                        st.after(at[p])
                        V.scalar_tensor_tensor(small[p][0:n, 3:4], small[p][0:n, 2:3], EPS, small[p][0:n, 1:2],
                                               ALU.mult, ALU.add).then_inc(s["var_ready"], 1)
                    for p, t, n, _ in tiles:
                        dve.wait_ge(s["root_done"], t + 1)
                        V.tensor_scalar(xn[p][0:n], hrow(t, n), small[p][0:n, 0:1], small[p][0:n, 5:6],
                                        ALU.subtract, ALU.mult).then_inc(s["normed"], 1)
                        V.tensor_scalar(x1[p][0:n], hrow(t, n), small[p][0:n, 0:1], small[p][0:n, 4:5],
                                        ALU.subtract, ALU.mult).then_inc(s["x1_done"], 1)
                else:
                    normalise(tiles, from_h, xn, M[0]["y_added"], s["stats_done"], s["var_ready"], s["root_done"], s["normed"])
                for p, t, n, _ in tiles:
                    dve.wait_ge(s["qkv_mm"], t + 1)
                    acc = pm[p][0:n, 0, 0:2 * D].rearrange("p (h d) -> p h d", d=HD)
                    bias = w["bqkv"][0:n, 0:2 * D].rearrange("p (h d) -> p h d", d=HD)
                    dst = qkpad[p][0:n, :, :, 0:HD].rearrange("p a h d -> p (a h) d") if l == 0 else qk[p][0:n]
                    V.tensor_tensor(dst, acc, bias, ALU.add).then_inc(s["qk_done" if l == 0 else "qk_added"], 1)
                    V.tensor_tensor(vone[p][0:n, :, 0:HD], pm[p][0:n, 1, 0:D].rearrange("p (h d) -> p h d", d=HD),
                                    w["bqkv"][0:n, 2 * D:3 * D].rearrange("p (h d) -> p h d", d=HD), ALU.add
                                    ).then_inc(s["v_done"], 1)
                if l == 1:
                    for p, t, n, _ in tiles:
                        dve.wait_ge(s["qk_added"], t + 1)
                        at[p] = st.did(V.tensor_tensor(rot[p][0:n], qk[p][0:n],
                                                       ropecos[0:n].unsqueeze(1).to_broadcast((n, 2 * H, HD)),
                                                       ALU.mult))
                    for p, t, n, _ in tiles:
                        st.after(at[p])
                        dve.wait_ge(s["swapped"], t * 2 + 2)
                        V.tensor_tensor(qkpad[p][0:n, :, :, 0:HD].rearrange("p a h d -> p (a h) d"),
                                        rot[p][0:n], rot2[p][0:n], ALU.add).then_inc(s["qk_done"], 1)
                for p, t, n, _ in tiles:
                    dve.wait_ge(s["qk_turned"], t + 1)
                    V.tensor_copy(qT[p][:, :, 0:n], three(pm[p], 1, n)).then_inc(s["qT_done"], 1)
                for p, t, n, _ in tiles:
                    for half in range(2):
                        dve.wait_ge(s["score_mm"], t * 2 + (half + 1))
                        to = qkpad[p][0:n, 0, :, HD] if l == 0 else negmax[p][0:n]
                        V.tensor_reduce(to.rearrange("p (c r) -> p r c", r=4)[:, 2 * half:2 * half + 2, :],
                                        scores(half, n), AX.X, ALU.max, negate=True).then_inc(s["max_done"], 1)
                if l == 1:
                    for p, t, n, _ in tiles:
                        dve.wait_ge(s["max_done"], t * 2 + 2)
                        at[p] = st.did(V.scalar_tensor_tensor(qkpad[p][0:n, 0, :, HD], sinks[0:n], -HD ** 0.5,
                                                              negmax[p][0:n], ALU.mult, ALU.min))
                    for p, t, n, _ in tiles:
                        st.after(at[p])
                        V.scalar_tensor_tensor(den[p][0:n], sinks[0:n], HD ** 0.5, qkpad[p][0:n, 0, :, HD],
                                               ALU.mult, ALU.add).then_inc(s["negmax_done"], 1)
                for p, t, n, _ in tiles:
                    dve.wait_ge(s["pv_mm"], t + 1)
                    acc = pm[p][0:n, 0, 0:H * (HD + 1)].rearrange("p (h d) -> p h d", d=HD + 1)
                    if l == 0:
                        at[p] = st.did(V.reciprocal(den[p][0:n], acc[:, :, HD]))
                    else:
                        dve.wait_ge(s["sink_exp"], t + 1)
                        at[p] = st.did(V.tensor_tensor(den[p][0:n], acc[:, :, HD], den[p][0:n], ALU.add))
                if l == 1:
                    for p, t, n, _ in tiles:
                        st.after(at[p])
                        at[p] = st.did(V.reciprocal(den[p][0:n], den[p][0:n]))
                for p, t, n, _ in tiles:
                    st.after(at[p])
                    acc = pm[p][0:n, 0, 0:H * (HD + 1)].rearrange("p (h d) -> p h d", d=HD + 1)
                    V.tensor_tensor(o[p][0:n], acc[:, :, 0:HD], den[p][0:n].unsqueeze(2).to_broadcast((n, H, HD)),
                                    ALU.mult).then_inc(s["o_done"], 1)
                for p, t, n, _ in tiles:
                    dve.wait_ge(s["proj_mm"], t + 1)
                    if l == 0:
                        dve.wait_ge(s["x1b_done"], t + 1)
                        V.tensor_tensor(x1[p][0:n], pm[p][0:n, 0, 0:D], x1b[p][0:n], ALU.add
                                        ).then_inc(s["y_done"], 1)
                    else:
                        at[p] = st.did(V.tensor_tensor(x1[p][0:n], pm[p][0:n, 0, 0:D], w["bproj"][0:n], ALU.add))
                if l == 1:
                    for p, t, n, _ in tiles:
                        st.after(at[p])
                        V.scalar_tensor_tensor(hrow(t, n), x1[p][0:n], rezero[0:n, 0:1], hrow(t, n),
                                               ALU.mult, ALU.add).then_inc(s["y_done"], 1)
                src = (lambda p, t, n: x1[p][0:n]) if l == 0 else from_h
                normalise(tiles, src, xn, s["y_done"], s["stats_done2"], s["var_ready2"], s["root_done2"], s["normed2"])
                for p, t, n, _ in tiles:
                    dve.wait_ge(s["logit_mm"], t + 1)
                    dst = logits[0:n, t, :] if isinstance(t, int) else \
                        logits[0:n, bass.ds(t, 1), :].rearrange("p o e -> p (o e)")
                    V.tensor_tensor(dst, pm[p][0:n, 0, 0:EXPERTS], bs[0:n, l], ALU.add
                                    ).then_inc(s["logit_done"], 1)
                _, t, _, _ = tiles[-1]
                dve.wait_ge(s["xT_done"], t + 1)
                if l == 0:
                    dve.wait_ge(s["h_added"], t + 1)

            def choose(l):
                m = M[l]
                shape = (R, TILES, EXPERTS, EXPERTS)
                mine = logits[:].unsqueeze(3).to_broadcast(shape)
                other = logits[:].unsqueeze(2).to_broadcast(shape)
                dve.wait_ge(L[l]["logit_done"], TILES)
                n = st.did(V.tensor_reduce(top[:], logits[:], AX.X, ALU.max))
                st.after(n)
                V.tensor_tensor(gates[:], logits[:], top[:].unsqueeze(2).to_broadcast((R, TILES, EXPERTS)),
                                ALU.subtract).then_inc(m["gates_shifted"], 1)
                st.did(V.tensor_tensor(cmp[:], other, mine, ALU.is_gt))
                n = st.did(V.tensor_tensor(cmq[:], other, mine, ALU.is_equal))
                st.after(n)
                n = st.did(V.tensor_tensor(cmq[:], cmq[:], earlier[:].unsqueeze(1).to_broadcast(shape), ALU.mult))
                st.after(n)
                n = st.did(V.tensor_tensor(cmp[:], cmp[:], cmq[:], ALU.add))
                st.after(n)
                n = st.did(V.tensor_reduce(rank[:], cmp[:], AX.X, ALU.add))
                dve.wait_ge(m["gates_exp"], 1)
                if l == 1:
                    st.did(V.tensor_reduce(gsum[:], gates[:], AX.X, ALU.add))
                st.after(st.n)
                n = st.did(V.scalar_tensor_tensor(gates[:], rank[:], 1.5 if l == 0 else 0.5, gates[:],
                                                  ALU.is_lt, ALU.mult))
                st.after(n)
                if l == 0:
                    n = st.did(V.tensor_reduce(gsum[:], gates[:], AX.X, ALU.add))
                    st.after(n)
                n = st.did(V.reciprocal(gsum[:], gsum[:]))
                st.after(n)
                V.tensor_tensor(gates[:], gates[:], gsum[:].unsqueeze(2).to_broadcast((R, TILES, EXPERTS)),
                                ALU.mult).then_inc(m["gates_done"], 1)
                for k, tiles in enumerate(CHUNKS):
                    n = sum(rows(t) for t in tiles)
                    dve.wait_ge(m["gatesT_mm"], k + 1)
                    V.tensor_copy(gatesT[:, tiles[0] * R:tiles[0] * R + n], ps[k // 2][0:EXPERTS, k % 2, 0:n]
                                  ).then_inc(m["gatesT_done"], 1)

            def experts(l):
                m = M[l]
                choose(l)
                dve.sem_inc(m["y_added"], Y_CREDIT)
                dve.wait_ge(m["gates_done"], 1)
                for t in range(TILES):
                    dve.wait_ge(m["down_mm"], DOWN_CREDIT + t + 1)
                    n = rows(t)
                    V.tensor_tensor(h[0:n, t, :], pm[t % 4 // 2][0:n, t % 2, 0:D], h[0:n, t, :], ALU.add
                                    ).then_inc(m["y_added"], 1)
                with dve.Fori(0, EXPERTS // 2) as i:
                    for p in range(2):
                        for t in range(TILES):
                            n, at = rows(t), FIRST + p * per_expert + t
                            dve.wait_ge(m["down_mm"], i * (2 * per_expert) + (DOWN_CREDIT + at + 1))
                            dve.wait_ge(m["y_added"], i * (2 * per_expert) + (Y_CREDIT + at - TILES + 1))
                            V.scalar_tensor_tensor(h[0:n, t, :], pm[t % 4 // 2][0:n, t % 2, 0:D],
                                                   gates[0:n, t, bass.ds(i * 2 + p, 1)], h[0:n, t, :],
                                                   ALU.mult, ALU.add).then_inc(m["y_added"], 1)

            dve.wait_ge(tok_in, TOK_IN)
            at = {}
            for s in range(5):
                for c in range(TC):
                    if s == 0:
                        at[c] = st.did(V.tensor_scalar(etok[:, c], wsh[:, s, c], gsh[:, s, c:c + 1], None, ALU.mult))
                        continue
                    st.after(at[c])
                    ins = V.scalar_tensor_tensor(etok[:, c], wsh[:, s, c], gsh[:, s, c:c + 1], etok[:, c],
                                                 ALU.mult, ALU.add)
                    if s < 4:
                        at[c] = st.did(ins)
                    else:
                        ins.then_inc(etok_done, 1)
            dve.wait_ge(tokrow_mm, 1)
            V.tensor_tensor(tokrow[:], pm[0][0:1, 0, 0:D], tokbias[:], ALU.add).then_inc(tokrow_done, 1)
            dve.wait_ge(base_mm, 1)
            n = st.did(V.tensor_copy(base[:], pm[0][0:R, 1, 0:D]))
            st.after(n)
            dve.wait_ge(pads_set, 5)
            dve.wait_ge(rest_in, REST_IN)
            V.tensor_copy(identb[:], ident[0:R, 0:R]).then_inc(masks_cast, 1)
            for k, m in enumerate((blockmask, causal_q, causal_k)):
                V.tensor_copy(m[:], masks[:, k].unsqueeze(1).to_broadcast((R, 3, R))).then_inc(masks_cast, 1)
            with dve.Fori(0, PAIRS) as i:
                st.enter(i, PER_PASS[0])
                tokens(pair(i))
                decay_attention(pair(i))
                heads_attention(0, pair(i))
                st.leave(PAIRS)
            tokens(LAST)
            decay_attention(LAST)
            heads_attention(0, LAST)
            experts(0)
            dve.wait_ge(M[0]["y_added"], Y_CREDIT + FIRST + per_expert * EXPERTS)
            with dve.Fori(0, PAIRS) as i:
                st.enter(i, PER_PASS[1])
                heads_attention(1, pair(i))
                st.leave(PAIRS)
            heads_attention(1, LAST)
            experts(1)

        @block.tensor
        def _(pe):
            def mm(dst, lhsT, rhs, first=True, last=True):
                return nc.tensor.matmul(dst, lhsT, rhs, start=first, stop=last, skip_group_check=True)

            def turn(dst, src, n):
                return nc.tensor.transpose(dst, src, ident[0:n, 0:n])

            def tokens(tiles):
                for p, t, n, _ in tiles:
                    pe.wait_ge(A["centred"], t + 1)
                    for c in range(TC):
                        last = turn(pm[p][0:TP, c // 4, c % 4 * R:c % 4 * R + n],
                                    xin[p][0:n, c * TP:(c + 1) * TP], n)
                    last.then_inc(A["tok_turned"], 1)
                for p, t, n, _ in tiles:
                    pe.wait_ge(A["tok_evac_act"], t + 1)
                    pe.wait_ge(A["tok_evac_dve"], t + 1)
                    for c in range(TC):
                        last = mm(pm[p][0:n, 0, 0:D], yT[p][:, c, 0:n], etok[:, c], c == 0, c == TC - 1)
                    last.then_inc(A["tok_mm"], 1)

            def turn_rows(tiles, bank, ready, done, src):
                for p, t, n, _ in tiles:
                    pe.wait_ge(ready, t + 1)
                    for c in range(2):
                        last = turn(pm[p][0:KD, bank, c * R:c * R + n], src(p, n, c), n)
                    last.then_inc(done, 1)

            def half_rows(p, n, c):
                return xn[p][0:n, c * KD:(c + 1) * KD]

            def decay_attention(tiles):
                turn_rows(tiles, 0, A["normed"], A["turned"], half_rows)
                for p, t, n, _ in tiles:
                    pe.wait_ge(A["xnT_done"], t + 1)
                    for j in range(4):
                        for c in range(2):
                            mm(pm[p][0:KD, 0, j * R:j * R + n], w_a[:, c, j * KD:(j + 1) * KD], xnT[p][:, c, 0:n],
                               c == 0, c == 1)
                    for c in range(2):
                        last = mm(pm[p][0:n, 1, 0:D], xnT[p][:, c, 0:n], w_a[:, c, 2 * D:3 * D], c == 0, c == 1)
                    last.then_inc(A["qkv_mm"], 1)
                for p, t, n, _ in tiles:
                    pe.wait_ge(A["qkv_done"], t * 2 + 2)
                    for c in range(2):
                        last = mm(pm[p][0:n, 0, 0:n], qkT_a[p][:, 2 + c, 0:n], qkT_a[p][:, c, 0:n], c == 0, c == 1)
                    last.then_inc(A["score_mm"], 1)
                for p, t, n, _ in tiles:
                    pe.wait_ge(A["score_done"], t + 1)
                    mm(pm[p][0:n, 1, 0:D], sT_a[p][0:n, 0:n], v_a[p][0:n]).then_inc(A["out_mm"], 1)

            def head_scores(half, n, mask, left, right, k):
                for r in (2 * half, 2 * half + 1):
                    mm(scores(half, n)[:, r % 2], identb[0:n, 0:n], mask[0:n, :, 0:n], True, False)
                for c in range(HC):
                    for r in (2 * half, 2 * half + 1):
                        last = mm(scores(half, n)[:, r % 2, c], left[HP * r:HP * r + k, c, 0:n],
                                  right[HP * r:HP * r + k, c, 0:n], False, True)
                return last

            def heads_attention(l, tiles):
                s, w = L[l], W[l]
                turn_rows(tiles, 0, s["normed"], s["turned"], half_rows)
                for p, t, n, _ in tiles:
                    pe.wait_ge(s["xnT_done"], t + 1)
                    for c in range(2):
                        mm(pm[p][0:n, 0, 0:2 * D], xnT[p][:, c, 0:n], w["qkv"][:, c, 0:2 * D], c == 0, c == 1)
                    for c in range(2):
                        last = mm(pm[p][0:n, 1, 0:D], xnT[p][:, c, 0:n], w["qkv"][:, c, 2 * D:3 * D], c == 0, c == 1)
                    last.then_inc(s["qkv_mm"], 1)

                def turn_heads(p, n, which, bank):
                    src = qkpad[p][0:n, which].rearrange("p (c r) d -> p c (r d)", c=HC)
                    for c in range(HC):
                        last = turn(pm[p][:, bank, c * R:c * R + n], src[:, c], n)
                    return last

                for p, t, n, _ in tiles:
                    pe.wait_ge(s["qk_done"], t + 1)
                    pe.wait_ge(s["v_done"], t + 1)
                    turn_heads(p, n, 1, 0)
                    turn_heads(p, n, 0, 1).then_inc(s["qk_turned"], 1)
                for j, (p, t, n, _) in enumerate(tiles):
                    pe.wait_ge(s["kT_done"], t + 1)
                    pe.wait_ge(s["qT_done"], t + 1)
                    for half in range(2):
                        if j == 1:
                            pe.wait_ge(s["max_done"], t * 2 + (half - 1))
                        head_scores(half, n, blockmask if l == 0 else causal_q, qT[p], kT[p], HD
                                    ).then_inc(s["score_mm"], 1)
                for p, t, n, _ in tiles:
                    pe.wait_ge(s["max_done"] if l == 0 else s["negmax_done"], t * 2 + 2 if l == 0 else t + 1)
                    turn_heads(p, n, 0, 1).then_inc(s["q_turned"], 1)
                for j, (p, t, n, _) in enumerate(tiles):
                    pe.wait_ge(s["qTm_done"], t + 1)
                    for half in range(2):
                        if j == 0:
                            pe.wait_ge(s["max_done"], (t + (len(tiles) - 1)) * 2 + (half + 1))
                        else:
                            pe.wait_ge(s["exp_done"], t * 2 + (half - 1))
                        head_scores(half, n, blockmask if l == 0 else causal_k, kT[p], qTm[p], HD + 1
                                    ).then_inc(s["scoreT_mm"], 1)
                for p, t, n, _ in tiles:
                    pe.wait_ge(s["exp_done"], t * 2 + 2)
                    acc = pm[p][0:n, 0, 0:H * (HD + 1)].rearrange("p (h d) -> p h d", d=HD + 1)
                    for hd in range(H):
                        last = mm(acc[:, hd], e[p][0:n, hd % 4, hd // 4, 0:n], vone[p][0:n, hd])
                    last.then_inc(s["pv_mm"], 1)
                turn_rows(tiles, 1, s["o_done"], s["o_turned"],
                          lambda p, n, c: o[p][0:n].rearrange("p h d -> p (h d)")[:, c * KD:(c + 1) * KD])
                for p, t, n, _ in tiles:
                    pe.wait_ge(s["oT_done"], t + 1)
                    for c in range(2):
                        last = mm(pm[p][0:n, 0, 0:D], oT[p][:, c, 0:n], w["proj"][:, c], c == 0, c == 1)
                    last.then_inc(s["proj_mm"], 1)
                turn_rows(tiles, 1, s["normed2"], s["turned2"], half_rows)
                for p, t, n, _ in tiles:
                    pe.wait_ge(s["xnT2_done"], t + 1)
                    for c in range(2):
                        last = mm(pm[p][0:n, 0, 0:EXPERTS], xnT[p][:, c, 0:n], w["gate"][:, c], c == 0, c == 1)
                    last.then_inc(s["logit_mm"], 1)

            def up(l, i, step):
                m = M[l]
                p, k = step % 6 // 3, step % 3
                if k == 0:
                    pe.wait_ge(w_in[l][p], (i + step // 6 + 1) * 48)
                tiles = CHUNKS[k]
                n, at = sum(rows(t) for t in tiles), tiles[0] * R
                for b in range(FB):
                    u = step * FB + b
                    pe.wait_ge(m["gelu_done"], i * (6 * FB) + (u + 1))
                    for c in range(2):
                        last = mm(ps[u % 4 // 2][:, u % 2, 0:n], w1[:, p, c, b * 128:(b + 1) * 128],
                                  xT[:, c, at:at + n], c == 0, c == 1)
                    last.then_inc(m["up_mm"], 1)

            def down(l, i, step):
                m = M[l]
                p, k = step // 3, step % 3
                pe.wait_ge(m["gelu_done"], i * (6 * FB) + (HID_BANKS + (step + 1) * FB))
                for j, t in enumerate(CHUNKS[k]):
                    n, at = rows(t), FIRST + p * per_expert + t
                    pe.wait_ge(m["y_added"], i * (2 * per_expert) + (at + 1))
                    for b in range(FB):
                        last = mm(pm[t % 4 // 2][0:n, t % 2, 0:D], hid[:, step % 2, b, j * R:j * R + n], w2[:, p, b],
                                  b == 0, b == FB - 1)
                    last.then_inc(m["down_mm"], 1)

            def experts(l):
                m = M[l]
                pe.wait_ge(m["gates_done"], 1)
                for k, tiles in enumerate(CHUNKS):
                    for j, t in enumerate(tiles):
                        last = turn(ps[k // 2][0:EXPERTS, k % 2, j * R:j * R + rows(t)], gates[0:rows(t), t, :],
                                    rows(t))
                    last.then_inc(m["gatesT_mm"], 1)
                pe.wait_ge(m["gatesT_done"], len(CHUNKS))
                pe.wait_ge(L[l]["xT_done"], TILES)
                pe.sem_inc(m["down_mm"], DOWN_CREDIT)
                for t in range(TILES):
                    pe.wait_ge(m["y_added"], t + 1)
                    mm(pm[t % 4 // 2][0:rows(t), t % 2, 0:D], gatesT[:, t * R:t * R + rows(t)], W[l]["b2"][:]
                       ).then_inc(m["down_mm"], 1)
                up(l, 0, 0)
                with pe.Fori(0, EXPERTS // 2 - 1) as i:
                    for step in range(6):
                        up(l, i, step + 1)
                        down(l, i, step)
                for step in range(6):
                    if step < 5:
                        up(l, EXPERTS // 2 - 1, step + 1)
                    down(l, EXPERTS // 2 - 1, step)

            pe.wait_ge(tok_in, TOK_IN)
            for s in range(5):
                for c in range(TC):
                    last = mm(pm[0][0:1, 0, 0:D], bsh[:, s, c:c + 1], wsh[:, s, c], s + c == 0, s + c == TC + 3)
            last.then_inc(tokrow_mm, 1)
            pe.wait_ge(tokrow_done, 1)
            mm(pm[0][0:R, 1, 0:D], roles[:, 0, :], tokrow[:], True, False)
            mm(pm[0][0:R, 1, 0:D], roles[:, 1, :], clsrow[:], False, True).then_inc(base_mm, 1)
            pe.wait_ge(etok_done, TC)
            pe.wait_ge(pads_set, 5)
            pe.wait_ge(rest_in, REST_IN)
            pe.wait_ge(masks_cast, 4)
            with pe.Fori(0, PAIRS) as i:
                tokens(pair(i))
                decay_attention(pair(i))
                heads_attention(0, pair(i))
            tokens(LAST)
            decay_attention(LAST)
            heads_attention(0, LAST)
            experts(0)
            with pe.Fori(0, PAIRS) as i:
                heads_attention(1, pair(i))
            heads_attention(1, LAST)
            experts(1)


def constants():
    i = np.arange(R)
    image, pos = i // N, i % N
    same = image[:, None] == image[None, :]
    later = pos[:, None] >= pos[None, :]
    decay = np.where(same.T & later.T, np.float32(0.99) ** (pos[None, :] - pos[:, None]).clip(0).astype(np.float32),
                     np.float32(0)) / np.sqrt(np.float32(D))

    def mask(keep):
        return np.where(keep, 0.0, -1e30).astype(np.float32)

    freqs = np.float32(1.0) / np.float32(10000.0) ** (np.arange(0, HD, 2, dtype=np.float32) / np.float32(HD))
    ang = pos[:, None].astype(np.float32) * freqs[None, :].astype(np.float32)
    cos = np.repeat(np.cos(ang), 2, axis=1).astype(np.float32)
    sin = np.repeat(np.sin(ang), 2, axis=1).astype(np.float32)
    sin[:, 0::2] *= -1
    cnt = np.zeros((C, len(SPOTS)), np.float32)
    for dy, dx in SHIFTS:
        for k, (y, x) in enumerate(SPOTS):
            cnt[:, k] += 0 <= y - 1 - dy < PATCH and 0 <= x - 1 - dx < PATCH
    cnt = cnt.reshape(-1)
    roles = np.stack([pos != 0, pos == 0])[None].astype(np.float32)
    n = np.arange(EXPERTS)
    return {
        "c_ident": np.eye(128, dtype=np.float32), 
        "c_masks": np.stack([mask(same), mask(same & later), mask(same & later.T)], axis=1),
        "c_decay": decay.astype(np.float32), "c_count": cnt, "c_rootcount": np.sqrt(cnt / PD).astype(np.float32),
        "c_roles": roles, "c_cos": cos, "c_sin": sin,
        "c_earlier": (n[None, :] < n[:, None]).astype(np.float32),
    }


def shift_sources():
    src = np.full((5, C, len(SPOTS)), -1)
    for s, (dy, dx) in enumerate(SHIFTS):
        for k, (y, x) in enumerate(SPOTS):
            ph, pw = y - 1 - dy, x - 1 - dx
            if 0 <= ph < PATCH and 0 <= pw < PATCH:
                for c in range(C):
                    src[s, c, k] = (ph * PATCH + pw) * 5 * C + s * C + c
    return src.reshape(5, KT)


def laid_out(x):
    f = {k: np.asarray(v) for k, v in x.items()}
    pad = np.pad(f["x"], ((0, 0), (0, 0), (1, 1), (1, 1)))
    side = IMG // PATCH
    ys, xs = np.array(SPOTS).T
    corner = np.arange(side) * PATCH
    got = pad[:, :, corner[:, None, None] + ys, corner[None, :, None] + xs]
    spots = got.transpose(0, 2, 3, 1, 4).reshape(B, side * side, KT)
    tokens = np.concatenate([np.zeros((B, 1, KT), np.float32), spots], axis=1).reshape(T, KT)
    src = shift_sources()

    def by_spot(v):
        padded = np.concatenate([v, np.zeros_like(v[:1])])
        got = padded[src]
        return np.ascontiguousarray(got.reshape((5, TC, TP) + v.shape[1:]).swapaxes(1, 2).swapaxes(0, 1))

    def halves(v):
        return np.ascontiguousarray(v.reshape(2, KD).T)

    a = {
        "x": np.ascontiguousarray(tokens), "cls_tok": f["cls_tok"].reshape(1, D),
        "wsh": by_spot(f["L0_tok_proj_weight"].T), "gsh": by_spot(f["L0_tok_ln_weight"]),
        "bsh": by_spot(f["L0_tok_ln_bias"]), "tok_bias": f["L0_tok_proj_bias"].reshape(1, D),
        "L0_attn_W_qkv": f["L0_attn_W_qkv"],
        "attn_bqk": np.ascontiguousarray(f["L0_attn_b_qkv"][:2 * D].reshape(4, KD).T),
        "attn_bv": np.ascontiguousarray(f["L0_attn_b_qkv"][2 * D:]),
        "qkv0": f["L0_ffn_qkv_w"], "bqkv0": f["L0_ffn_qkv_b"], "gain0": halves(f["L0_ffn_ln1_g"]),
        "shift0": halves(f["L0_ffn_ln1_b"]), "proj0": f["L0_ffn_proj_w"], "bproj0": f["L0_ffn_proj_b"],
        "gate0": f["L0_ffn_gate_w"], "w1_0": f["L0_ffn_w1"], "w2_0": f["L0_ffn_w2"], "b2_0": f["L0_ffn_b2"],
        "gain2": halves(f["L0_ffn_ln2_g"]), "shift2": halves(f["L0_ffn_ln2_b"]),
        "qkv1": f["L1_attn_W_attn"], "bqkv1": f["L1_attn_b_attn"], "gain1": halves(f["L1_attn_norm_scale"]),
        "shift1": halves(f["L1_attn_norm_bias"]), "proj1": f["L1_attn_W_proj"], "bproj1": f["L1_attn_b_proj"],
        "gate1": f["L1_ffn_Ws"], "w1_1": f["L1_ffn_W1"], "w2_1": f["L1_ffn_W2"], "b2_1": f["L1_ffn_b2"],
        "sinks": f["L1_attn_sinks"], "rezero": f["L1_attn_rezero"],
        "bs": np.stack([np.zeros(EXPERTS, np.float32), f["L1_ffn_bs"]]),
    }
    for l, b1 in enumerate((f["L0_ffn_b1"], f["L1_ffn_b1"])):
        a[f"b1_{l}"] = np.ascontiguousarray(b1.reshape(EXPERTS, FB, 128).transpose(0, 2, 1))
    return a


def kernel(**inputs):
    import concourse.bacc as bacc
    from concourse.bass_utils import run_bass_kernel_spmd

    nc = bacc.Bacc("TRN2", target_bir_lowering=False, num_devices=1)
    arrays = {**laid_out(inputs), **constants()}
    a = {k: nc.dram_tensor(f"in_{k}", v.shape, mybir.dt.from_np(v.dtype), kind="ExternalInput").ap()
         for k, v in arrays.items()}
    out = nc.dram_tensor("out", (T, D), F32, kind="ExternalOutput").ap()
    build(nc, a, out)
    r = run_bass_kernel_spmd(nc, [{f"in_{k}": v for k, v in arrays.items()}], core_ids=[0])
    return r.results[0]["out"].reshape(B, N, D)
```

```python
from contextlib import ExitStack

import numpy as np

import concourse.bass as bass
from concourse import mybir

F32 = mybir.dt.float32
BF16 = mybir.dt.bfloat16
I32 = mybir.dt.int32
ALU = mybir.AluOpType
ACT = mybir.ActivationFunctionType
AX = mybir.AxisListType

B, C, IMG, PATCH = 32, 3, 96, 16
D = 192
N = (IMG // PATCH) ** 2 + 1
T = B * N
R = 3 * N
TILES = -(-T // R)
TAIL = T - (TILES - 1) * R
PAIRS = (TILES - 1) // 2
KD = 96
H, HD = 12, 16
HP = 32
HC = H * HP // 128
EXPERTS, FF = 8, 768
FB = FF // 128
SHIFTS = ((0, 0), (0, -1), (0, 1), (-1, 0), (1, 0))
HALO = PATCH + 2
SPOTS = [(i, j) for i in range(HALO) for j in range(HALO)
         if not (i in (0, HALO - 1) and j in (0, HALO - 1))]
KT = C * len(SPOTS)
TC = 8
TP = KT // TC
PD = PATCH * PATCH * 5 * C
EPS = 1e-5
CHUNK = 4
CHUNKS = [range(a, min(a + CHUNK, TILES)) for a in range(0, TILES, CHUNK)]
BLK = 128
PICKS = (2, 1)
BLOCKS = [(k * T - EXPERTS) // BLK + EXPERTS for k in PICKS]
FILLS = -(-T // BLK)
HALF = FF // 2
PER_PASS = (12, 14)


def rows(t):
    return TAIL if t == TILES - 1 else R


class Room:

    def __init__(self, whole):
        self.whole, self.at = whole, 0

    def take(self, shape):
        n = int(np.prod(shape[1:]))
        flat = self.whole[0:shape[0], self.at:self.at + n]
        self.at += n
        assert self.at <= self.whole.shape[1]
        names = "abc"[:len(shape) - 1]
        return flat.rearrange(f"p ({' '.join(names)}) -> p {' '.join(names)}", **dict(zip(names, shape[1:])))


def build(nc, a, out):
    with ExitStack() as ctx:
        def sb(name, shape, dt=F32):
            return ctx.enter_context(nc.sbuf_tensor(name, shape, dt))

        def pb(name, shape, dt=F32):
            return ctx.enter_context(nc.psum_tensor(name, shape, dt))

        def sem(name):
            return ctx.enter_context(nc.semaphore(name))

        ident = sb("ident", [128, 128])
        identb = sb("identb", [R, R], BF16)
        blockmask = sb("blockmask", [R, 3, R], BF16)
        causal_q = sb("causal_q", [R, 3, R], BF16)
        causal_k = sb("causal_k", [R, 3, R], BF16)
        decay = sb("decay", [R, R])
        w2 = sb("w2", [128, FB, EXPERTS, D])
        w2_room = Room(w2[:].rearrange("p b e n -> p (b e n)"))
        count = w2_room.take([R, KT])
        rootcount = w2_room.take([R, KT])
        w1 = sb("w1", [128, 2, EXPERTS, FF])
        wsh = w1[0:TP].rearrange("p c e n -> p (c e n)")[:, 0:5 * TC * D].rearrange("p (s c d) -> p s c d", s=5, c=TC)
        gsh = sb("gsh", [TP, 5, TC])
        bsh = sb("bsh", [TP, 5, TC])
        etok = w2_room.take([TP, TC, D])
        clsrow = sb("clsrow", [1, D])
        tokbias = sb("tokbias", [1, D])
        tokrow = sb("tokrow", [1, D])
        roles = sb("roles", [1, 2, R])
        base = sb("base", [R, D])
        w_a = sb("w_a", [KD, 2, 3 * D])
        bqk_a = sb("bqk_a", [KD, 4])
        bv_a = sb("bv_a", [R, D])
        ropecos = sb("ropecos", [R, HD])
        ropesin = sb("ropesin", [R, HD])
        W = []
        for l in range(2):
            W.append(dict(
                qkv=sb(f"qkv{l}", [KD, 2, 3 * D]), bqkv=sb(f"bqkv{l}", [R, 3 * D]),
                gain=sb(f"gain{l}", [KD, 2]), shift=sb(f"shift{l}", [KD, 2]),
                proj=sb(f"proj{l}", [KD, 2, D]), bproj=sb(f"bproj{l}", [R, D]),
                gate=sb(f"gate{l}", [KD, 2, EXPERTS]),
                b2=sb(f"b2_{l}", [EXPERTS, D]),
            ))
        gain2 = sb("gain2", [KD, 2])
        shift2 = sb("shift2", [KD, 2])
        sinks = sb("sinks", [R, H])
        rezero = sb("rezero", [R, 1])
        bs = sb("bs", [R, 2, EXPERTS])

        h = sb("h", [R, TILES, D])
        xall = sb("xall", [R, TILES, D])
        logits = sb("logits", [R, TILES, EXPERTS])
        gates = sb("gates", [R, TILES, EXPERTS])
        earlier = sb("earlier", [R, EXPERTS, EXPERTS])
        e_store = sb("e_store", [128, 2 * 4 * HC * R])
        e_room, other = Room(e_store[:]), Room(e_store[:])
        e = [e_room.take([R, 4, HC, R]) for _ in range(2)]
        hb = other.take([BLK, FF])
        cmp = other.take([R, TILES, EXPERTS, EXPERTS])
        cmq = other.take([R, TILES, EXPERTS, EXPERTS])
        masks = cmp.rearrange("r t e f -> r (t e f)")[:, 0:3 * R].rearrange("r (k n) -> r k n", k=3)
        rank = sb("rank", [R, TILES, EXPERTS])
        top = sb("top", [R, TILES])
        gsum = sb("gsum", [R, TILES])
        gatesT = sb("gatesT", [EXPERTS, T])
        valid = sb("valid", [R, TILES])
        below = sb("below", [R, R])
        ones = sb("ones", [R, R])
        fills = sb("fills", [R, FILLS])
        blockno = sb("blockno", [1, max(BLOCKS)])
        keep = sb("keep", [R, TILES, EXPERTS])
        nfill = sb("nfill", [R, EXPERTS, FILLS])
        nblocks = sb("nblocks", [R, EXPERTS])
        before = sb("before", [R, EXPERTS, EXPERTS])
        startblock = sb("startblock", [R, EXPERTS])
        endblock = sb("endblock", [R, EXPERTS])
        ended = sb("ended", [1, max(BLOCKS), EXPERTS])
        expertf = sb("expertf", [1, max(BLOCKS)])
        expert = sb("expert", [1, max(BLOCKS)], I32)
        pos = sb("pos", [R, TILES, EXPERTS])
        picked = sb("picked", [R, TILES, EXPERTS])
        slotf = sb("slotf", [R, 2, TILES])
        slot = sb("slot", [R, 2, TILES], I32)
        weight = sb("weight", [R, 2, TILES])
        back = Room(w2_room.whole).take([R, 2, TILES, D])
        xb = sb("xb", [BLK, D])
        xbT = sb("xbT", [KD + 1, 2, BLK])
        hbT = sb("hbT", [128, FB, BLK])
        yb = sb("yb", [BLK, D])
        zeros = sb("zeros", [BLK, D])
        def slots(name, shape, dt=F32):
            return [sb(f"{name}_{p}", shape, dt) for p in range(2)]

        xin = [w2_room.take([R, KT]) for _ in range(2)]
        zin = [w2_room.take([R, KT]) for _ in range(2)]
        yT = [w2_room.take([TP, TC, R]) for _ in range(2)]
        small = slots("small", [R, 16])
        stats = slots("stats", [R, 6])
        minushalf = sb("minushalf", [R, 2])
        xn = slots("xn", [R, D])
        xnT = slots("xnT", [KD, 2, R])
        qkT_a = slots("qkT_a", [KD, 4, R])
        v_a = slots("v_a", [R, D])
        sT_a = slots("sT_a", [R, R])
        x1 = slots("x1", [R, D])
        x1b = slots("x1b", [R, D])
        qk = slots("qk", [R, 2 * H, HD])
        rot = slots("rot", [R, 2 * H, HD])
        rot2 = slots("rot2", [R, 2 * H, HD])
        qkpad = slots("qkpad", [R, 2, H, HP])
        vone = slots("vone", [R, H, HD + 1])
        kT = slots("kT", [128, HC, R])
        qT = slots("qT", [128, HC, R])
        qTm = slots("qTm", [128, HC, R])
        negmax = slots("negmax", [R, H])
        den = slots("den", [R, H])
        o = slots("o", [R, H, HD])
        oT = slots("oT", [KD, 2, R])

        ps = [pb(f"ps{i}", [128, 2, 512]) for i in range(2)]
        pm = [pb(f"pm{i}", [128, 2, 512]) for i in range(2)]

        tok_in = sem("tok_in")
        rest_in = sem("rest_in")
        etok_done = sem("etok_done")
        tokrow_mm, tokrow_done, base_mm, base_done = (sem(x) for x in
                                                      ("tokrow_mm", "tokrow_done", "base_mm", "base_done"))
        pads_set, masks_cast = sem("pads_set"), sem("masks_cast")
        x_in = [sem(f"x_in{p}") for p in range(2)]
        def sems(names, tag=""):
            return {n: sem(n + tag) for n in names.split()}

        A = sems("centred weighted squared tok_var tok_root stats_done var_ready root_done tok_turned tok_evac_act tok_evac_dve tok_mm h0_done normed turned "
                 "xnT_done qkv_mm qkv_done score_mm score_done out_mm h1_done", "_a")
        L = sems("stats_done stats_done2 var_ready root_done var_ready2 root_done2 normed turned xnT_done qkv_mm qk_added swapped qk_done v_done qk_turned kT_done qT_done "
                  "score_mm max_done negmax_done sink_exp q_turned qTm_done scoreT_mm exp_done pv_mm o_done "
                  "o_turned oT_done proj_mm x1_done x1b_done y_done normed2 turned2 xnT2_done logit_mm logit_done "
                  "kept h_added", "_l")
        M = [sems("gates_shifted gates_exp gates_done gatesT_mm gatesT_done bias_mm bias_added keep_done slots_mm "
                  "experts_found slots_done scattered x_turned xbT_done up_mm gelu_done h_turned hbT_done down_mm "
                  "y_evac h_done", f"_m{l}") for l in range(2)]
        w_in = [sem(f"w_in_{l}") for l in range(2)]
        xb_in = [sem(f"xb_in_{l}") for l in range(2)]
        y_stored = [sem(f"y_stored_{l}") for l in range(2)]
        back_in = [sem(f"back_in_{t}") for t in range(TILES)]
        zero_set, zero_filled = sem("zero_set"), sem("zero_filled")
        dve_step = sem("dve_step")
        pool_step = sem("pool_step")
        out_done = sem("out_done")
        xs = [nc.dram_tensor(f"xs{l}", (BLOCKS[l] * BLK, D), F32, kind="Internal").ap() for l in range(2)]
        ys = [nc.dram_tensor(f"ys{l}", (BLOCKS[l] * BLK, D), F32, kind="Internal").ap() for l in range(2)]
        backs = [16 * PICKS[0], 16 * (PICKS[0] + PICKS[1])]

        block = ctx.enter_context(nc.Block())

        def tile_of(buf, t, n):
            return buf[0:n, t, :] if isinstance(t, int) else buf[0:n, bass.ds(t, 1), :].rearrange("p o d -> p (o d)")

        def hrow(t, n):
            return tile_of(h, t, n)

        def pair(i, l=0):
            return [(0, i * 2, R, i * 2 + l * TILES), (1, i * 2 + 1, R, i * 2 + (1 + l * TILES))]

        def tail(l=0):
            return [(0, TILES - 1, TAIL, TILES - 1 + l * TILES)]

        class Steps:

            def __init__(self, eng, s):
                self.eng, self.s, self.base, self.n, self.i, self.per = eng, s, 0, 0, None, 0

            def enter(self, i, per):
                self.base, self.n, self.i, self.per = self.base + self.n, 0, i, per

            def leave(self, passes):
                assert self.n == self.per, (self.n, self.per)
                self.base, self.n, self.i = self.base + passes * self.per, 0, None

            def did(self, ins):
                ins.then_inc(self.s, 1)
                self.n += 1
                return self.n

            def after(self, n):
                v = self.base + n
                self.eng.wait_ge(self.s, v if self.i is None else self.i * self.per + v)

        def two(buf, bank, parts, n):
            return buf[0:parts, bank, 0:2 * R].rearrange("p (c n) -> p c n", c=2)[:, :, 0:n]

        def bias_bank(k):
            return [ps[0][:, 0], ps[0][:, 1], ps[1][:, 0], ps[1][:, 1], pm[0][:, 0], pm[0][:, 1]][k]

        def gatesT_bank(k):
            return [pm[1][:, 0], pm[1][:, 1], ps[1][:, 0]][k]

        def three(buf, bank, n, parts=128):
            return buf[0:parts, bank, 0:HC * R].rearrange("p (c n) -> p c n", c=HC)[:, :, 0:n]

        def scores(half, n):
            return ps[half][0:n, :, 0:HC * R].rearrange("p r (c n) -> p r c n", c=HC)[:, :, :, 0:n]

        PADS = 7
        Y_CREDIT = 1
        tok_loads = [(count[:], a["c_count"].partition_broadcast(R)), (gsh[:], a["gsh"]), (bsh[:], a["bsh"])]
        tok_loads += [(wsh[:, s], a["wsh"][:, s]) for s in range(5)]
        tok_loads += [(rootcount[:], a["c_rootcount"].partition_broadcast(R)), (ident[:], a["c_ident"]),
                      (roles[:], a["c_roles"]), (clsrow[:], a["cls_tok"]), (tokbias[:], a["tok_bias"])]
        rest_loads = [
            (w_a[:], a["L0_attn_W_qkv"].rearrange("(c p) n -> p c n", p=KD)), (bqk_a[:], a["attn_bqk"]),
            (bv_a[:], a["attn_bv"].partition_broadcast(R)), (decay[:], a["c_decay"]), (masks[:], a["c_masks"])]
        for l in range(2):
            w = W[l]
            rest_loads += [
                (w["qkv"][:], a[f"qkv{l}"].rearrange("(c p) n -> p c n", p=KD)),
                (w["bqkv"][:], a[f"bqkv{l}"].partition_broadcast(R)), (w["gain"][:], a[f"gain{l}"]),
                (w["shift"][:], a[f"shift{l}"]), (w["proj"][:], a[f"proj{l}"].rearrange("(c p) n -> p c n", p=KD)),
                (w["bproj"][:], a[f"bproj{l}"].partition_broadcast(R)),
                (w["gate"][:], a[f"gate{l}"].rearrange("(c p) n -> p c n", p=KD)),
                (w["b2"][:], a[f"b2_{l}"])]
        rest_loads += [(gain2[:], a["gain2"]), (shift2[:], a["shift2"]), (ropecos[:], a["c_cos"]),
                       (ropesin[:], a["c_sin"]), (sinks[:], a["sinks"].partition_broadcast(R)),
                       (rezero[:], a["rezero"].partition_broadcast(R)), (bs[:], a["bs"].partition_broadcast(R)),
                       (earlier[:], a["c_earlier"].partition_broadcast(R)), (valid[:], a["c_valid"]),
                       (below[:], a["c_below"]), (fills[:], a["c_fills"].partition_broadcast(R)),
                       (blockno[:], a["c_blockno"])]
        TOK_IN, REST_IN = 16 * len(tok_loads), 16 * len(rest_loads)

        @block.sync
        def _(sp):
            for dst, src in tok_loads:
                sp.dma_start(dst, src).then_inc(tok_in, 16)
            for dst, src in rest_loads:
                sp.dma_start(dst, src).then_inc(rest_in, 16)

            sp.wait_ge(zero_set, 1)
            for l in range(2):
                sp.dma_start(xs[l].rearrange("(b p) d -> p b d", p=BLK),
                             zeros[:].unsqueeze(1).to_broadcast((BLK, BLOCKS[l], D))).then_inc(zero_filled, 16)

            def load_w1(l):
                for c in range(2):
                    sp.dma_start(w1[0:KD, c], a[f"w1_{l}"][:, c * KD:(c + 1) * KD, :].rearrange("e p n -> p e n")
                                 ).then_inc(w_in[l], 16)
                sp.dma_start(w1[KD:KD + 1, 0], a[f"b1_{l}"]).then_inc(w_in[l], 16)

            def load_w2(l):
                for b in range(FB):
                    sp.dma_start(w2[:, b], a[f"w2_{l}"][:, b * 128:(b + 1) * 128, :].rearrange("e p n -> p e n")
                                 ).then_inc(w_in[l], 16)

            def load_block(l, b):
                at = slice(b * BLK, (b + 1) * BLK) if isinstance(b, int) else bass.ds(b * BLK, BLK)
                if not isinstance(b, int) or b:
                    sp.wait_ge(M[l]["x_turned"], b)
                sp.dma_start(xb[:], xs[l][at, :]).then_inc(xb_in[l], 16)

            def store_block(l, b):
                at = slice(b * BLK, (b + 1) * BLK) if isinstance(b, int) else bass.ds(b * BLK, BLK)
                sp.wait_ge(M[l]["y_evac"], Y_CREDIT + b + 1)
                sp.dma_start(ys[l][at, :], yb[:]).then_inc(y_stored[l], 16)

            def blocks(l):
                n = BLOCKS[l]
                sp.wait_ge(M[l]["scattered"], 16 * PICKS[l] * TILES)
                for b in range(3):
                    load_block(l, b)
                with sp.Fori(0, n - 3) as b:
                    load_block(l, b + 3)
                    store_block(l, b)
                for b in range(n - 3, n):
                    store_block(l, b)

            sp.wait_ge(etok_done, TC)
            sp.wait_ge(tokrow_mm, 1)
            load_w1(0)
            sp.wait_ge(A["h1_done"], TILES)
            load_w2(0)
            blocks(0)
            sp.wait_ge(M[0]["h_done"], 2 * TILES)
            load_w1(1)
            load_w2(1)
            blocks(1)
            sp.wait_ge(M[1]["h_done"], TILES)
            full = (TILES - 1) * R
            sp.dma_start(out[0:full, :].rearrange("(t p) d -> p t d", p=R), h[:, 0:TILES - 1, :]
                         ).then_inc(out_done, 16)
            sp.dma_start(out[full:T, :], h[0:TAIL, TILES - 1, :]).then_inc(out_done, 16)
            sp.wait_ge(out_done, 32)

        @block.scalar
        def _(act):
            def copy(dst, src):
                return nc.scalar.activation(dst, src, ACT.Copy)

            def affine(dst, src, gain, shift, n):
                for c in range(2):
                    last = nc.scalar.activation(dst[:, c, 0:n], src[:, c, 0:n], ACT.Identity,
                                                bias=shift[:, c:c + 1], scale=gain[:, c:c + 1])
                return last

            def tokens(tiles):
                for p, t, n, _ in tiles:
                    act.wait_ge(A["weighted"], t + 1)
                    nc.scalar.activation(zin[p][0:n], zin[p][0:n], ACT.Square,
                                         accum_out=small[p][0:n, 7:8]).then_inc(A["squared"], 1)
                for p, t, n, _ in tiles:
                    act.wait_ge(A["tok_turned"], t + 1)
                    copy(yT[p][:, 0:4, 0:n], pm[p][0:TP, 0, 0:4 * R].rearrange("p (c n) -> p c n", c=4)[:, :, 0:n]
                         ).then_inc(A["tok_evac_act"], 1)

            def decay_attention(tiles):
                for p, t, n, _ in tiles:
                    act.wait_ge(A["turned"], t + 1)
                    copy(xnT[p][:, :, 0:n], two(pm[p], 0, KD, n)).then_inc(A["xnT_done"], 1)

            def heads_attention(l, tiles):
                s, w = L, W[l]
                for p, t, n, k in tiles:
                    act.wait_ge(s["turned"], k + 1)
                    affine(xnT[p], two(pm[p], 0, KD, n), w["gain"], w["shift"], n).then_inc(s["xnT_done"], 1)
                for p, t, n, k in tiles:
                    act.wait_ge(s["qk_turned"], k + 1)
                    copy(kT[p][:, :, 0:n], three(pm[p], 0, n)).then_inc(s["kT_done"], 1)
                if l == 1:
                    for p, t, n, k in tiles:
                        act.wait_ge(s["negmax_done"], t + 1)
                        nc.scalar.activation(den[p][0:n], den[p][0:n], ACT.Exp, scale=HD ** -0.5
                                             ).then_inc(s["sink_exp"], 1)
                for p, t, n, k in tiles:
                    act.wait_ge(s["q_turned"], k + 1)
                    copy(qTm[p][:, :, 0:n], three(pm[p], 1, n)).then_inc(s["qTm_done"], 1)
                for p, t, n, k in tiles:
                    for half in range(2):
                        act.wait_ge(s["scoreT_mm"], k * 2 + (half + 1))
                        nc.scalar.activation(e[p][0:n, 2 * half:2 * half + 2, :, 0:n], scores(half, n), ACT.Exp,
                                             scale=HD ** -0.5).then_inc(s["exp_done"], 1)
                for p, t, n, k in tiles:
                    act.wait_ge(s["o_turned"], k + 1)
                    copy(oT[p][:, :, 0:n], two(pm[p], 1, KD, n)).then_inc(s["oT_done"], 1)
                for p, t, n, k in tiles:
                    act.wait_ge(s["turned2"], k + 1)
                    if l == 0:
                        last = affine(xnT[p], two(pm[p], 1, KD, n), gain2, shift2, n)
                    else:
                        last = copy(xnT[p][:, :, 0:n], two(pm[p], 1, KD, n))
                    last.then_inc(s["xnT2_done"], 1)

            def experts(l):
                m = M[l]
                act.wait_ge(m["gates_shifted"], 1)
                nc.scalar.activation(gates[:], gates[:], ACT.Exp).then_inc(m["gates_exp"], 1)
                with act.Fori(0, BLOCKS[l]) as b:
                    for half in range(2):
                        act.wait_ge(m["up_mm"], b * 2 + (half + 1))
                        nc.scalar.activation(hb[:, half * HALF:(half + 1) * HALF], ps[0][:, half, 0:HALF], ACT.Gelu
                                             ).then_inc(m["gelu_done"], 1)

            for p in range(2):
                act.dma_start(xin[p][:], a["x"][p * R:(p + 1) * R, :]).then_inc(x_in[p], 16)
            act.wait_ge(rest_in, REST_IN)
            with act.Fori(0, PAIRS - 1) as i:
                tokens(pair(i))
                for p, t, n, _ in pair(i):
                    act.dma_start(xin[p][:], a["x"][bass.ds((t + 2) * R, R), :]).then_inc(x_in[p], 16)
                decay_attention(pair(i))
                heads_attention(0, pair(i))
            tokens(pair(PAIRS - 1))
            act.dma_start(xin[0][0:TAIL], a["x"][(TILES - 1) * R:T, :]).then_inc(x_in[0], 16)
            decay_attention(pair(PAIRS - 1))
            heads_attention(0, pair(PAIRS - 1))
            tokens(tail())
            decay_attention(tail())
            heads_attention(0, tail())
            experts(0)
            with act.Fori(0, PAIRS) as i:
                heads_attention(1, pair(i, 1))
            heads_attention(1, tail(1))
            experts(1)

        @block.gpsimd
        def _(pool):
            for p in range(2):
                nc.gpsimd.memset(qkpad[p][:], 0.0).then_inc(pool_step, 1)
                nc.gpsimd.memset(vone[p][:], 1.0).then_inc(pads_set, 1)
            nc.gpsimd.memset(logits[:], 0.0).then_inc(pads_set, 1)
            nc.gpsimd.memset(minushalf[:], -0.5).then_inc(pool_step, 1)
            nc.gpsimd.memset(zeros[:], 0.0).then_inc(zero_set, 1)
            nc.gpsimd.memset(ones[:], 1.0).then_inc(pads_set, 1)
            pool.wait_ge(pool_step, 3)
            for p in range(2):
                nc.gpsimd.memset(qkpad[p][:, 1, :, HD:HD + 1], 1.0).then_inc(pads_set, 1)
            pool.wait_ge(tok_in, TOK_IN)
            pool.wait_ge(rest_in, REST_IN)

            def root(tiles, ready, done, src, dst, m=1):
                for p, t, n, k in tiles:
                    pool.wait_ge(ready, k + 1)
                    nc.gpsimd.tensor_tensor(small[p][0:n, dst:dst + m], small[p][0:n, src:src + m],
                                            minushalf[0:n, 0:m], ALU.pow).then_inc(done, 1)

            def tokens(tiles):
                for p, t, n, _ in tiles:
                    pool.wait_ge(A["centred"], t + 1)
                    nc.gpsimd.tensor_tensor(zin[p][0:n], xin[p][0:n], rootcount[0:n], ALU.mult
                                            ).then_inc(A["weighted"], 1)
                root(tiles, A["tok_var"], A["tok_root"], 8, 9)
                root(tiles, A["var_ready"], A["root_done"], 2, 4)

            def heads_attention(l, tiles):
                s = L
                root(tiles, s["var_ready"], s["root_done"], 2, 4, 2 - l)
                if l == 0:
                    for p, t, n, k in tiles:
                        pool.wait_ge(s["x1_done"], k + 1)
                        nc.gpsimd.tensor_tensor(x1b[p][0:n], x1[p][0:n], W[0]["bproj"][0:n], ALU.add
                                                ).then_inc(s["x1b_done"], 1)
                else:
                    for p, t, n, k in tiles:
                        pool.wait_ge(s["qk_added"], t + 1)
                        for c in range(2):
                            last = nc.gpsimd.tensor_tensor(
                                rot2[p][0:n, :, c::2], qk[p][0:n, :, 1 - c::2],
                                ropesin[0:n, c::2].unsqueeze(1).to_broadcast((n, 2 * H, HD // 2)), ALU.mult)
                            last.then_inc(s["swapped"], 1)
                root(tiles, s["var_ready2"], s["root_done2"], 2, 4)
                if l == 0:
                    for p, t, n, k in tiles:
                        pool.wait_ge(s["y_done"], k + 1)
                        nc.gpsimd.tensor_tensor(hrow(t, n), hrow(t, n), x1[p][0:n], ALU.add
                                                ).then_inc(s["h_added"], 1)
                for p, t, n, k in tiles:
                    pool.wait_ge(s["normed2"], k + 1)
                    nc.gpsimd.tensor_copy(tile_of(xall, t, n), xn[p][0:n]).then_inc(s["kept"], 1)

            def experts(l):
                m = M[l]
                pool.wait_ge(m["slots_done"], 1)
                pool.wait_ge(zero_filled, 32)
                pool.wait_ge(L["kept"], (l + 1) * TILES)
                for t in range(TILES):
                    for j in range(PICKS[l]):
                        at = bass.IndirectOffsetOnAxis(ap=slot[0:rows(t), j, t:t + 1], axis=0)
                        nc.gpsimd.indirect_dma_start(out=xs[l], out_offset=at, in_=xall[0:rows(t), t, :],
                                                     in_offset=None).then_inc(m["scattered"], 16)
                pool.wait_ge(y_stored[l], 16 * (Y_CREDIT + BLOCKS[l]))
                for t in range(TILES):
                    for j in range(PICKS[l]):
                        at = bass.IndirectOffsetOnAxis(ap=slot[0:rows(t), j, t:t + 1], axis=0)
                        nc.gpsimd.indirect_dma_start(out=back[0:rows(t), j, t, :], out_offset=None, in_=ys[l],
                                                     in_offset=at).then_inc(back_in[t], 16)

            with pool.Fori(0, PAIRS) as i:
                tokens(pair(i))
                heads_attention(0, pair(i))
            tokens(tail())
            heads_attention(0, tail())
            experts(0)
            with pool.Fori(0, PAIRS) as i:
                heads_attention(1, pair(i, 1))
            heads_attention(1, tail(1))
            experts(1)

        @block.vector
        def _(dve):
            V = nc.vector
            st = Steps(dve, dve_step)

            def wait_alone(ready, value):
                dve.wait_ge(pads_set, PADS)
                dve.wait_ge(ready, value)

            def row_stats(tiles, src, ready, stats_done, done):
                at = {}
                for p, t, n, k in tiles:
                    wait_alone(ready, k + 1)
                    V.bn_stats(stats[p][0:n], src(p, t, n)).then_inc(stats_done, 1)
                for p, t, n, k in tiles:
                    wait_alone(stats_done, k + 1)
                    at[p] = st.did(V.bn_aggr(small[p][0:n, 0:2], stats[p][0:n]))
                for p, t, n, k in tiles:
                    st.after(at[p])
                    ins = V.tensor_scalar(small[p][0:n, 2:3], small[p][0:n, 1:2], EPS, None, ALU.add)
                    if done is None:
                        at[p] = st.did(ins)
                    else:
                        ins.then_inc(done, 1)
                return at

            def normalise(tiles, src, dst, ready, stats_done, var_ready, root_done, done):
                row_stats(tiles, src, ready, stats_done, var_ready)
                for p, t, n, k in tiles:
                    dve.wait_ge(root_done, k + 1)
                    V.tensor_scalar(dst[p][0:n], src(p, t, n), small[p][0:n, 0:1], small[p][0:n, 4:5],
                                    ALU.subtract, ALU.mult).then_inc(done, 1)

            def from_h(p, t, n):
                return hrow(t, n)

            def tokens(tiles, loads):
                at = {}
                for p, t, n, _ in tiles:
                    dve.wait_ge(x_in[p], loads * 16)
                    at[p] = st.did(V.tensor_tensor_reduce(zin[p][0:n], xin[p][0:n], count[0:n], 1.0 / PD, 0.0,
                                                          ALU.mult, ALU.add, small[p][0:n, 6:7]))
                for p, t, n, _ in tiles:
                    st.after(at[p])
                    V.tensor_scalar(xin[p][0:n], xin[p][0:n], small[p][0:n, 6:7], None, ALU.subtract
                                    ).then_inc(A["centred"], 1)
                for p, t, n, _ in tiles:
                    dve.wait_ge(A["tok_turned"], t + 1)
                    V.tensor_copy(yT[p][:, 4:8, 0:n], pm[p][0:TP, 1, 0:4 * R].rearrange(
                        "p (c n) -> p c n", c=4)[:, :, 0:n]).then_inc(A["tok_evac_dve"], 1)
                for p, t, n, _ in tiles:
                    dve.wait_ge(A["squared"], t + 1)
                    V.tensor_scalar(small[p][0:n, 8:9], small[p][0:n, 7:8], EPS, None, ALU.add
                                    ).then_inc(A["tok_var"], 1)
                for p, t, n, _ in tiles:
                    dve.wait_ge(A["tok_root"], t + 1)
                    dve.wait_ge(A["tok_mm"], t + 1)
                    V.scalar_tensor_tensor(hrow(t, n), pm[p][0:n, 0, 0:D], small[p][0:n, 9:10], base[0:n],
                                           ALU.mult, ALU.add).then_inc(A["h0_done"], 1)

            def decay_attention(tiles):
                normalise(tiles, from_h, xn, A["h0_done"], A["stats_done"], A["var_ready"], A["root_done"], A["normed"])
                for p, t, n, _ in tiles:
                    dve.wait_ge(A["qkv_mm"], t + 1)
                    V.tensor_tensor(qkT_a[p][:, :, 0:n],
                                    pm[p][0:KD, 0, 0:4 * R].rearrange("p (c n) -> p c n", c=4)[:, :, 0:n],
                                    bqk_a[:].unsqueeze(2).to_broadcast((KD, 4, n)), ALU.add
                                    ).then_inc(A["qkv_done"], 1)
                    V.tensor_tensor(v_a[p][0:n], pm[p][0:n, 1, 0:D], bv_a[0:n], ALU.add).then_inc(A["qkv_done"], 1)
                for p, t, n, _ in tiles:
                    dve.wait_ge(A["score_mm"], t + 1)
                    V.tensor_tensor(sT_a[p][0:n, 0:n], pm[p][0:n, 0, 0:n], decay[0:n, 0:n], ALU.mult
                                    ).then_inc(A["score_done"], 1)
                for p, t, n, _ in tiles:
                    dve.wait_ge(A["out_mm"], t + 1)
                    V.tensor_tensor(hrow(t, n), hrow(t, n), pm[p][0:n, 1, 0:D], ALU.add).then_inc(A["h1_done"], 1)

            def heads_attention(l, tiles):
                s, w = L, W[l]
                at = {}
                if l == 0:
                    at = row_stats(tiles, from_h, A["h1_done"], s["stats_done"], None)
                    for p, t, n, k in tiles:
                        st.after(at[p])
                        V.scalar_tensor_tensor(small[p][0:n, 3:4], small[p][0:n, 2:3], EPS, small[p][0:n, 1:2],
                                               ALU.mult, ALU.add).then_inc(s["var_ready"], 1)
                    for p, t, n, k in tiles:
                        dve.wait_ge(s["root_done"], k + 1)
                        V.tensor_scalar(xn[p][0:n], hrow(t, n), small[p][0:n, 0:1], small[p][0:n, 5:6],
                                        ALU.subtract, ALU.mult).then_inc(s["normed"], 1)
                        V.tensor_scalar(x1[p][0:n], hrow(t, n), small[p][0:n, 0:1], small[p][0:n, 4:5],
                                        ALU.subtract, ALU.mult).then_inc(s["x1_done"], 1)
                else:
                    normalise(tiles, from_h, xn, M[0]["h_done"], s["stats_done"], s["var_ready"], s["root_done"], s["normed"])
                for p, t, n, k in tiles:
                    dve.wait_ge(s["qkv_mm"], k + 1)
                    acc = pm[p][0:n, 0, 0:2 * D].rearrange("p (h d) -> p h d", d=HD)
                    bias = w["bqkv"][0:n, 0:2 * D].rearrange("p (h d) -> p h d", d=HD)
                    dst = qkpad[p][0:n, :, :, 0:HD].rearrange("p a h d -> p (a h) d") if l == 0 else qk[p][0:n]
                    V.tensor_tensor(dst, acc, bias, ALU.add).then_inc(s["qk_done" if l == 0 else "qk_added"], 1)
                    V.tensor_tensor(vone[p][0:n, :, 0:HD], pm[p][0:n, 1, 0:D].rearrange("p (h d) -> p h d", d=HD),
                                    w["bqkv"][0:n, 2 * D:3 * D].rearrange("p (h d) -> p h d", d=HD), ALU.add
                                    ).then_inc(s["v_done"], 1)
                if l == 1:
                    for p, t, n, k in tiles:
                        dve.wait_ge(s["qk_added"], t + 1)
                        at[p] = st.did(V.tensor_tensor(rot[p][0:n], qk[p][0:n],
                                                       ropecos[0:n].unsqueeze(1).to_broadcast((n, 2 * H, HD)),
                                                       ALU.mult))
                    for p, t, n, k in tiles:
                        st.after(at[p])
                        dve.wait_ge(s["swapped"], t * 2 + 2)
                        V.tensor_tensor(qkpad[p][0:n, :, :, 0:HD].rearrange("p a h d -> p (a h) d"),
                                        rot[p][0:n], rot2[p][0:n], ALU.add).then_inc(s["qk_done"], 1)
                for p, t, n, k in tiles:
                    dve.wait_ge(s["qk_turned"], k + 1)
                    V.tensor_copy(qT[p][:, :, 0:n], three(pm[p], 1, n)).then_inc(s["qT_done"], 1)
                for p, t, n, k in tiles:
                    for half in range(2):
                        dve.wait_ge(s["score_mm"], k * 2 + (half + 1))
                        to = qkpad[p][0:n, 0, :, HD] if l == 0 else negmax[p][0:n]
                        V.tensor_reduce(to.rearrange("p (c r) -> p r c", r=4)[:, 2 * half:2 * half + 2, :],
                                        scores(half, n), AX.X, ALU.max, negate=True).then_inc(s["max_done"], 1)
                if l == 1:
                    for p, t, n, k in tiles:
                        dve.wait_ge(s["max_done"], k * 2 + 2)
                        at[p] = st.did(V.scalar_tensor_tensor(qkpad[p][0:n, 0, :, HD], sinks[0:n], -HD ** 0.5,
                                                              negmax[p][0:n], ALU.mult, ALU.min))
                    for p, t, n, k in tiles:
                        st.after(at[p])
                        V.scalar_tensor_tensor(den[p][0:n], sinks[0:n], HD ** 0.5, qkpad[p][0:n, 0, :, HD],
                                               ALU.mult, ALU.add).then_inc(s["negmax_done"], 1)
                for p, t, n, k in tiles:
                    dve.wait_ge(s["pv_mm"], k + 1)
                    acc = pm[p][0:n, 0, 0:H * (HD + 1)].rearrange("p (h d) -> p h d", d=HD + 1)
                    if l == 0:
                        at[p] = st.did(V.reciprocal(den[p][0:n], acc[:, :, HD]))
                    else:
                        dve.wait_ge(s["sink_exp"], t + 1)
                        at[p] = st.did(V.tensor_tensor(den[p][0:n], acc[:, :, HD], den[p][0:n], ALU.add))
                if l == 1:
                    for p, t, n, k in tiles:
                        st.after(at[p])
                        at[p] = st.did(V.reciprocal(den[p][0:n], den[p][0:n]))
                for p, t, n, k in tiles:
                    st.after(at[p])
                    acc = pm[p][0:n, 0, 0:H * (HD + 1)].rearrange("p (h d) -> p h d", d=HD + 1)
                    V.tensor_tensor(o[p][0:n], acc[:, :, 0:HD], den[p][0:n].unsqueeze(2).to_broadcast((n, H, HD)),
                                    ALU.mult).then_inc(s["o_done"], 1)
                for p, t, n, k in tiles:
                    dve.wait_ge(s["proj_mm"], k + 1)
                    if l == 0:
                        dve.wait_ge(s["x1b_done"], k + 1)
                        V.tensor_tensor(x1[p][0:n], pm[p][0:n, 0, 0:D], x1b[p][0:n], ALU.add
                                        ).then_inc(s["y_done"], 1)
                    else:
                        at[p] = st.did(V.tensor_tensor(x1[p][0:n], pm[p][0:n, 0, 0:D], w["bproj"][0:n], ALU.add))
                if l == 1:
                    for p, t, n, k in tiles:
                        st.after(at[p])
                        V.scalar_tensor_tensor(hrow(t, n), x1[p][0:n], rezero[0:n, 0:1], hrow(t, n),
                                               ALU.mult, ALU.add).then_inc(s["y_done"], 1)
                src = (lambda p, t, n: x1[p][0:n]) if l == 0 else from_h
                normalise(tiles, src, xn, s["y_done"], s["stats_done2"], s["var_ready2"], s["root_done2"], s["normed2"])
                for p, t, n, k in tiles:
                    dve.wait_ge(s["logit_mm"], k + 1)
                    V.tensor_tensor(tile_of(logits, t, n), pm[p][0:n, 0, 0:EXPERTS], bs[0:n, l], ALU.add
                                    ).then_inc(s["logit_done"], 1)
                _, _, _, k = tiles[-1]
                dve.wait_ge(s["kept"], k + 1)
                if l == 0:
                    dve.wait_ge(s["h_added"], k + 1)

            def choose(l):
                m = M[l]
                shape = (R, TILES, EXPERTS, EXPERTS)
                mine = logits[:].unsqueeze(3).to_broadcast(shape)
                other = logits[:].unsqueeze(2).to_broadcast(shape)
                dve.wait_ge(L["logit_done"], (l + 1) * TILES)
                n = st.did(V.tensor_reduce(top[:], logits[:], AX.X, ALU.max))
                st.after(n)
                V.tensor_tensor(gates[:], logits[:], top[:].unsqueeze(2).to_broadcast((R, TILES, EXPERTS)),
                                ALU.subtract).then_inc(m["gates_shifted"], 1)
                st.did(V.tensor_tensor(cmp[:], other, mine, ALU.is_gt))
                n = st.did(V.tensor_tensor(cmq[:], other, mine, ALU.is_equal))
                st.after(n)
                n = st.did(V.tensor_tensor(cmq[:], cmq[:], earlier[:].unsqueeze(1).to_broadcast(shape), ALU.mult))
                st.after(n)
                n = st.did(V.tensor_tensor(cmp[:], cmp[:], cmq[:], ALU.add))
                st.after(n)
                n = st.did(V.tensor_reduce(rank[:], cmp[:], AX.X, ALU.add))
                st.after(n)
                V.scalar_tensor_tensor(keep[:], rank[:], PICKS[l] - 0.5, valid[:].unsqueeze(2).to_broadcast(
                    (R, TILES, EXPERTS)), ALU.is_lt, ALU.mult).then_inc(m["keep_done"], 1)
                dve.wait_ge(m["gates_exp"], 1)
                if l == 1:
                    st.did(V.tensor_reduce(gsum[:], gates[:], AX.X, ALU.add))
                    st.after(st.n)
                dve.wait_ge(m["keep_done"], 1)
                n = st.did(V.tensor_tensor(gates[:], keep[:], gates[:], ALU.mult))
                st.after(n)
                if l == 0:
                    n = st.did(V.tensor_reduce(gsum[:], gates[:], AX.X, ALU.add))
                    st.after(n)
                    n = st.did(V.tensor_scalar(gsum[:], gsum[:], 1e-30, None, ALU.max))
                    st.after(n)
                n = st.did(V.reciprocal(gsum[:], gsum[:]))
                st.after(n)
                V.tensor_tensor(gates[:], gates[:], gsum[:].unsqueeze(2).to_broadcast((R, TILES, EXPERTS)),
                                ALU.mult).then_inc(m["gates_done"], 1)

            def find_slots(l):
                m = M[l]
                each = (R, TILES, EXPERTS)
                dve.wait_ge(m["slots_mm"], 1)
                taken, placed = ps[0][0:R, 1, 0:EXPERTS], ps[0][0:R, 0, 0:TILES * EXPERTS].rearrange(
                    "r (t e) -> r t e", e=EXPERTS)
                n = st.did(V.tensor_tensor(nfill[:], taken.unsqueeze(2).to_broadcast((R, EXPERTS, FILLS)),
                                           fills[:].unsqueeze(1).to_broadcast((R, EXPERTS, FILLS)), ALU.is_gt))
                st.after(n)
                n = st.did(V.tensor_reduce(nblocks[:], nfill[:], AX.X, ALU.add))
                st.after(n)
                n = st.did(V.tensor_tensor(before[:], earlier[:], nblocks[:].unsqueeze(1).to_broadcast(
                    (R, EXPERTS, EXPERTS)), ALU.mult))
                st.after(n)
                n = st.did(V.tensor_reduce(startblock[:], before[:], AX.X, ALU.add))
                st.after(n)
                n = st.did(V.scalar_tensor_tensor(pos[:], startblock[:].unsqueeze(1).to_broadcast(each), float(BLK),
                                                  placed, ALU.mult, ALU.add))
                for j in range(PICKS[l]):
                    st.after(n)
                    n = st.did(V.scalar_tensor_tensor(picked[:], rank[:], float(j), pos[:], ALU.is_equal, ALU.mult))
                    st.after(n)
                    n = st.did(V.tensor_reduce(slotf[:, j], picked[:], AX.X, ALU.add))
                st.after(n)
                V.tensor_copy(slot[:, 0:PICKS[l]], slotf[:, 0:PICKS[l]]).then_inc(m["slots_done"], 1)
                nb = BLOCKS[l]
                n = st.did(V.tensor_tensor(endblock[:], startblock[:], nblocks[:], ALU.add))
                st.after(n)
                n = st.did(V.tensor_tensor(ended[:, 0:nb], endblock[0:1].unsqueeze(1).to_broadcast((1, nb, EXPERTS)),
                                           blockno[:, 0:nb].unsqueeze(2).to_broadcast((1, nb, EXPERTS)), ALU.is_le))
                st.after(n)
                n = st.did(V.tensor_reduce(expertf[:, 0:nb], ended[:, 0:nb], AX.X, ALU.add))
                st.after(n)
                V.tensor_scalar(expert[:, 0:nb], expertf[:, 0:nb], EXPERTS - 1.0, None, ALU.min
                                ).then_inc(m["experts_found"], 1)

            def slot_weights(l):
                for j in range(PICKS[l]):
                    st.after(st.n)
                    n = st.did(V.scalar_tensor_tensor(picked[:], rank[:], float(j), gates[:], ALU.is_equal, ALU.mult))
                    st.after(n)
                    n = st.did(V.tensor_reduce(weight[:, j], picked[:], AX.X, ALU.add))
                st.after(n)

            def experts(l):
                m = M[l]
                choose(l)
                find_slots(l)
                dve.wait_ge(m["gates_done"], 1)
                slot_weights(l)
                for k, tiles in enumerate(CHUNKS):
                    n = sum(rows(t) for t in tiles)
                    dve.wait_ge(m["gatesT_mm"], k + 1)
                    V.tensor_copy(gatesT[:, tiles[0] * R:tiles[0] * R + n], gatesT_bank(k)[0:EXPERTS, 0:n]
                                  ).then_inc(m["gatesT_done"], 1)
                dve.wait_ge(m["bias_mm"], TILES)
                for t in range(TILES):
                    n = rows(t)
                    V.tensor_tensor(h[0:n, t, :], bias_bank(t // 2)[0:n, t % 2 * D:(t % 2 + 1) * D], h[0:n, t, :],
                                    ALU.add).then_inc(m["bias_added"], 1)
                dve.sem_inc(m["y_evac"], Y_CREDIT)
                if l == 0:
                    dve.sem_inc(m["h_done"], TILES)
                dve.sem_inc(y_stored[l], 16 * Y_CREDIT)

                def rows_turned(b):
                    dve.wait_ge(m["x_turned"], b + 1)
                    src = pm[0][0:KD, 0, 0:2 * BLK].rearrange("p (c n) -> p c n", c=2)
                    if l == 1:
                        V.tensor_copy(xbT[0:KD], src).then_inc(m["xbT_done"], 2)
                        return
                    for c in range(2):
                        V.tensor_scalar(xbT[0:KD, c], src[:, c], gain2[:, c:c + 1], shift2[:, c:c + 1],
                                        ALU.mult, ALU.add).then_inc(m["xbT_done"], 1)

                def block(b, ahead):
                    dve.wait_ge(m["h_turned"], b + 1)
                    V.tensor_copy(hbT[:], ps[1][:].rearrange("p k n -> p (k n)")[:, 0:FF].rearrange(
                        "p (k n) -> p k n", k=FB)).then_inc(m["hbT_done"], 1)
                    if ahead:
                        rows_turned(b + 2)
                    dve.wait_ge(m["down_mm"], b + 1)
                    dve.wait_ge(y_stored[l], b * 16 + 16 * Y_CREDIT)
                    V.tensor_copy(yb[:], pm[0][:, 1, 0:D]).then_inc(m["y_evac"], 1)

                for b in range(2):
                    rows_turned(b)
                with dve.Fori(0, BLOCKS[l] - 2) as b:
                    block(b, True)
                for b in range(BLOCKS[l] - 2, BLOCKS[l]):
                    block(b, False)
                for t in range(TILES):
                    dve.wait_ge(back_in[t], backs[l])
                    n = rows(t)
                    for j in range(PICKS[l]):
                        ins = V.scalar_tensor_tensor(h[0:n, t, :], back[0:n, j, t, :], weight[0:n, j, t:t + 1],
                                                     h[0:n, t, :], ALU.mult, ALU.add)
                        if j == PICKS[l] - 1:
                            ins.then_inc(m["h_done"], 1)
                        else:
                            st.did(ins)
                            st.after(st.n)

            V.memset(xbT[KD:KD + 1, 0], 1.0).then_inc(pads_set, 1)
            dve.wait_ge(tok_in, TOK_IN)
            at = {}
            for s in range(5):
                for c in range(TC):
                    if s == 0:
                        at[c] = st.did(V.tensor_scalar(etok[:, c], wsh[:, s, c], gsh[:, s, c:c + 1], None, ALU.mult))
                        continue
                    st.after(at[c])
                    ins = V.scalar_tensor_tensor(etok[:, c], wsh[:, s, c], gsh[:, s, c:c + 1], etok[:, c],
                                                 ALU.mult, ALU.add)
                    if s < 4:
                        at[c] = st.did(ins)
                    else:
                        ins.then_inc(etok_done, 1)
            dve.wait_ge(tokrow_mm, 1)
            V.tensor_tensor(tokrow[:], pm[0][0:1, 0, 0:D], tokbias[:], ALU.add).then_inc(tokrow_done, 1)
            dve.wait_ge(base_mm, 1)
            n = st.did(V.tensor_copy(base[:], pm[0][0:R, 1, 0:D]))
            st.after(n)
            dve.wait_ge(pads_set, PADS)
            dve.wait_ge(rest_in, REST_IN)
            V.tensor_copy(identb[:], ident[0:R, 0:R]).then_inc(masks_cast, 1)
            for k, m in enumerate((blockmask, causal_q, causal_k)):
                V.tensor_copy(m[:], masks[:, k].unsqueeze(1).to_broadcast((R, 3, R))).then_inc(masks_cast, 1)
            with dve.Fori(0, PAIRS) as i:
                st.enter(i, PER_PASS[0])
                tokens(pair(i), i + 1)
                decay_attention(pair(i))
                heads_attention(0, pair(i))
                st.leave(PAIRS)
            tokens(tail(), PAIRS + 1)
            decay_attention(tail())
            heads_attention(0, tail())
            experts(0)
            with dve.Fori(0, PAIRS) as i:
                st.enter(i, PER_PASS[1])
                heads_attention(1, pair(i, 1))
                st.leave(PAIRS)
            heads_attention(1, tail(1))
            experts(1)

        @block.tensor
        def _(pe):
            def mm(dst, lhsT, rhs, first=True, last=True):
                return nc.tensor.matmul(dst, lhsT, rhs, start=first, stop=last, skip_group_check=True)

            def turn(dst, src, n):
                return nc.tensor.transpose(dst, src, ident[0:n, 0:n])

            def tokens(tiles):
                for p, t, n, _ in tiles:
                    pe.wait_ge(A["centred"], t + 1)
                    for c in range(TC):
                        last = turn(pm[p][0:TP, c // 4, c % 4 * R:c % 4 * R + n],
                                    xin[p][0:n, c * TP:(c + 1) * TP], n)
                    last.then_inc(A["tok_turned"], 1)
                for p, t, n, _ in tiles:
                    pe.wait_ge(A["tok_evac_act"], t + 1)
                    pe.wait_ge(A["tok_evac_dve"], t + 1)
                    for c in range(TC):
                        last = mm(pm[p][0:n, 0, 0:D], yT[p][:, c, 0:n], etok[:, c], c == 0, c == TC - 1)
                    last.then_inc(A["tok_mm"], 1)

            def turn_rows(tiles, bank, ready, done, src):
                for p, t, n, k in tiles:
                    pe.wait_ge(ready, k + 1)
                    for c in range(2):
                        last = turn(pm[p][0:KD, bank, c * R:c * R + n], src(p, n, c), n)
                    last.then_inc(done, 1)

            def half_rows(p, n, c):
                return xn[p][0:n, c * KD:(c + 1) * KD]

            def decay_attention(tiles):
                turn_rows(tiles, 0, A["normed"], A["turned"], half_rows)
                for p, t, n, _ in tiles:
                    pe.wait_ge(A["xnT_done"], t + 1)
                    for j in range(4):
                        for c in range(2):
                            mm(pm[p][0:KD, 0, j * R:j * R + n], w_a[:, c, j * KD:(j + 1) * KD], xnT[p][:, c, 0:n],
                               c == 0, c == 1)
                    for c in range(2):
                        last = mm(pm[p][0:n, 1, 0:D], xnT[p][:, c, 0:n], w_a[:, c, 2 * D:3 * D], c == 0, c == 1)
                    last.then_inc(A["qkv_mm"], 1)
                for p, t, n, _ in tiles:
                    pe.wait_ge(A["qkv_done"], t * 2 + 2)
                    for c in range(2):
                        last = mm(pm[p][0:n, 0, 0:n], qkT_a[p][:, 2 + c, 0:n], qkT_a[p][:, c, 0:n], c == 0, c == 1)
                    last.then_inc(A["score_mm"], 1)
                for p, t, n, _ in tiles:
                    pe.wait_ge(A["score_done"], t + 1)
                    mm(pm[p][0:n, 1, 0:D], sT_a[p][0:n, 0:n], v_a[p][0:n]).then_inc(A["out_mm"], 1)

            def head_scores(half, n, mask, left, right, k):
                for r in (2 * half, 2 * half + 1):
                    mm(scores(half, n)[:, r % 2], identb[0:n, 0:n], mask[0:n, :, 0:n], True, False)
                for c in range(HC):
                    for r in (2 * half, 2 * half + 1):
                        last = mm(scores(half, n)[:, r % 2, c], left[HP * r:HP * r + k, c, 0:n],
                                  right[HP * r:HP * r + k, c, 0:n], False, True)
                return last

            def heads_attention(l, tiles):
                s, w = L, W[l]
                turn_rows(tiles, 0, s["normed"], s["turned"], half_rows)
                for p, t, n, k in tiles:
                    pe.wait_ge(s["xnT_done"], k + 1)
                    for c in range(2):
                        mm(pm[p][0:n, 0, 0:2 * D], xnT[p][:, c, 0:n], w["qkv"][:, c, 0:2 * D], c == 0, c == 1)
                    for c in range(2):
                        last = mm(pm[p][0:n, 1, 0:D], xnT[p][:, c, 0:n], w["qkv"][:, c, 2 * D:3 * D], c == 0, c == 1)
                    last.then_inc(s["qkv_mm"], 1)

                def turn_heads(p, n, which, bank):
                    src = qkpad[p][0:n, which].rearrange("p (c r) d -> p c (r d)", c=HC)
                    for c in range(HC):
                        last = turn(pm[p][:, bank, c * R:c * R + n], src[:, c], n)
                    return last

                for p, t, n, k in tiles:
                    pe.wait_ge(s["qk_done"], k + 1)
                    pe.wait_ge(s["v_done"], k + 1)
                    turn_heads(p, n, 1, 0)
                    turn_heads(p, n, 0, 1).then_inc(s["qk_turned"], 1)
                for j, (p, t, n, k) in enumerate(tiles):
                    pe.wait_ge(s["kT_done"], k + 1)
                    pe.wait_ge(s["qT_done"], k + 1)
                    for half in range(2):
                        if j == 1:
                            pe.wait_ge(s["max_done"], k * 2 + (half - 1))
                        head_scores(half, n, blockmask if l == 0 else causal_q, qT[p], kT[p], HD
                                    ).then_inc(s["score_mm"], 1)
                for p, t, n, k in tiles:
                    pe.wait_ge(s["max_done"] if l == 0 else s["negmax_done"], k * 2 + 2 if l == 0 else t + 1)
                    turn_heads(p, n, 0, 1).then_inc(s["q_turned"], 1)
                for j, (p, t, n, k) in enumerate(tiles):
                    pe.wait_ge(s["qTm_done"], k + 1)
                    for half in range(2):
                        if j == 0:
                            pe.wait_ge(s["max_done"], (k + (len(tiles) - 1)) * 2 + (half + 1))
                        else:
                            pe.wait_ge(s["exp_done"], k * 2 + (half - 1))
                        head_scores(half, n, blockmask if l == 0 else causal_k, kT[p], qTm[p], HD + 1
                                    ).then_inc(s["scoreT_mm"], 1)
                for p, t, n, k in tiles:
                    pe.wait_ge(s["exp_done"], k * 2 + 2)
                    acc = pm[p][0:n, 0, 0:H * (HD + 1)].rearrange("p (h d) -> p h d", d=HD + 1)
                    for hd in range(H):
                        last = mm(acc[:, hd], e[p][0:n, hd % 4, hd // 4, 0:n], vone[p][0:n, hd])
                    last.then_inc(s["pv_mm"], 1)
                turn_rows(tiles, 1, s["o_done"], s["o_turned"],
                          lambda p, n, c: o[p][0:n].rearrange("p h d -> p (h d)")[:, c * KD:(c + 1) * KD])
                for p, t, n, k in tiles:
                    pe.wait_ge(s["oT_done"], k + 1)
                    for c in range(2):
                        last = mm(pm[p][0:n, 0, 0:D], oT[p][:, c, 0:n], w["proj"][:, c], c == 0, c == 1)
                    last.then_inc(s["proj_mm"], 1)
                turn_rows(tiles, 1, s["normed2"], s["turned2"], half_rows)
                for p, t, n, k in tiles:
                    pe.wait_ge(s["xnT2_done"], k + 1)
                    for c in range(2):
                        last = mm(pm[p][0:n, 0, 0:EXPERTS], xnT[p][:, c, 0:n], w["gate"][:, c], c == 0, c == 1)
                    last.then_inc(s["logit_mm"], 1)

            def experts(l):
                m = M[l]
                pe.wait_ge(m["keep_done"], 1)
                mm(ps[0][0:R, 0, 0:TILES * EXPERTS], below[:], keep[:].rearrange("r t e -> r (t e)"), True, False)
                for t in range(TILES - 1):
                    later = TILES - 1 - t
                    mm(ps[0][0:R, 0, (t + 1) * EXPERTS:TILES * EXPERTS].rearrange("r (t e) -> r t e", e=EXPERTS),
                       ones[:], keep[:, t].unsqueeze(1).to_broadcast((R, later, EXPERTS)), False, t == TILES - 2)
                for t in range(TILES):
                    last = mm(ps[0][0:R, 1, 0:EXPERTS], ones[:], keep[:, t], t == 0, t == TILES - 1)
                last.then_inc(m["slots_mm"], 1)
                pe.wait_ge(m["gates_done"], 1)
                for k, tiles in enumerate(CHUNKS):
                    for j, t in enumerate(tiles):
                        last = turn(gatesT_bank(k)[0:EXPERTS, j * R:j * R + rows(t)], gates[0:rows(t), t, :], rows(t))
                    last.then_inc(m["gatesT_mm"], 1)
                pe.wait_ge(m["gatesT_done"], len(CHUNKS))
                pe.wait_ge(m["experts_found"], 1)
                for t in range(TILES):
                    mm(bias_bank(t // 2)[0:rows(t), t % 2 * D:(t % 2 + 1) * D], gatesT[:, t * R:t * R + rows(t)],
                       W[l]["b2"][:]).then_inc(m["bias_mm"], 1)
                pe.wait_ge(m["bias_added"], TILES)
                pe.wait_ge(w_in[l], 16 * (3 + FB))

                def expert_of(b):
                    one = slice(b, b + 1) if isinstance(b, int) else bass.ds(b, 1)
                    return bass.ds(pe.value_load(expert[:, one], min_val=0, max_val=EXPERTS - 1), 1)

                def turn_x(b):
                    pe.wait_ge(xb_in[l], b * 16 + 16)
                    for c in range(2):
                        last = turn(pm[0][0:KD, 0, c * BLK:(c + 1) * BLK], xb[:, c * KD:(c + 1) * KD], BLK)
                    last.then_inc(m["x_turned"], 1)

                def up(b):
                    e = expert_of(b)
                    pe.wait_ge(m["xbT_done"], b * 2 + 2)
                    for half in range(2):
                        cols = slice(half * HALF, (half + 1) * HALF)
                        mm(ps[0][:, half, 0:HALF], xbT[:, 0], w1[0:KD + 1, 0, e, cols].rearrange("p o n -> p (o n)"),
                           True, False)
                        mm(ps[0][:, half, 0:HALF], xbT[0:KD, 1], w1[0:KD, 1, e, cols].rearrange("p o n -> p (o n)"),
                           False, True).then_inc(m["up_mm"], 1)

                def turn_h(b):
                    pe.wait_ge(m["gelu_done"], b * 2 + 2)
                    for k in range(FB):
                        last = turn(ps[1][:, k // 4, k % 4 * BLK:(k % 4 + 1) * BLK], hb[:, k * 128:(k + 1) * 128], BLK)
                    last.then_inc(m["h_turned"], 1)

                def down(b):
                    e = expert_of(b)
                    pe.wait_ge(m["hbT_done"], b + 1)
                    pe.wait_ge(m["y_evac"], b + Y_CREDIT)
                    for k in range(FB):
                        last = mm(pm[0][:, 1, 0:D], hbT[:, k], w2[:, k, e].rearrange("p o n -> p (o n)"),
                                  k == 0, k == FB - 1)
                    last.then_inc(m["down_mm"], 1)

                turn_x(0)
                up(0)
                turn_x(1)
                with pe.Fori(0, BLOCKS[l] - 2) as b:
                    turn_h(b)
                    up(b + 1)
                    turn_x(b + 2)
                    down(b)
                b = BLOCKS[l] - 2
                turn_h(b)
                up(b + 1)
                down(b)
                turn_h(b + 1)
                down(b + 1)

            pe.wait_ge(tok_in, TOK_IN)
            for s in range(5):
                for c in range(TC):
                    last = mm(pm[0][0:1, 0, 0:D], bsh[:, s, c:c + 1], wsh[:, s, c], s + c == 0, s + c == TC + 3)
            last.then_inc(tokrow_mm, 1)
            pe.wait_ge(tokrow_done, 1)
            mm(pm[0][0:R, 1, 0:D], roles[:, 0, :], tokrow[:], True, False)
            mm(pm[0][0:R, 1, 0:D], roles[:, 1, :], clsrow[:], False, True).then_inc(base_mm, 1)
            pe.wait_ge(etok_done, TC)
            pe.wait_ge(pads_set, PADS)
            pe.wait_ge(rest_in, REST_IN)
            pe.wait_ge(masks_cast, 4)
            with pe.Fori(0, PAIRS) as i:
                tokens(pair(i))
                decay_attention(pair(i))
                heads_attention(0, pair(i))
            tokens(tail())
            decay_attention(tail())
            heads_attention(0, tail())
            experts(0)
            with pe.Fori(0, PAIRS) as i:
                heads_attention(1, pair(i, 1))
            heads_attention(1, tail(1))
            experts(1)


def constants():
    i = np.arange(R)
    image, pos = i // N, i % N
    same = image[:, None] == image[None, :]
    later = pos[:, None] >= pos[None, :]
    decay = np.where(same.T & later.T, np.float32(0.99) ** (pos[None, :] - pos[:, None]).clip(0).astype(np.float32),
                     np.float32(0)) / np.sqrt(np.float32(D))

    def mask(keep):
        return np.where(keep, 0.0, -1e30).astype(np.float32)

    freqs = np.float32(1.0) / np.float32(10000.0) ** (np.arange(0, HD, 2, dtype=np.float32) / np.float32(HD))
    ang = pos[:, None].astype(np.float32) * freqs[None, :].astype(np.float32)
    cos = np.repeat(np.cos(ang), 2, axis=1).astype(np.float32)
    sin = np.repeat(np.sin(ang), 2, axis=1).astype(np.float32)
    sin[:, 0::2] *= -1
    cnt = np.zeros((C, len(SPOTS)), np.float32)
    for dy, dx in SHIFTS:
        for k, (y, x) in enumerate(SPOTS):
            cnt[:, k] += 0 <= y - 1 - dy < PATCH and 0 <= x - 1 - dx < PATCH
    cnt = cnt.reshape(-1)
    roles = np.stack([pos != 0, pos == 0])[None].astype(np.float32)
    n = np.arange(EXPERTS)
    valid = (np.arange(TILES) * R)[None, :] + i[:, None] < T
    return {
        "c_ident": np.eye(128, dtype=np.float32), 
        "c_masks": np.stack([mask(same), mask(same & later), mask(same & later.T)], axis=1),
        "c_decay": decay.astype(np.float32), "c_count": cnt, "c_rootcount": np.sqrt(cnt / PD).astype(np.float32),
        "c_roles": roles, "c_cos": cos, "c_sin": sin,
        "c_valid": valid.astype(np.float32), "c_below": (i[:, None] < i[None, :]).astype(np.float32),
        "c_fills": (BLK * np.arange(FILLS)).astype(np.float32),
        "c_blockno": np.arange(max(BLOCKS)).astype(np.float32)[None],
        "c_earlier": (n[None, :] < n[:, None]).astype(np.float32),
    }


def shift_sources():
    src = np.full((5, C, len(SPOTS)), -1)
    for s, (dy, dx) in enumerate(SHIFTS):
        for k, (y, x) in enumerate(SPOTS):
            ph, pw = y - 1 - dy, x - 1 - dx
            if 0 <= ph < PATCH and 0 <= pw < PATCH:
                for c in range(C):
                    src[s, c, k] = (ph * PATCH + pw) * 5 * C + s * C + c
    return src.reshape(5, KT)


def laid_out(x):
    f = {k: np.asarray(v) for k, v in x.items()}
    pad = np.pad(f["x"], ((0, 0), (0, 0), (1, 1), (1, 1)))
    side = IMG // PATCH
    ys, xs = np.array(SPOTS).T
    corner = np.arange(side) * PATCH
    got = pad[:, :, corner[:, None, None] + ys, corner[None, :, None] + xs]
    spots = got.transpose(0, 2, 3, 1, 4).reshape(B, side * side, KT)
    tokens = np.concatenate([np.zeros((B, 1, KT), np.float32), spots], axis=1).reshape(T, KT)
    src = shift_sources()

    def by_spot(v):
        padded = np.concatenate([v, np.zeros_like(v[:1])])
        got = padded[src]
        return np.ascontiguousarray(got.reshape((5, TC, TP) + v.shape[1:]).swapaxes(1, 2).swapaxes(0, 1))

    def halves(v):
        return np.ascontiguousarray(v.reshape(2, KD).T)

    a = {
        "x": np.ascontiguousarray(tokens), "cls_tok": f["cls_tok"].reshape(1, D),
        "wsh": by_spot(f["L0_tok_proj_weight"].T), "gsh": by_spot(f["L0_tok_ln_weight"]),
        "bsh": by_spot(f["L0_tok_ln_bias"]), "tok_bias": f["L0_tok_proj_bias"].reshape(1, D),
        "L0_attn_W_qkv": f["L0_attn_W_qkv"],
        "attn_bqk": np.ascontiguousarray(f["L0_attn_b_qkv"][:2 * D].reshape(4, KD).T),
        "attn_bv": np.ascontiguousarray(f["L0_attn_b_qkv"][2 * D:]),
        "qkv0": f["L0_ffn_qkv_w"], "bqkv0": f["L0_ffn_qkv_b"], "gain0": halves(f["L0_ffn_ln1_g"]),
        "shift0": halves(f["L0_ffn_ln1_b"]), "proj0": f["L0_ffn_proj_w"], "bproj0": f["L0_ffn_proj_b"],
        "gate0": f["L0_ffn_gate_w"], "w1_0": f["L0_ffn_w1"], "w2_0": f["L0_ffn_w2"], "b2_0": f["L0_ffn_b2"],
        "gain2": halves(f["L0_ffn_ln2_g"]), "shift2": halves(f["L0_ffn_ln2_b"]),
        "qkv1": f["L1_attn_W_attn"], "bqkv1": f["L1_attn_b_attn"], "gain1": halves(f["L1_attn_norm_scale"]),
        "shift1": halves(f["L1_attn_norm_bias"]), "proj1": f["L1_attn_W_proj"], "bproj1": f["L1_attn_b_proj"],
        "gate1": f["L1_ffn_Ws"], "w1_1": f["L1_ffn_W1"], "w2_1": f["L1_ffn_W2"], "b2_1": f["L1_ffn_b2"],
        "sinks": f["L1_attn_sinks"], "rezero": f["L1_attn_rezero"],
        "bs": np.stack([np.zeros(EXPERTS, np.float32), f["L1_ffn_bs"]]),
    }
    for l, b1 in enumerate((f["L0_ffn_b1"], f["L1_ffn_b1"])):
        a[f"b1_{l}"] = b1.reshape(1, EXPERTS, FF)
    return a


def kernel(**inputs):
    import concourse.bacc as bacc
    from concourse.bass_utils import run_bass_kernel_spmd

    nc = bacc.Bacc("TRN2", target_bir_lowering=False, num_devices=1)
    arrays = {**laid_out(inputs), **constants()}
    a = {k: nc.dram_tensor(f"in_{k}", v.shape, mybir.dt.from_np(v.dtype), kind="ExternalInput").ap()
         for k, v in arrays.items()}
    out = nc.dram_tensor("out", (T, D), F32, kind="ExternalOutput").ap()
    build(nc, a, out)
    r = run_bass_kernel_spmd(nc, [{f"in_{k}": v for k, v in arrays.items()}], core_ids=[0])
    return r.results[0]["out"].reshape(B, N, D)
```

```python
from contextlib import ExitStack

import numpy as np

import concourse.bass as bass
from concourse import mybir

F32 = mybir.dt.float32
BF16 = mybir.dt.bfloat16
I32 = mybir.dt.int32
ALU = mybir.AluOpType
ACT = mybir.ActivationFunctionType
AX = mybir.AxisListType

B, C, IMG, PATCH = 32, 3, 96, 16
D = 192
N = (IMG // PATCH) ** 2 + 1
T = B * N
R = 3 * N
TILES = -(-T // R)
TAIL = T - (TILES - 1) * R
PAIRS = (TILES - 1) // 2
KD = 96
H, HD = 12, 16
HP = 32
HC = H * HP // 128
QUADS = 128 // HP
SINK_ROW = HD + 4
K1 = R + 1
EXPERTS, FF = 8, 768
FB = FF // 128
SHIFTS = ((0, 0), (0, -1), (0, 1), (-1, 0), (1, 0))
HALO = PATCH + 2
SPOTS = [(i, j) for i in range(HALO) for j in range(HALO)
         if not (i in (0, HALO - 1) and j in (0, HALO - 1))]
KT = C * len(SPOTS)
TC = 8
TP = KT // TC
PD = PATCH * PATCH * 5 * C
EPS = 1e-5
CHUNK = 4
CHUNKS = [range(a, min(a + CHUNK, TILES)) for a in range(0, TILES, CHUNK)]
BLK = 128
PICKS = (2, 1)
BLOCKS = [(k * T - EXPERTS) // BLK + EXPERTS for k in PICKS]
FILLS = -(-T // BLK)
HALF = FF // 2
PER_PASS = (8, 2, 4)


def rows(t):
    return TAIL if t == TILES - 1 else R


class Room:

    def __init__(self, whole):
        self.whole, self.at = whole, 0

    def take(self, shape):
        n = int(np.prod(shape[1:]))
        flat = self.whole[0:shape[0], self.at:self.at + n]
        self.at += n
        assert self.at <= self.whole.shape[1]
        names = "abc"[:len(shape) - 1]
        return flat.rearrange(f"p ({' '.join(names)}) -> p {' '.join(names)}", **dict(zip(names, shape[1:])))


def build(nc, a, out):
    with ExitStack() as ctx:
        def sb(name, shape, dt=F32):
            return ctx.enter_context(nc.sbuf_tensor(name, shape, dt))

        def pb(name, shape, dt=F32):
            return ctx.enter_context(nc.psum_tensor(name, shape, dt))

        def sem(name):
            return ctx.enter_context(nc.semaphore(name))

        ident = sb("ident", [128, 128])
        identb = sb("identb", [K1, K1], BF16)
        causal_q = sb("causal_q", [K1, QUADS, K1], BF16)
        causal_k = sb("causal_k", [K1, QUADS, R], BF16)
        pick = sb("pick", [128, HC, H])
        spread = sb("spread", [H, HC, 128])
        decay = sb("decay", [R, R])
        w2 = sb("w2", [128, FB, EXPERTS, D])
        w2_room = Room(w2[:].rearrange("p b e n -> p (b e n)"))
        count = w2_room.take([R, KT])
        rootcount = w2_room.take([R, KT])
        w1 = sb("w1", [128, 2, EXPERTS, FF])
        wsh = w1[0:TP].rearrange("p c e n -> p (c e n)")[:, 0:5 * TC * D].rearrange("p (s c d) -> p s c d", s=5, c=TC)
        gsh = sb("gsh", [TP, 5, TC])
        bsh = sb("bsh", [TP, 5, TC])
        etok = w2_room.take([TP, TC, D])
        clsrow = sb("clsrow", [1, D])
        tokbias = sb("tokbias", [1, D])
        tokrow = sb("tokrow", [1, D])
        roles = sb("roles", [1, 2, R])
        base = sb("base", [R, D])
        w_a = sb("w_a", [KD, 2, 3 * D])
        bqk_a = sb("bqk_a", [KD, 4])
        bv_a = sb("bv_a", [R, D])
        ropecos = sb("ropecos", [R, HD])
        ropesin = sb("ropesin", [R, HD])
        W = []
        for l in range(2):
            W.append(dict(
                qkv=sb(f"qkv{l}", [KD, 2, 3 * D]), bqkv=sb(f"bqkv{l}", [R, 3 * D]),
                gain=sb(f"gain{l}", [KD, 2]), shift=sb(f"shift{l}", [KD, 2]),
                proj=sb(f"proj{l}", [128, HC, D]),
                gate=sb(f"gate{l}", [KD, 2, EXPERTS]),
                b2=sb(f"b2_{l}", [EXPERTS, D]),
            ))
        gain2 = sb("gain2", [KD, 2])
        shift2 = sb("shift2", [KD, 2])
        sinks = sb("sinks", [128, HC])
        rezero = sb("rezero", [R, 1])
        bs = sb("bs", [R, 2, EXPERTS])

        h = sb("h", [R, TILES, D])
        xall = sb("xall", [R, TILES, D])
        stats_all = sb("stats_all", [R, TILES, 6])
        means = sb("means", [R, TILES, 2])
        variances = sb("variances", [R, TILES])
        roots = sb("roots", [R, TILES, 2])
        logits = sb("logits", [R, TILES, EXPERTS])
        gates = sb("gates", [R, TILES, EXPERTS])
        earlier = sb("earlier", [R, EXPERTS, EXPERTS])
        e_store = sb("e_store", [128, 2 * H * R])
        e_room, other = Room(e_store[:]), Room(e_store[:])
        e = [e_room.take([K1, HC, QUADS, R]) for _ in range(2)]
        masks = Room(e_store[:]).take([K1, 3, K1])
        hb = other.take([BLK, FF])
        cmp = other.take([R, TILES, EXPERTS, EXPERTS])
        cmq = other.take([R, TILES, EXPERTS, EXPERTS])
        rank = sb("rank", [R, TILES, EXPERTS])
        top = sb("top", [R, TILES])
        gsum = sb("gsum", [R, TILES])
        gatesT = sb("gatesT", [EXPERTS, T])
        valid = sb("valid", [R, TILES])
        below = sb("below", [R, R], BF16)
        ones = sb("ones", [R, R], BF16)
        fills = sb("fills", [R, FILLS])
        blockno = sb("blockno", [1, max(BLOCKS)])
        keep = sb("keep", [R, TILES, EXPERTS], BF16)
        nfill = sb("nfill", [R, EXPERTS, FILLS])
        nblocks = sb("nblocks", [R, EXPERTS])
        before = sb("before", [R, EXPERTS, EXPERTS])
        startblock = sb("startblock", [R, EXPERTS])
        endblock = sb("endblock", [R, EXPERTS])
        ended = sb("ended", [1, max(BLOCKS), EXPERTS])
        expertf = sb("expertf", [1, max(BLOCKS)])
        expert = sb("expert", [1, max(BLOCKS)], I32)
        pos = sb("pos", [R, TILES, EXPERTS])
        picked = sb("picked", [R, TILES, EXPERTS])
        slotf = sb("slotf", [R, 2, TILES])
        slot = sb("slot", [R, 2, TILES], I32)
        weight = sb("weight", [R, 2, TILES])
        back = Room(w2_room.whole).take([R, 2, TILES, D])
        xb = sb("xb", [BLK, D])
        xbT = sb("xbT", [KD + 1, 2, BLK])
        scratch = [sb(f"scratch_{p}", [128, 3 * 2 * D]) for p in range(2)]
        rooms0, rooms1 = [Room(x[:]) for x in scratch], [Room(x[:]) for x in scratch]
        room = Room(scratch[0][:])
        hbT = room.take([128, FB, BLK])
        yb = room.take([BLK, D])
        def slots(name, shape, dt=F32):
            return [sb(f"{name}_{p}", shape, dt) for p in range(2)]

        xin = [w2_room.take([R, KT]) for _ in range(2)]
        zin = [w2_room.take([R, KT]) for _ in range(2)]
        yT = [w2_room.take([TP, TC, R]) for _ in range(2)]
        small = slots("small", [R, 16])
        stats = slots("stats", [R, 6])
        minushalf = sb("minushalf", [R, 2])
        xn = slots("xn", [R, D])
        xnT = slots("xnT", [KD, 2, R])
        qkT_a = [x.take([KD, 4, R]) for x in rooms0]
        v_a = [x.take([R, D]) for x in rooms0]
        sT_a = [x.take([R, R]) for x in rooms0]
        qk = [x.take([R, 2 * H, HD]) for x in rooms1]
        rot = [x.take([R, 2 * H, HD]) for x in rooms1]
        rot2 = [x.take([R, 2 * H, HD]) for x in rooms1]
        qkpad = slots("qkpad", [R, 2, H, HP])
        vone = slots("vone", [K1, H, HP])
        kT = slots("kT", [128, HC, K1])
        qT = slots("qT", [128, HC, R])
        kTd = slots("kTd", [128, HC, QUADS, K1])
        qTd = slots("qTd", [128, HC, QUADS, R])
        inverse = slots("inverse", [H, R])
        oTs = qT
        oT = kT

        ps = [pb(f"ps{i}", [128, 2, 512]) for i in range(2)]
        pm = [pb(f"pm{i}", [128, 2, 512]) for i in range(2)]

        first_in = sem("first_in")
        tok_in = sem("tok_in")
        rest_in = sem("rest_in")
        etok_done = sem("etok_done")
        tokrow_mm, tokrow_done, base_mm = (sem(x) for x in ("tokrow_mm", "tokrow_done", "base_mm"))
        pads_set, masks_cast = sem("pads_set"), sem("masks_cast")
        x_in = [sem(f"x_in{p}") for p in range(2)]
        def sems(names, tag=""):
            return {n: sem(n + tag) for n in names.split()}

        A = sems("centred weighted squared tok_var tok_root stats_done var_ready root_done tok_turned "
                 "tok_evac_act tok_evac_dve tok_mm h0_done normed turned kept_stats kept_var rooted "
                 "xnT_done qkv_mm qkv_done score_mm score_done out_mm h1_done", "_a")
        L = sems("kept_stats kept_var rooted normed turned xnT_done qkv_mm qk_added swapped qk_done v_done "
                  "qk_turned kTd_act kTd_dve qT_done kT_done "
                  "score_mm max_done q_turned qTd_act qTd_dve scoreT_mm exp_done pv_mm oTs_done "
                  "sums_mm inverted spread_mm oT_done proj_mm y_done normed2 turned2 xnT2_done logit_mm h_added", "_l")
        M = [sems("logit_done gates_shifted gates_exp gates_done gatesT_mm gatesT_done bias_mm bias_added "
                  "keep_done slots_mm "
                  "experts_found slots_done scattered x_turned xbT_done up_mm gelu_done h_turned hbT_done down_mm "
                  "y_evac h_done", f"_m{l}") for l in range(2)]
        w_in = [sem(f"w_in_{l}") for l in range(2)]
        xb_in = [sem(f"xb_in_{l}") for l in range(2)]
        y_stored = [sem(f"y_stored_{l}") for l in range(2)]
        back_in = [sem(f"back_in_{t}") for t in range(TILES)]
        var_known, roots_done = sem("var_known"), sem("roots_done")
        zero_set, zero_filled = sem("zero_set"), sem("zero_filled")
        dve_step = sem("dve_step")
        pool_step = sem("pool_step")
        out_done = sem("out_done")
        xs = [nc.dram_tensor(f"xs{l}", (BLOCKS[l] * BLK, D), F32, kind="Internal").ap() for l in range(2)]
        ys = [nc.dram_tensor(f"ys{l}", (BLOCKS[l] * BLK, D), F32, kind="Internal").ap() for l in range(2)]
        backs = [16 * PICKS[0], 16 * (PICKS[0] + PICKS[1])]

        block = ctx.enter_context(nc.Block())

        def tile_of(buf, t, n):
            return buf[0:n, t, :] if isinstance(t, int) else buf[0:n, bass.ds(t, 1), :].rearrange("p o d -> p (o d)")

        def hrow(t, n):
            return tile_of(h, t, n)

        def pair(i, l=0):
            return [(0, i * 2, R, i * 2 + l * TILES), (1, i * 2 + 1, R, i * 2 + (1 + l * TILES))]

        def pair_after(i, l=0, ahead=1):
            first = 2 * ahead
            return [(p, i * 2 + (first + p), R, i * 2 + (first + p + l * TILES)) for p in range(2)]

        def tail(l=0):
            return [(0, TILES - 1, TAIL, TILES - 1 + l * TILES)]

        class Steps:

            def __init__(self, eng, s):
                self.eng, self.s, self.base, self.n, self.i, self.per = eng, s, 0, 0, None, 0

            def enter(self, i, per):
                self.base, self.n, self.i, self.per = self.base + self.n, 0, i, per

            def leave(self, passes):
                assert self.n == self.per, (self.n, self.per)
                self.base, self.n, self.i = self.base + passes * self.per, 0, None

            def did(self, ins):
                ins.then_inc(self.s, 1)
                self.n += 1
                return self.n

            def after(self, n):
                v = self.base + n
                self.eng.wait_ge(self.s, v if self.i is None else self.i * self.per + v)

        def two(buf, bank, parts, n):
            return buf[0:parts, bank, 0:2 * R].rearrange("p (c n) -> p c n", c=2)[:, :, 0:n]

        def bias_bank(k):
            return [ps[0][:, 0], ps[0][:, 1], ps[1][:, 0], ps[1][:, 1], pm[0][:, 0], pm[0][:, 1]][k]

        def gatesT_bank(k):
            return [pm[1][:, 0], pm[1][:, 1], ps[1][:, 0]][k]

        def three(buf, bank, n, parts=128):
            return buf[0:parts, bank, 0:HC * R].rearrange("p (c n) -> p c n", c=HC)[:, :, 0:n]

        def two_of_bank(t, n):
            return ps[t % 4 // 2][0:KD, t % 2, 0:2 * R].rearrange("p (c n) -> p c n", c=2)[:, :, 0:n]

        def score_bank(use, parts, m):
            return ps[use % 4 // 2][0:parts, use % 2, 0:QUADS * m].rearrange("p (r m) -> p r m", r=QUADS)

        def own_quadrants(bufd, r, n):
            return bufd[HP * r:HP * (r + 1), :, r, 0:n]

        PADS = 8
        ROOT_CREDIT = 2
        Y_CREDIT = 1
        first_loads = [(count[:], a["c_count"].partition_broadcast(R)), (ident[:], a["c_ident"]),
                       (rootcount[:], a["c_rootcount"].partition_broadcast(R))]
        tok_loads = [(gsh[:], a["gsh"]), (bsh[:], a["bsh"])]
        tok_loads += [(wsh[:, s], a["wsh"][:, s]) for s in range(5)]
        tok_loads += [(roles[:], a["c_roles"]), (clsrow[:], a["cls_tok"]), (tokbias[:], a["tok_bias"])]
        rest_loads = [
            (w_a[:], a["L0_attn_W_qkv"].rearrange("(c p) n -> p c n", p=KD)), (bqk_a[:], a["attn_bqk"]),
            (bv_a[:], a["attn_bv"].partition_broadcast(R)), (decay[:], a["c_decay"]), (masks[:], a["c_masks"]),
            (pick[:], a["c_pick"]), (spread[:], a["c_spread"])]
        for p in range(2):
            rest_loads += [(qkpad[p][:], a["c_pads"]), (vone[p][:], a["c_vone"])]
        for l in range(2):
            w = W[l]
            rest_loads += [
                (w["qkv"][:], a[f"qkv{l}"].rearrange("(c p) n -> p c n", p=KD)),
                (w["bqkv"][:], a[f"bqkv{l}"].partition_broadcast(R)), (w["gain"][:], a[f"gain{l}"]),
                (w["shift"][:], a[f"shift{l}"]), (w["proj"][:], a[f"proj{l}"]),
                (w["gate"][:], a[f"gate{l}"].rearrange("(c p) n -> p c n", p=KD)),
                (w["b2"][:], a[f"b2_{l}"])]
        rest_loads += [(gain2[:], a["gain2"]), (shift2[:], a["shift2"]), (ropecos[:], a["c_cos"]),
                       (ropesin[:], a["c_sin"]), (sinks[:], a["sinks"]),
                       (rezero[:], a["rezero"].partition_broadcast(R)), (bs[:], a["bs"].partition_broadcast(R)),
                       (earlier[:], a["c_earlier"].partition_broadcast(R)), (valid[:], a["c_valid"]),
                       (fills[:], a["c_fills"].partition_broadcast(R)),
                       (blockno[:], a["c_blockno"])]
        FIRST_IN, TOK_IN, REST_IN = (16 * len(x) for x in (first_loads, tok_loads, rest_loads))

        @block.sync
        def _(sp):
            for dst, src in first_loads:
                sp.dma_start(dst, src).then_inc(first_in, 16)
            for dst, src in tok_loads:
                sp.dma_start(dst, src).then_inc(tok_in, 16)
            for dst, src in rest_loads:
                sp.dma_start(dst, src).then_inc(rest_in, 16)

            sp.wait_ge(zero_set, 1)
            for l in range(2):
                sp.dma_start(xs[l].rearrange("(b p) d -> p b d", p=BLK),
                             xb[:].unsqueeze(1).to_broadcast((BLK, BLOCKS[l], D))).then_inc(zero_filled, 16)

            def load_w1(l):
                for c in range(2):
                    sp.dma_start(w1[0:KD, c], a[f"w1_{l}"][:, c * KD:(c + 1) * KD, :].rearrange("e p n -> p e n")
                                 ).then_inc(w_in[l], 16)
                sp.dma_start(w1[KD:KD + 1, 0], a[f"b1_{l}"]).then_inc(w_in[l], 16)

            def load_w2(l):
                for b in range(FB):
                    sp.dma_start(w2[:, b], a[f"w2_{l}"][:, b * 128:(b + 1) * 128, :].rearrange("e p n -> p e n")
                                 ).then_inc(w_in[l], 16)

            def load_block(l, b):
                at = slice(b * BLK, (b + 1) * BLK) if isinstance(b, int) else bass.ds(b * BLK, BLK)
                if not isinstance(b, int) or b:
                    sp.wait_ge(M[l]["x_turned"], b)
                sp.dma_start(xb[:], xs[l][at, :]).then_inc(xb_in[l], 16)

            def store_block(l, b):
                at = slice(b * BLK, (b + 1) * BLK) if isinstance(b, int) else bass.ds(b * BLK, BLK)
                sp.wait_ge(M[l]["y_evac"], Y_CREDIT + b + 1)
                sp.dma_start(ys[l][at, :], yb[:]).then_inc(y_stored[l], 16)

            def blocks(l):
                n = BLOCKS[l]
                sp.wait_ge(M[l]["scattered"], 16 * PICKS[l] * TILES)
                for b in range(3):
                    load_block(l, b)
                with sp.Fori(0, n - 3) as b:
                    load_block(l, b + 3)
                    store_block(l, b)
                for b in range(n - 3, n):
                    store_block(l, b)

            sp.wait_ge(etok_done, TC)
            sp.wait_ge(tokrow_mm, 1)
            load_w1(0)
            sp.wait_ge(A["h1_done"], TILES)
            for p in range(2):
                sp.wait_ge(x_in[p], 16 * (PAIRS + 1))
            load_w2(0)
            blocks(0)
            sp.wait_ge(M[0]["h_done"], TILES)
            load_w1(1)
            load_w2(1)
            blocks(1)
            full = (TILES - 1) * R
            sp.wait_ge(M[1]["h_done"], TILES - 1)
            sp.dma_start(out[0:full, :].rearrange("(t p) d -> p t d", p=R), h[:, 0:TILES - 1, :]
                         ).then_inc(out_done, 16)
            sp.wait_ge(M[1]["h_done"], TILES)
            sp.dma_start(out[full:T, :], h[0:TAIL, TILES - 1, :]).then_inc(out_done, 16)
            sp.wait_ge(out_done, 32)

        @block.scalar
        def _(act):
            def copy(dst, src):
                return nc.scalar.activation(dst, src, ACT.Copy)

            def affine(dst, src, gain, shift, n):
                for c in range(2):
                    last = nc.scalar.activation(dst[:, c, 0:n], src[:, c, 0:n], ACT.Identity,
                                                bias=shift[:, c:c + 1], scale=gain[:, c:c + 1])
                return last

            def tokens(tiles):
                for p, t, n, _ in tiles:
                    act.wait_ge(A["tok_turned"], t + 1)
                    copy(yT[p][:, 0:4, 0:n], ps[p][0:TP, 0, 0:4 * R].rearrange("p (c n) -> p c n", c=4)[:, :, 0:n]
                         ).then_inc(A["tok_evac_act"], 1)
                for p, t, n, _ in tiles:
                    act.wait_ge(A["weighted"], t + 1)
                    nc.scalar.activation(zin[p][0:n], zin[p][0:n], ACT.Square,
                                         accum_out=small[p][0:n, 7:8]).then_inc(A["squared"], 1)

            def load_pixels(p, t):
                at = slice(t * R, (t + 1) * R) if isinstance(t, int) else bass.ds(t * R, R)
                act.dma_start(xin[p][:], a["x"][at, :]).then_inc(x_in[p], 16)

            def decay_attention(tiles, following=()):
                for p, t, n, _ in tiles:
                    act.wait_ge(A["turned"], t + 1)
                    copy(xnT[p][:, :, 0:n], two(pm[p], 0, KD, n)).then_inc(A["xnT_done"], 1)
                tokens(following)

            def project(l, tiles):
                for p, t, n, k in tiles:
                    act.wait_ge(L["turned"], k + 1)
                    affine(xnT[p], two(ps[p], 0, KD, n), W[l]["gain"], W[l]["shift"], n
                           ).then_inc(L["xnT_done"], 1)

            def heads_attention(l, tiles, following=()):
                s = L
                for p, t, n, k in tiles:
                    act.wait_ge(s["qk_turned"], k + 1)
                    for r in range(QUADS - 1):
                        last = copy(own_quadrants(kTd[p], r, n), three(pm[p], 0, n)[HP * r:HP * (r + 1)])
                    last.then_inc(s["kTd_act"], 1)
                for p, t, n, k in tiles:
                    act.wait_ge(s["kTd_dve"], k + 1)
                    copy(kT[p][:, :, 0:n], three(pm[p], 0, n)).then_inc(s["kT_done"], 1)
                for p, t, n, k in tiles:
                    act.wait_ge(s["q_turned"], k + 1)
                    for r in range(QUADS - 1):
                        last = copy(own_quadrants(qTd[p], r, n), three(pm[p], 1, n)[HP * r:HP * (r + 1)])
                    last.then_inc(s["qTd_act"], 1)
                for p, t, n, k in tiles:
                    for c in range(HC):
                        act.wait_ge(s["scoreT_mm"], k * HC + (c + 1))
                        nc.scalar.activation(e[p][0:n + l, c, :, 0:n], score_bank(6 + 3 * p + c, n + l, n), ACT.Exp,
                                             scale=HD ** -0.5).then_inc(s["exp_done"], 1)
                for p, t, n, k in tiles:
                    act.wait_ge(s["pv_mm"], k + 1)
                    copy(oTs[p][:, :, 0:n], three(pm[p], 0, n)).then_inc(s["oTs_done"], 1)
                project(l, following)

            def route(l):
                for t in range(TILES):
                    k, n = t + l * TILES, rows(t)
                    act.wait_ge(L["turned2"], k + 1)
                    if t >= 2:
                        act.wait_ge(L["logit_mm"], k - 1)
                    src = two_of_bank(t, n)
                    if l == 0:
                        last = affine(xnT[t % 2], src, gain2, shift2, n)
                    else:
                        last = copy(xnT[t % 2][:, :, 0:n], src)
                    last.then_inc(L["xnT2_done"], 1)

            def experts(l):
                m = M[l]
                act.wait_ge(m["gates_shifted"], 1)
                nc.scalar.activation(gates[:], gates[:], ACT.Exp).then_inc(m["gates_exp"], 1)
                with act.Fori(0, BLOCKS[l]) as b:
                    for half in range(2):
                        act.wait_ge(m["up_mm"], b * 2 + (half + 1))
                        nc.scalar.activation(hb[:, half * HALF:(half + 1) * HALF], ps[0][:, half, 0:HALF], ACT.Gelu
                                             ).then_inc(m["gelu_done"], 1)

            for p in range(2):
                load_pixels(p, p)
            tokens(pair(0))
            for p in range(2):
                load_pixels(p, p + 2)
            act.wait_ge(rest_in, REST_IN)
            with act.Fori(0, PAIRS - 1) as i:
                decay_attention(pair(i), pair_after(i))
                for p in range(2):
                    load_pixels(p, i * 2 + (p + 4))
            decay_attention(pair(PAIRS - 1), tail())
            decay_attention(tail())
            project(0, pair(0))
            with act.Fori(0, PAIRS - 1) as i:
                heads_attention(0, pair(i, 0), pair_after(i, 0))
            heads_attention(0, pair(PAIRS - 1, 0), tail(0))
            heads_attention(0, tail(0))
            route(0)
            experts(0)
            project(1, pair(0, 1))
            with act.Fori(0, PAIRS - 1) as i:
                heads_attention(1, pair(i, 1), pair_after(i, 1))
            heads_attention(1, pair(PAIRS - 1, 1), tail(1))
            heads_attention(1, tail(1))
            route(1)
            experts(1)

        @block.gpsimd
        def _(pool):
            for p in range(2):
                nc.gpsimd.memset(kTd[p][:], 0.0).then_inc(pads_set, 1)
                nc.gpsimd.memset(qTd[p][:], 0.0).then_inc(pads_set, 1)
            nc.gpsimd.memset(logits[:], 0.0).then_inc(pads_set, 1)
            nc.gpsimd.memset(means[:], 0.0).then_inc(pads_set, 1)
            nc.gpsimd.memset(minushalf[:], -0.5).then_inc(pool_step, 1)
            nc.gpsimd.memset(xb[:], 0.0).then_inc(zero_set, 1)
            nc.gpsimd.memset(ones[:], 1.0).then_inc(pads_set, 1)
            pool.wait_ge(pool_step, 1)
            pool.wait_ge(first_in, FIRST_IN)

            def root(tiles, ready, done, src, dst, m=1):
                for p, t, n, k in tiles:
                    pool.wait_ge(ready, k + 1)
                    nc.gpsimd.tensor_tensor(small[p][0:n, dst:dst + m], small[p][0:n, src:src + m],
                                            minushalf[0:n, 0:m], ALU.pow).then_inc(done, 1)

            def pixels(tiles):
                for p, t, n, _ in tiles:
                    pool.wait_ge(A["centred"], t + 1)
                    nc.gpsimd.tensor_tensor(zin[p][0:n], xin[p][0:n], rootcount[0:n], ALU.mult
                                            ).then_inc(A["weighted"], 1)

            def tokens(tiles):
                root(tiles, A["tok_var"], A["tok_root"], 8, 9)

            def kept_roots(tiles, s, m):
                for p, t, n, k in tiles:
                    pool.wait_ge(s["kept_var"], k + 1)
                    nc.gpsimd.tensor_tensor(tile_of(roots, t, n)[:, 0:m], small[p][0:n, 12:12 + m],
                                            minushalf[0:n, 0:m], ALU.pow).then_inc(s["rooted"], 1)

            def decay_attention(tiles, following=(), previous=()):
                root(tiles, A["var_ready"], A["root_done"], 2, 4)
                pixels(following)
                kept_roots(previous, A, 2)
                tokens(following)

            def rotate(tiles):
                for p, t, n, k in tiles:
                    pool.wait_ge(L["qk_added"], t + 1)
                    for c in range(2):
                        nc.gpsimd.tensor_tensor(
                            rot2[p][0:n, :, c::2], qk[p][0:n, :, 1 - c::2],
                            ropesin[0:n, c::2].unsqueeze(1).to_broadcast((n, 2 * H, HD // 2)), ALU.mult
                        ).then_inc(L["swapped"], 1)

            def heads_attention(l, tiles, following=()):
                s = L
                if l == 1:
                    rotate(following)
                if l == 0:
                    for p, t, n, k in tiles:
                        pool.wait_ge(s["y_done"], k + 1)
                        nc.gpsimd.tensor_tensor(hrow(t, n), hrow(t, n), tile_of(xall, t, n), ALU.add
                                                ).then_inc(s["h_added"], 1)
                kept_roots(tiles, s, 1)

            def experts(l):
                m = M[l]
                pool.wait_ge(m["slots_done"], 1)
                pool.wait_ge(zero_filled, 32)
                pool.wait_ge(L["normed2"], (l + 1) * TILES)
                for t in range(TILES):
                    for j in range(PICKS[l]):
                        at = bass.IndirectOffsetOnAxis(ap=slot[0:rows(t), j, t:t + 1], axis=0)
                        nc.gpsimd.indirect_dma_start(out=xs[l], out_offset=at, in_=xall[0:rows(t), t, :],
                                                     in_offset=None).then_inc(m["scattered"], 16)
                pool.wait_ge(y_stored[l], 16 * (Y_CREDIT + BLOCKS[l]))
                for t in range(TILES):
                    for j in range(PICKS[l]):
                        at = bass.IndirectOffsetOnAxis(ap=slot[0:rows(t), j, t:t + 1], axis=0)
                        nc.gpsimd.indirect_dma_start(out=back[0:rows(t), j, t, :], out_offset=None, in_=ys[l],
                                                     in_offset=at).then_inc(back_in[t], 16)
                if l == 0:
                    pool.wait_ge(var_known, 1)
                    nc.gpsimd.tensor_tensor(roots[:, :, 0], variances[:], minushalf[:, 0:1].to_broadcast((R, TILES)),
                                            ALU.pow).then_inc(roots_done, 1)

            pixels(pair(0))
            pool.wait_ge(rest_in, REST_IN)
            tokens(pair(0))
            decay_attention(pair(0), pair(1))
            with pool.Fori(0, PAIRS - 2) as i:
                decay_attention(pair_after(i), pair_after(i, ahead=2), pair(i))
            decay_attention(pair(PAIRS - 1), tail(), pair(PAIRS - 2))
            decay_attention(tail(), (), pair(PAIRS - 1))
            kept_roots(tail(), A, 2)
            with pool.Fori(0, PAIRS - 1) as i:
                heads_attention(0, pair(i, 0), pair_after(i, 0))
            heads_attention(0, pair(PAIRS - 1, 0), tail(0))
            heads_attention(0, tail(0))
            experts(0)
            rotate(pair(0, 1))
            with pool.Fori(0, PAIRS - 1) as i:
                heads_attention(1, pair(i, 1), pair_after(i, 1))
            heads_attention(1, pair(PAIRS - 1, 1), tail(1))
            heads_attention(1, tail(1))
            experts(1)

        @block.vector
        def _(dve):
            V = nc.vector
            st = Steps(dve, dve_step)

            def wait_alone(ready, value):
                dve.wait_ge(pads_set, PADS)
                dve.wait_ge(ready, value)

            def row_stats(tiles, src, ready, stats_done, done):
                at = {}
                for p, t, n, k in tiles:
                    wait_alone(ready, k + 1)
                    V.bn_stats(stats[p][0:n], src(p, t, n)).then_inc(stats_done, 1)
                for p, t, n, k in tiles:
                    wait_alone(stats_done, k + 1)
                    at[p] = st.did(V.bn_aggr(small[p][0:n, 0:2], stats[p][0:n]))
                for p, t, n, k in tiles:
                    st.after(at[p])
                    ins = V.tensor_scalar(small[p][0:n, 2:3], small[p][0:n, 1:2], EPS, None, ALU.add)
                    if done is None:
                        at[p] = st.did(ins)
                    else:
                        ins.then_inc(done, 1)
                return at

            def normalise(tiles, src, dst, ready, stats_done, var_ready, root_done, done):
                row_stats(tiles, src, ready, stats_done, var_ready)
                for p, t, n, k in tiles:
                    dve.wait_ge(root_done, k + 1)
                    V.tensor_scalar(dst[p][0:n], src(p, t, n), small[p][0:n, 0:1], small[p][0:n, 4:5],
                                    ALU.subtract, ALU.mult).then_inc(done, 1)

            def from_h(p, t, n):
                return hrow(t, n)

            def pixels(tiles, loads):
                at = {}
                for p, t, n, _ in tiles:
                    dve.wait_ge(x_in[p], loads * 16)
                    at[p] = st.did(V.tensor_tensor_reduce(zin[p][0:n], xin[p][0:n], count[0:n], 1.0 / PD, 0.0,
                                                          ALU.mult, ALU.add, small[p][0:n, 6:7]))
                for p, t, n, _ in tiles:
                    st.after(at[p])
                    V.tensor_scalar(xin[p][0:n], xin[p][0:n], small[p][0:n, 6:7], None, ALU.subtract
                                    ).then_inc(A["centred"], 1)

            def tokens_turned(tiles):
                for p, t, n, _ in tiles:
                    dve.wait_ge(A["tok_turned"], t + 1)
                    V.tensor_copy(yT[p][:, 4:8, 0:n], ps[p][0:TP, 1, 0:4 * R].rearrange(
                        "p (c n) -> p c n", c=4)[:, :, 0:n]).then_inc(A["tok_evac_dve"], 1)

            def tokens(tiles):
                for p, t, n, _ in tiles:
                    dve.wait_ge(A["squared"], t + 1)
                    V.tensor_scalar(small[p][0:n, 8:9], small[p][0:n, 7:8], EPS, None, ALU.add
                                    ).then_inc(A["tok_var"], 1)
                for p, t, n, _ in tiles:
                    dve.wait_ge(A["tok_root"], t + 1)
                    dve.wait_ge(A["tok_mm"], t + 1)
                    V.scalar_tensor_tensor(hrow(t, n), ps[p][0:n, 0, 0:D], small[p][0:n, 9:10], base[0:n],
                                           ALU.mult, ALU.add).then_inc(A["h0_done"], 1)

            def keep_stats(tiles, src, ready, s, twice):
                at = {}
                for p, t, n, k in tiles:
                    wait_alone(ready, k + 1)
                    V.bn_stats(stats[p][0:n], src(p, t, n)).then_inc(s["kept_stats"], 1)
                for p, t, n, k in tiles:
                    wait_alone(s["kept_stats"], k + 1)
                    at[p] = st.did(V.bn_aggr(small[p][0:n, 10:12], stats[p][0:n]))
                for p, t, n, k in tiles:
                    st.after(at[p])
                    dve.wait_ge(s["rooted"], k + 1)
                    V.tensor_copy(tile_of(means, t, n), small[p][0:n, 10:12])
                    ins = V.tensor_scalar(small[p][0:n, 12:13], small[p][0:n, 11:12], EPS, None, ALU.add)
                    if twice:
                        at[p] = st.did(ins)
                    else:
                        ins.then_inc(s["kept_var"], 1)
                if twice:
                    for p, t, n, k in tiles:
                        st.after(at[p])
                        V.scalar_tensor_tensor(small[p][0:n, 13:14], small[p][0:n, 12:13], EPS, small[p][0:n, 11:12],
                                               ALU.mult, ALU.add).then_inc(s["kept_var"], 1)

            def decay_attention(tiles, following=(), loads=None, previous=()):
                normalise(tiles, from_h, xn, A["h0_done"], A["stats_done"], A["var_ready"], A["root_done"], A["normed"])
                pixels(following, loads)
                keep_stats(previous, from_h, A["h1_done"], A, True)
                for p, t, n, _ in tiles:
                    dve.wait_ge(A["qkv_mm"], t + 1)
                    V.tensor_tensor(qkT_a[p][:, :, 0:n],
                                    pm[p][0:KD, 0, 0:4 * R].rearrange("p (c n) -> p c n", c=4)[:, :, 0:n],
                                    bqk_a[:].unsqueeze(2).to_broadcast((KD, 4, n)), ALU.add
                                    ).then_inc(A["qkv_done"], 1)
                    V.tensor_tensor(v_a[p][0:n], pm[p][0:n, 1, 0:D], bv_a[0:n], ALU.add).then_inc(A["qkv_done"], 1)
                for p, t, n, _ in tiles:
                    dve.wait_ge(A["score_mm"], t + 1)
                    V.tensor_tensor(sT_a[p][0:n, 0:n], pm[p][0:n, 0, 0:n], decay[0:n, 0:n], ALU.mult
                                    ).then_inc(A["score_done"], 1)
                tokens_turned(following)
                for p, t, n, _ in tiles:
                    dve.wait_ge(A["out_mm"], t + 1)
                    V.tensor_tensor(hrow(t, n), hrow(t, n), pm[p][0:n, 1, 0:D], ALU.add).then_inc(A["h1_done"], 1)
                tokens(following)

            def normed(l, tiles):
                for p, t, n, k in tiles:
                    V.tensor_scalar(xn[p][0:n], hrow(t, n), tile_of(means, t, n)[:, 0:1],
                                    tile_of(roots, t, n)[:, 1 - l:2 - l], ALU.subtract, ALU.mult
                                    ).then_inc(L["normed"], 1)
                    if l == 0:
                        V.tensor_scalar(tile_of(xall, t, n), hrow(t, n), tile_of(means, t, n)[:, 0:1],
                                        tile_of(roots, t, n)[:, 0:1], ALU.subtract, ALU.mult)

            def qkv_added(l, tiles):
                s, w = L, W[l]
                for p, t, n, k in tiles:
                    dve.wait_ge(s["qkv_mm"], k + 1)
                    acc = ps[p][0:n, 0, 0:2 * D].rearrange("p (h d) -> p h d", d=HD)
                    bias = w["bqkv"][0:n, 0:2 * D].rearrange("p (h d) -> p h d", d=HD)
                    dst = qkpad[p][0:n, :, :, 0:HD].rearrange("p a h d -> p (a h) d") if l == 0 else qk[p][0:n]
                    V.tensor_tensor(dst, acc, bias, ALU.add).then_inc(s["qk_done" if l == 0 else "qk_added"], 1)
                    V.memset(qkpad[p][0:n, 0, :, HD], 0.0)
                    if l == 1 and n == TAIL:
                        st.did(V.memset(vone[p][64:K1, :, 0:HD], 0.0))
                        st.after(st.n)
                    V.tensor_tensor(vone[p][0:n, :, 0:HD], ps[p][0:n, 1, 0:D].rearrange(
                        "p (h d) -> p h d", d=HD), w["bqkv"][0:n, 2 * D:3 * D].rearrange("p (h d) -> p h d", d=HD),
                        ALU.add).then_inc(s["v_done"], 1)

            def rotate(tiles):
                s, at = L, {}
                for p, t, n, k in tiles:
                    dve.wait_ge(s["qk_added"], t + 1)
                    at[p] = st.did(V.tensor_tensor(rot[p][0:n], qk[p][0:n],
                                                   ropecos[0:n].unsqueeze(1).to_broadcast((n, 2 * H, HD)), ALU.mult))
                for p, t, n, k in tiles:
                    st.after(at[p])
                    dve.wait_ge(s["swapped"], t * 2 + 2)
                    V.tensor_tensor(qkpad[p][0:n, :, :, 0:HD].rearrange("p a h d -> p (a h) d"),
                                    rot[p][0:n], rot2[p][0:n], ALU.add).then_inc(s["qk_done"], 1)

            def keep_y_stats(l, tiles):
                keep_stats(tiles, from_h if l else (lambda p, t, n: tile_of(xall, t, n)), L["y_done"], L, False)

            def heads_attention(l, tiles, following=(), previous=()):
                s = L
                for p, t, n, k in tiles:
                    dve.wait_ge(s["qk_turned"], k + 1)
                    r = QUADS - 1
                    V.tensor_copy(own_quadrants(kTd[p], r, n), three(pm[p], 0, n)[HP * r:HP * (r + 1)]
                                  ).then_inc(s["kTd_dve"], 1)
                    V.tensor_copy(qT[p][:, :, 0:n], three(pm[p], 1, n)).then_inc(s["qT_done"], 1)
                for p, t, n, k in tiles:
                    for c in range(HC):
                        dve.wait_ge(s["score_mm"], k * HC + (c + 1))
                        V.tensor_reduce(qkpad[p][0:n, 0, QUADS * c:QUADS * (c + 1), HD],
                                        score_bank(3 * p + c, n, n + l), AX.X, ALU.max, negate=True
                                        ).then_inc(s["max_done"], 1)
                for p, t, n, k in tiles:
                    dve.wait_ge(s["q_turned"], k + 1)
                    r = QUADS - 1
                    V.tensor_copy(own_quadrants(qTd[p], r, n), three(pm[p], 1, n)[HP * r:HP * (r + 1)]
                                  ).then_inc(s["qTd_dve"], 1)
                normed(l, following)
                keep_y_stats(l, previous)
                for p, t, n, k in tiles:
                    dve.wait_ge(s["sums_mm"], k + 1)
                    V.reciprocal(inverse[p][:, 0:n], pm[p][0:H, 1, 0:n]).then_inc(s["inverted"], 1)
                for p, t, n, k in tiles:
                    dve.wait_ge(s["spread_mm"], k + 1)
                    V.tensor_tensor(oT[p][:, :, 0:n], oTs[p][:, :, 0:n], three(pm[p], 1, n), ALU.mult
                                    ).then_inc(s["oT_done"], 1)
                for p, t, n, k in tiles:
                    dve.wait_ge(s["proj_mm"], k + 1)
                    if l == 0:
                        V.tensor_tensor(tile_of(xall, t, n), pm[p][0:n, 0, 0:D], tile_of(xall, t, n), ALU.add
                                        ).then_inc(s["y_done"], 1)
                    else:
                        V.scalar_tensor_tensor(hrow(t, n), pm[p][0:n, 0, 0:D], rezero[0:n, 0:1], hrow(t, n),
                                               ALU.mult, ALU.add).then_inc(s["y_done"], 1)
                qkv_added(l, following)
                if l == 1:
                    rotate(following)

            def all_variances(at, ready):
                for t in range(TILES):
                    st.after(at[t])
                    n = st.did(V.bn_aggr(means[0:rows(t), t], stats_all[0:rows(t), t]))
                st.after(n)
                V.tensor_scalar(variances[:], means[:, :, 1], EPS, None, ALU.add).then_inc(ready, 1)

            def route(l):
                m, src = M[l], xall if l == 0 else h
                dve.wait_ge(L["rooted"], (l + 1) * TILES + ROOT_CREDIT)
                if l == 0:
                    dve.wait_ge(L["h_added"], TILES)
                for t in range(TILES):
                    n = rows(t)
                    V.tensor_scalar(xall[0:n, t], src[0:n, t], means[0:n, t, 0:1], roots[0:n, t, 0:1],
                                    ALU.subtract, ALU.mult).then_inc(L["normed2"], 1)
                dve.wait_ge(L["logit_mm"], (l + 1) * TILES)
                full = TILES - 1
                for n, tiles in ((R, slice(0, full)), (TAIL, slice(full, TILES))):
                    count = tiles.stop - tiles.start
                    V.tensor_tensor(logits[0:n, tiles], pm[0][0:n, 0, 0:TILES * EXPERTS].rearrange(
                        "r (t e) -> r t e", t=TILES)[:, tiles], bs[0:n, l].unsqueeze(1).to_broadcast(
                        (n, count, EXPERTS)), ALU.add).then_inc(m["logit_done"], 1)

            def choose(l):
                m = M[l]
                shape = (R, TILES, EXPERTS, EXPERTS)
                mine = logits[:].unsqueeze(3).to_broadcast(shape)
                other = logits[:].unsqueeze(2).to_broadcast(shape)
                dve.wait_ge(m["logit_done"], 2)
                n = st.did(V.tensor_reduce(top[:], logits[:], AX.X, ALU.max))
                st.after(n)
                V.tensor_tensor(gates[:], logits[:], top[:].unsqueeze(2).to_broadcast((R, TILES, EXPERTS)),
                                ALU.subtract).then_inc(m["gates_shifted"], 1)
                st.did(V.tensor_tensor(cmp[:], other, mine, ALU.is_gt))
                n = st.did(V.tensor_tensor(cmq[:], other, mine, ALU.is_equal))
                st.after(n)
                n = st.did(V.tensor_tensor(cmq[:], cmq[:], earlier[:].unsqueeze(1).to_broadcast(shape), ALU.mult))
                st.after(n)
                n = st.did(V.tensor_tensor(cmp[:], cmp[:], cmq[:], ALU.add))
                st.after(n)
                n = st.did(V.tensor_reduce(rank[:], cmp[:], AX.X, ALU.add))
                st.after(n)
                V.scalar_tensor_tensor(keep[:], rank[:], PICKS[l] - 0.5, valid[:].unsqueeze(2).to_broadcast(
                    (R, TILES, EXPERTS)), ALU.is_lt, ALU.mult).then_inc(m["keep_done"], 1)
                dve.wait_ge(m["gates_exp"], 1)
                if l == 1:
                    st.did(V.tensor_reduce(gsum[:], gates[:], AX.X, ALU.add))
                    st.after(st.n)
                dve.wait_ge(m["keep_done"], 1)
                n = st.did(V.tensor_tensor(gates[:], keep[:], gates[:], ALU.mult))
                st.after(n)
                if l == 0:
                    n = st.did(V.tensor_reduce(gsum[:], gates[:], AX.X, ALU.add))
                    st.after(n)
                    n = st.did(V.tensor_scalar(gsum[:], gsum[:], 1e-30, None, ALU.max))
                    st.after(n)
                n = st.did(V.reciprocal(gsum[:], gsum[:]))
                st.after(n)
                V.tensor_tensor(gates[:], gates[:], gsum[:].unsqueeze(2).to_broadcast((R, TILES, EXPERTS)),
                                ALU.mult).then_inc(m["gates_done"], 1)

            def find_slots(l):
                m = M[l]
                each = (R, TILES, EXPERTS)
                dve.wait_ge(m["slots_mm"], 1)
                taken, placed = ps[0][0:R, 1, 0:EXPERTS], ps[0][0:R, 0, 0:TILES * EXPERTS].rearrange(
                    "r (t e) -> r t e", e=EXPERTS)
                n = st.did(V.tensor_tensor(nfill[:], taken.unsqueeze(2).to_broadcast((R, EXPERTS, FILLS)),
                                           fills[:].unsqueeze(1).to_broadcast((R, EXPERTS, FILLS)), ALU.is_gt))
                st.after(n)
                n = st.did(V.tensor_reduce(nblocks[:], nfill[:], AX.X, ALU.add))
                st.after(n)
                n = st.did(V.tensor_tensor(before[:], earlier[:], nblocks[:].unsqueeze(1).to_broadcast(
                    (R, EXPERTS, EXPERTS)), ALU.mult))
                st.after(n)
                n = st.did(V.tensor_reduce(startblock[:], before[:], AX.X, ALU.add))
                st.after(n)
                n = st.did(V.scalar_tensor_tensor(pos[:], startblock[:].unsqueeze(1).to_broadcast(each), float(BLK),
                                                  placed, ALU.mult, ALU.add))
                for j in range(PICKS[l]):
                    st.after(n)
                    n = st.did(V.scalar_tensor_tensor(picked[:], rank[:], float(j), pos[:], ALU.is_equal, ALU.mult))
                    st.after(n)
                    n = st.did(V.tensor_reduce(slotf[:, j], picked[:], AX.X, ALU.add))
                st.after(n)
                V.tensor_copy(slot[:, 0:PICKS[l]], slotf[:, 0:PICKS[l]]).then_inc(m["slots_done"], 1)
                nb = BLOCKS[l]
                n = st.did(V.tensor_tensor(endblock[:], startblock[:], nblocks[:], ALU.add))
                st.after(n)
                n = st.did(V.tensor_tensor(ended[:, 0:nb], endblock[0:1].unsqueeze(1).to_broadcast((1, nb, EXPERTS)),
                                           blockno[:, 0:nb].unsqueeze(2).to_broadcast((1, nb, EXPERTS)), ALU.is_le))
                st.after(n)
                n = st.did(V.tensor_reduce(expertf[:, 0:nb], ended[:, 0:nb], AX.X, ALU.add))
                st.after(n)
                V.tensor_scalar(expert[:, 0:nb], expertf[:, 0:nb], EXPERTS - 1.0, None, ALU.min
                                ).then_inc(m["experts_found"], 1)

            def slot_weights(l):
                for j in range(PICKS[l]):
                    st.after(st.n)
                    n = st.did(V.scalar_tensor_tensor(picked[:], rank[:], float(j), gates[:], ALU.is_equal, ALU.mult))
                    st.after(n)
                    n = st.did(V.tensor_reduce(weight[:, j], picked[:], AX.X, ALU.add))
                st.after(n)

            def experts(l):
                m = M[l]
                choose(l)
                find_slots(l)
                dve.wait_ge(m["gates_done"], 1)
                slot_weights(l)
                for k, tiles in enumerate(CHUNKS):
                    n = sum(rows(t) for t in tiles)
                    dve.wait_ge(m["gatesT_mm"], k + 1)
                    V.tensor_copy(gatesT[:, tiles[0] * R:tiles[0] * R + n], gatesT_bank(k)[0:EXPERTS, 0:n]
                                  ).then_inc(m["gatesT_done"], 1)
                dve.wait_ge(m["bias_mm"], TILES)
                for t in range(TILES):
                    n = rows(t)
                    V.tensor_tensor(h[0:n, t, :], bias_bank(t // 2)[0:n, t % 2 * D:(t % 2 + 1) * D], h[0:n, t, :],
                                    ALU.add).then_inc(m["bias_added"], 1)
                dve.sem_inc(m["y_evac"], Y_CREDIT)
                dve.sem_inc(y_stored[l], 16 * Y_CREDIT)

                def rows_turned(b):
                    dve.wait_ge(m["x_turned"], b + 1)
                    src = pm[0][0:KD, 0, 0:2 * BLK].rearrange("p (c n) -> p c n", c=2)
                    if l == 1:
                        V.tensor_copy(xbT[0:KD], src).then_inc(m["xbT_done"], 2)
                        return
                    for c in range(2):
                        V.tensor_scalar(xbT[0:KD, c], src[:, c], gain2[:, c:c + 1], shift2[:, c:c + 1],
                                        ALU.mult, ALU.add).then_inc(m["xbT_done"], 1)

                def block(b, ahead):
                    dve.wait_ge(m["h_turned"], b + 1)
                    V.tensor_copy(hbT[:], ps[1][:].rearrange("p k n -> p (k n)")[:, 0:FF].rearrange(
                        "p (k n) -> p k n", k=FB)).then_inc(m["hbT_done"], 1)
                    if ahead:
                        rows_turned(b + 2)
                    dve.wait_ge(m["down_mm"], b + 1)
                    dve.wait_ge(y_stored[l], b * 16 + 16 * Y_CREDIT)
                    V.tensor_copy(yb[:], pm[0][:, 1, 0:D]).then_inc(m["y_evac"], 1)

                for b in range(2):
                    rows_turned(b)
                with dve.Fori(0, BLOCKS[l] - 2) as b:
                    block(b, True)
                for b in range(BLOCKS[l] - 2, BLOCKS[l]):
                    block(b, False)
                at = []
                for t in range(TILES):
                    dve.wait_ge(back_in[t], backs[l])
                    n = rows(t)
                    for j in range(PICKS[l]):
                        ins = V.scalar_tensor_tensor(h[0:n, t, :], back[0:n, j, t, :], weight[0:n, j, t:t + 1],
                                                     h[0:n, t, :], ALU.mult, ALU.add)
                        if j == PICKS[l] - 1:
                            ins.then_inc(m["h_done"], 1)
                        else:
                            st.did(ins)
                            st.after(st.n)
                    if l == 0:
                        dve.wait_ge(m["h_done"], t + 1)
                        at.append(st.did(V.bn_stats(stats_all[0:n, t], h[0:n, t])))
                if l == 0:
                    all_variances(at, var_known)
                    dve.wait_ge(roots_done, 1)

            dve.wait_ge(first_in, FIRST_IN)
            pixels(pair(0), 1)
            tokens_turned(pair(0))
            V.memset(xbT[KD:KD + 1, 0], 1.0).then_inc(pads_set, 1)
            dve.wait_ge(tok_in, TOK_IN)
            at = {}
            for s in range(5):
                for c in range(TC):
                    if s == 0:
                        at[c] = st.did(V.tensor_scalar(etok[:, c], wsh[:, s, c], gsh[:, s, c:c + 1], None, ALU.mult))
                        continue
                    st.after(at[c])
                    ins = V.scalar_tensor_tensor(etok[:, c], wsh[:, s, c], gsh[:, s, c:c + 1], etok[:, c],
                                                 ALU.mult, ALU.add)
                    if s < 4:
                        at[c] = st.did(ins)
                    else:
                        ins.then_inc(etok_done, 1)
            dve.wait_ge(tokrow_mm, 1)
            V.tensor_tensor(tokrow[:], pm[0][0:1, 0, 0:D], tokbias[:], ALU.add).then_inc(tokrow_done, 1)
            dve.wait_ge(base_mm, 1)
            n = st.did(V.tensor_copy(base[:], pm[0][0:R, 1, 0:D]))
            st.after(n)
            dve.wait_ge(pads_set, PADS)
            dve.wait_ge(rest_in, REST_IN)
            V.tensor_copy(identb[:], ident[0:K1, 0:K1]).then_inc(masks_cast, 1)
            for k, (m, cols) in enumerate(((causal_q, K1), (causal_k, R))):
                V.tensor_copy(m[:], masks[:, k, 0:cols].unsqueeze(1).to_broadcast((K1, QUADS, cols))
                              ).then_inc(masks_cast, 1)
            V.tensor_copy(below[:], masks[0:R, 2, 0:R]).then_inc(masks_cast, 1)
            sinks_scaled = st.did(V.tensor_scalar(sinks[:], sinks[:], HD ** 0.5, None, ALU.mult))

            def sink_key(p, n):
                st.did(V.tensor_copy(kT[p][:, :, n], sinks[:]))
                for r in range(QUADS):
                    st.did(V.tensor_copy(kTd[p][HP * r:HP * (r + 1), :, r, n], sinks[HP * r:HP * (r + 1)]))
            tokens(pair(0))
            dve.sem_inc(A["rooted"], ROOT_CREDIT)
            dve.sem_inc(L["rooted"], ROOT_CREDIT)
            decay_attention(pair(0), pair(1), 2)
            with dve.Fori(0, PAIRS - 2) as i:
                st.enter(i, PER_PASS[0])
                decay_attention(pair_after(i), pair_after(i, ahead=2), i + 3, pair(i))
                st.leave(PAIRS - 2)
            decay_attention(pair(PAIRS - 1), tail(), PAIRS + 1, pair(PAIRS - 2))
            decay_attention(tail(), previous=pair(PAIRS - 1))
            keep_stats(tail(), from_h, A["h1_done"], A, True)
            dve.wait_ge(A["rooted"], TILES + ROOT_CREDIT)
            normed(0, pair(0))
            qkv_added(0, pair(0))
            heads_attention(0, pair(0), pair(1))
            with dve.Fori(0, PAIRS - 2) as i:
                st.enter(i, PER_PASS[1])
                heads_attention(0, pair_after(i), pair_after(i, ahead=2), pair(i))
                st.leave(PAIRS - 2)
            heads_attention(0, pair(PAIRS - 1), tail(), pair(PAIRS - 2))
            heads_attention(0, tail(), (), pair(PAIRS - 1))
            keep_y_stats(0, tail())
            route(0)
            experts(0)
            for p in range(2):
                sink_key(p, R)
            st.after(st.n)
            normed(1, pair(0, 1))
            qkv_added(1, pair(0, 1))
            rotate(pair(0, 1))
            heads_attention(1, pair(0, 1), pair(1, 1))
            with dve.Fori(0, PAIRS - 2) as i:
                st.enter(i, PER_PASS[2])
                heads_attention(1, pair_after(i, 1), pair_after(i, 1, 2), pair(i, 1))
                st.leave(PAIRS - 2)
            heads_attention(1, pair(PAIRS - 1, 1), tail(1), pair(PAIRS - 2, 1))
            sink_key(0, TAIL)
            st.after(st.n)
            heads_attention(1, tail(1), (), pair(PAIRS - 1, 1))
            keep_y_stats(1, tail(1))
            route(1)
            experts(1)

        @block.tensor
        def _(pe):
            def mm(dst, lhsT, rhs, first=True, last=True):
                return nc.tensor.matmul(dst, lhsT, rhs, start=first, stop=last, skip_group_check=True)

            def turn(dst, src, n):
                return nc.tensor.transpose(dst, src, ident[0:n, 0:n])

            def turn_pixels(tiles):
                for p, t, n, _ in tiles:
                    pe.wait_ge(A["centred"], t + 1)
                    for c in range(TC):
                        last = turn(ps[p][0:TP, c // 4, c % 4 * R:c % 4 * R + n],
                                    xin[p][0:n, c * TP:(c + 1) * TP], n)
                    last.then_inc(A["tok_turned"], 1)

            def tokens(tiles):
                for p, t, n, _ in tiles:
                    pe.wait_ge(A["tok_evac_act"], t + 1)
                    pe.wait_ge(A["tok_evac_dve"], t + 1)
                    for c in range(TC):
                        last = mm(ps[p][0:n, 0, 0:D], yT[p][:, c, 0:n], etok[:, c], c == 0, c == TC - 1)
                    last.then_inc(A["tok_mm"], 1)

            def turn_rows(tiles, banks, ready, done):
                for p, t, n, k in tiles:
                    pe.wait_ge(ready, k + 1)
                    for c in range(2):
                        last = turn(banks[p][0:KD, 0, c * R:c * R + n], xn[p][0:n, c * KD:(c + 1) * KD], n)
                    last.then_inc(done, 1)

            def turn_normed(tiles):
                turn_rows(tiles, ps, L["normed"], L["turned"])

            def project(l, tiles):
                w = W[l]
                for p, t, n, k in tiles:
                    pe.wait_ge(L["xnT_done"], k + 1)
                    for c in range(2):
                        mm(ps[p][0:n, 0, 0:2 * D], xnT[p][:, c, 0:n], w["qkv"][:, c, 0:2 * D], c == 0, c == 1)
                    for c in range(2):
                        last = mm(ps[p][0:n, 1, 0:D], xnT[p][:, c, 0:n], w["qkv"][:, c, 2 * D:3 * D],
                                  c == 0, c == 1)
                    last.then_inc(L["qkv_mm"], 1)

            def decay_attention(tiles, following=()):
                turn_rows(tiles, pm, A["normed"], A["turned"])
                for p, t, n, _ in tiles:
                    pe.wait_ge(A["xnT_done"], t + 1)
                    for j in range(4):
                        for c in range(2):
                            mm(pm[p][0:KD, 0, j * R:j * R + n], w_a[:, c, j * KD:(j + 1) * KD], xnT[p][:, c, 0:n],
                               c == 0, c == 1)
                    for c in range(2):
                        last = mm(pm[p][0:n, 1, 0:D], xnT[p][:, c, 0:n], w_a[:, c, 2 * D:3 * D], c == 0, c == 1)
                    last.then_inc(A["qkv_mm"], 1)
                turn_pixels(following)
                for p, t, n, _ in tiles:
                    pe.wait_ge(A["qkv_done"], t * 2 + 2)
                    for c in range(2):
                        last = mm(pm[p][0:n, 0, 0:n], qkT_a[p][:, 2 + c, 0:n], qkT_a[p][:, c, 0:n], c == 0, c == 1)
                    last.then_inc(A["score_mm"], 1)
                tokens(following[0:1])
                for p, t, n, _ in tiles:
                    pe.wait_ge(A["score_done"], t + 1)
                    mm(pm[p][0:n, 1, 0:D], sT_a[p][0:n, 0:n], v_a[p][0:n]).then_inc(A["out_mm"], 1)
                tokens(following[1:])

            def chunk_scores(dst, mask, left, right):
                if mask is not None:
                    mm(dst, identb[0:mask.shape[0], 0:dst.shape[0]], mask, True, False)
                return mm(dst, left, right, mask is None, True)

            def heads_attention(l, tiles, following=()):
                s, w = L, W[l]
                def turn_heads(p, n, which, bank):
                    src = qkpad[p][0:n, which].rearrange("p (c r) d -> p c (r d)", c=HC)
                    for c in range(HC):
                        last = turn(pm[p][:, bank, c * R:c * R + n], src[:, c], n)
                    return last

                for p, t, n, k in tiles:
                    pe.wait_ge(s["qk_done"], k + 1)
                    pe.wait_ge(s["v_done"], k + 1)
                    turn_heads(p, n, 1, 0)
                    turn_heads(p, n, 0, 1).then_inc(s["qk_turned"], 1)
                for p, t, n, k in tiles:
                    pe.wait_ge(s["kTd_act"], k + 1)
                    pe.wait_ge(s["qT_done"], k + 1)
                    m = n + l
                    for c in range(HC):
                        if p == 1 and c:
                            pe.wait_ge(s["max_done"], k * HC - (HC - c))
                        chunk_scores(score_bank(3 * p + c, n, m), causal_q[0:n, :, 0:m] if l else None,
                                     qT[p][:, c, 0:n], kTd[p][:, c, :, 0:m]).then_inc(s["score_mm"], 1)
                for p, t, n, k in tiles:
                    pe.wait_ge(s["max_done"], k * HC + HC)
                    turn_heads(p, n, 0, 1).then_inc(s["q_turned"], 1)
                for p, t, n, k in tiles:
                    pe.wait_ge(s["kT_done"], k + 1)
                    pe.wait_ge(s["qTd_act"], k + 1)
                    pe.wait_ge(s["qTd_dve"], k + 1)
                    m = n + l
                    for c in range(HC):
                        if p == 1 and c:
                            pe.wait_ge(s["exp_done"], k * HC - (HC - c))
                        chunk_scores(score_bank(6 + 3 * p + c, m, n), causal_k[0:m, :, 0:n] if l else None,
                                     kT[p][:, c, 0:m], qTd[p][:, c, :, 0:n]).then_inc(s["scoreT_mm"], 1)
                for p, t, n, k in tiles:
                    for c in range(HC):
                        pe.wait_ge(s["exp_done"], k * HC + (c + 1))
                        for r in range(QUADS):
                            last = mm(pm[p][HP * r:HP * (r + 1), 0, c * R:c * R + n],
                                      vone[p][0:n + l, QUADS * c + r], e[p][0:n + l, c, r, 0:n])
                    last.then_inc(s["pv_mm"], 1)
                turn_normed(following)
                for p, t, n, k in tiles:
                    pe.wait_ge(s["oTs_done"], k + 1)
                    for c in range(HC):
                        last = mm(pm[p][0:H, 1, 0:n], pick[:, c], oTs[p][:, c, 0:n], c == 0, c == HC - 1)
                    last.then_inc(s["sums_mm"], 1)
                project(l, following[0:1])
                for p, t, n, k in tiles:
                    pe.wait_ge(s["inverted"], k + 1)
                    for c in range(HC):
                        last = mm(three(pm[p], 1, n)[:, c], spread[:, c], inverse[p][:, 0:n])
                    last.then_inc(s["spread_mm"], 1)
                for p, t, n, k in tiles:
                    pe.wait_ge(s["oT_done"], k + 1)
                    for c in range(HC):
                        last = mm(pm[p][0:n, 0, 0:D], oT[p][:, c, 0:n], w["proj"][:, c], c == 0, c == HC - 1)
                    last.then_inc(s["proj_mm"], 1)
                project(l, following[1:])

            def route(l):
                def turn_tile(t):
                    k, n = t + l * TILES, rows(t)
                    pe.wait_ge(L["normed2"], k + 1)
                    if t >= 4:
                        pe.wait_ge(L["xnT2_done"], k - 3)
                    for c in range(2):
                        last = turn(two_of_bank(t, n)[:, c], xall[0:n, t, c * KD:(c + 1) * KD], n)
                    last.then_inc(L["turned2"], 1)

                turn_tile(0)
                turn_tile(1)
                for t in range(TILES):
                    k, n = t + l * TILES, rows(t)
                    if t + 2 < TILES:
                        turn_tile(t + 2)
                    pe.wait_ge(L["xnT2_done"], k + 1)
                    for c in range(2):
                        last = mm(pm[0][0:n, 0, t * EXPERTS:(t + 1) * EXPERTS], xnT[t % 2][:, c, 0:n],
                                  W[l]["gate"][:, c], c == 0, c == 1)
                    last.then_inc(L["logit_mm"], 1)

            def experts(l):
                m = M[l]
                pe.wait_ge(m["keep_done"], 1)
                mm(ps[0][0:R, 0, 0:TILES * EXPERTS], below[:], keep[:].rearrange("r t e -> r (t e)"), True, False)
                for t in range(TILES - 1):
                    later = TILES - 1 - t
                    mm(ps[0][0:R, 0, (t + 1) * EXPERTS:TILES * EXPERTS].rearrange("r (t e) -> r t e", e=EXPERTS),
                       ones[:], keep[:, t].unsqueeze(1).to_broadcast((R, later, EXPERTS)), False, t == TILES - 2)
                for t in range(TILES):
                    last = mm(ps[0][0:R, 1, 0:EXPERTS], ones[:], keep[:, t], t == 0, t == TILES - 1)
                last.then_inc(m["slots_mm"], 1)
                pe.wait_ge(m["gates_done"], 1)
                for k, tiles in enumerate(CHUNKS):
                    for j, t in enumerate(tiles):
                        last = turn(gatesT_bank(k)[0:EXPERTS, j * R:j * R + rows(t)], gates[0:rows(t), t, :], rows(t))
                    last.then_inc(m["gatesT_mm"], 1)
                pe.wait_ge(m["gatesT_done"], len(CHUNKS))
                pe.wait_ge(m["experts_found"], 1)
                for t in range(TILES):
                    mm(bias_bank(t // 2)[0:rows(t), t % 2 * D:(t % 2 + 1) * D], gatesT[:, t * R:t * R + rows(t)],
                       W[l]["b2"][:]).then_inc(m["bias_mm"], 1)
                pe.wait_ge(m["bias_added"], TILES)
                pe.wait_ge(w_in[l], 16 * (3 + FB))

                def expert_of(b):
                    one = slice(b, b + 1) if isinstance(b, int) else bass.ds(b, 1)
                    return bass.ds(pe.value_load(expert[:, one], min_val=0, max_val=EXPERTS - 1), 1)

                def turn_x(b):
                    pe.wait_ge(xb_in[l], b * 16 + 16)
                    for c in range(2):
                        last = turn(pm[0][0:KD, 0, c * BLK:(c + 1) * BLK], xb[:, c * KD:(c + 1) * KD], BLK)
                    last.then_inc(m["x_turned"], 1)

                def up(b):
                    e = expert_of(b)
                    pe.wait_ge(m["xbT_done"], b * 2 + 2)
                    for half in range(2):
                        cols = slice(half * HALF, (half + 1) * HALF)
                        mm(ps[0][:, half, 0:HALF], xbT[:, 0], w1[0:KD + 1, 0, e, cols].rearrange("p o n -> p (o n)"),
                           True, False)
                        mm(ps[0][:, half, 0:HALF], xbT[0:KD, 1], w1[0:KD, 1, e, cols].rearrange("p o n -> p (o n)"),
                           False, True).then_inc(m["up_mm"], 1)

                def turn_h(b):
                    pe.wait_ge(m["gelu_done"], b * 2 + 2)
                    for k in range(FB):
                        last = turn(ps[1][:, k // 4, k % 4 * BLK:(k % 4 + 1) * BLK], hb[:, k * 128:(k + 1) * 128], BLK)
                    last.then_inc(m["h_turned"], 1)

                def down(b):
                    e = expert_of(b)
                    pe.wait_ge(m["hbT_done"], b + 1)
                    pe.wait_ge(m["y_evac"], b + Y_CREDIT)
                    for k in range(FB):
                        last = mm(pm[0][:, 1, 0:D], hbT[:, k], w2[:, k, e].rearrange("p o n -> p (o n)"),
                                  k == 0, k == FB - 1)
                    last.then_inc(m["down_mm"], 1)

                turn_x(0)
                up(0)
                turn_x(1)
                with pe.Fori(0, BLOCKS[l] - 2) as b:
                    turn_h(b)
                    up(b + 1)
                    turn_x(b + 2)
                    down(b)
                b = BLOCKS[l] - 2
                turn_h(b)
                up(b + 1)
                down(b)
                turn_h(b + 1)
                down(b + 1)

            pe.wait_ge(first_in, FIRST_IN)
            turn_pixels(pair(0))
            pe.wait_ge(tok_in, TOK_IN)
            for s in range(5):
                for c in range(TC):
                    last = mm(pm[0][0:1, 0, 0:D], bsh[:, s, c:c + 1], wsh[:, s, c], s + c == 0, s + c == TC + 3)
            last.then_inc(tokrow_mm, 1)
            pe.wait_ge(tokrow_done, 1)
            mm(pm[0][0:R, 1, 0:D], roles[:, 0, :], tokrow[:], True, False)
            mm(pm[0][0:R, 1, 0:D], roles[:, 1, :], clsrow[:], False, True).then_inc(base_mm, 1)
            pe.wait_ge(etok_done, TC)
            pe.wait_ge(pads_set, PADS)
            pe.wait_ge(rest_in, REST_IN)
            pe.wait_ge(masks_cast, 4)
            tokens(pair(0))
            with pe.Fori(0, PAIRS - 1) as i:
                decay_attention(pair(i), pair_after(i))
            decay_attention(pair(PAIRS - 1), tail())
            decay_attention(tail())
            turn_normed(pair(0))
            project(0, pair(0))
            with pe.Fori(0, PAIRS - 1) as i:
                heads_attention(0, pair(i, 0), pair_after(i, 0))
            heads_attention(0, pair(PAIRS - 1, 0), tail(0))
            heads_attention(0, tail(0))
            route(0)
            experts(0)
            turn_normed(pair(0, 1))
            project(1, pair(0, 1))
            with pe.Fori(0, PAIRS - 1) as i:
                heads_attention(1, pair(i, 1), pair_after(i, 1))
            heads_attention(1, pair(PAIRS - 1, 1), tail(1))
            heads_attention(1, tail(1))
            route(1)
            experts(1)


def constants():
    i = np.arange(R)
    image, pos = i // N, i % N
    same = image[:, None] == image[None, :]
    later = pos[:, None] >= pos[None, :]
    decay = np.where(same.T & later.T, np.float32(0.99) ** (pos[None, :] - pos[:, None]).clip(0).astype(np.float32),
                     np.float32(0)) / np.sqrt(np.float32(D))

    causal = np.zeros((3, K1, K1), np.float32)
    causal[0, :R, :R] = np.where(same & (pos[None, :] > pos[:, None]), -1e30, 0)
    causal[1] = causal[0].T
    causal[2, :R, :R] = i[:, None] < i[None, :]
    pads = np.zeros((R, 2, H, HP), np.float32)
    pads[:, 1, :, HD] = 1
    for k in range(3):
        pads[:, 0, :, HD + 1 + k] = (image == k)[:, None]
        pads[:, 1, :, HD + 1 + k] = np.where(image == k, 0, -1e30)[:, None]
    pads[:, 0, :, SINK_ROW] = 1
    vone = np.zeros((K1, H, HP), np.float32)
    vone[:, :, HD] = 1
    row = np.arange(128)
    head = np.arange(HC)[:, None] * QUADS + row[None, :] // HP
    spread = head[None] == np.arange(H)[:, None, None]
    pick = spread.transpose(2, 1, 0) & (row % HP == HD)[:, None, None]
    freqs = np.float32(1.0) / np.float32(10000.0) ** (np.arange(0, HD, 2, dtype=np.float32) / np.float32(HD))
    ang = pos[:, None].astype(np.float32) * freqs[None, :].astype(np.float32)
    cos = np.repeat(np.cos(ang), 2, axis=1).astype(np.float32)
    sin = np.repeat(np.sin(ang), 2, axis=1).astype(np.float32)
    sin[:, 0::2] *= -1
    cnt = np.zeros((C, len(SPOTS)), np.float32)
    for dy, dx in SHIFTS:
        for k, (y, x) in enumerate(SPOTS):
            cnt[:, k] += 0 <= y - 1 - dy < PATCH and 0 <= x - 1 - dx < PATCH
    cnt = cnt.reshape(-1)
    roles = np.stack([pos != 0, pos == 0])[None].astype(np.float32)
    n = np.arange(EXPERTS)
    valid = (np.arange(TILES) * R)[None, :] + i[:, None] < T
    return {
        "c_ident": np.eye(128, dtype=np.float32),
        "c_masks": np.ascontiguousarray(causal.swapaxes(0, 1)),
        "c_pads": pads, "c_vone": vone, "c_spread": spread.astype(np.float32),
        "c_pick": np.ascontiguousarray(pick).astype(np.float32),
        "c_decay": decay.astype(np.float32), "c_count": cnt, "c_rootcount": np.sqrt(cnt / PD).astype(np.float32),
        "c_roles": roles, "c_cos": cos, "c_sin": sin,
        "c_valid": valid.astype(np.float32),
        "c_fills": (BLK * np.arange(FILLS)).astype(np.float32),
        "c_blockno": np.arange(max(BLOCKS)).astype(np.float32)[None],
        "c_earlier": (n[None, :] < n[:, None]).astype(np.float32),
    }


def shift_sources():
    src = np.full((5, C, len(SPOTS)), -1)
    for s, (dy, dx) in enumerate(SHIFTS):
        for k, (y, x) in enumerate(SPOTS):
            ph, pw = y - 1 - dy, x - 1 - dx
            if 0 <= ph < PATCH and 0 <= pw < PATCH:
                for c in range(C):
                    src[s, c, k] = (ph * PATCH + pw) * 5 * C + s * C + c
    return src.reshape(5, KT)


def laid_out(x):
    f = {k: np.asarray(v) for k, v in x.items()}
    pad = np.pad(f["x"], ((0, 0), (0, 0), (1, 1), (1, 1)))
    side = IMG // PATCH
    ys, xs = np.array(SPOTS).T
    corner = np.arange(side) * PATCH
    got = pad[:, :, corner[:, None, None] + ys, corner[None, :, None] + xs]
    spots = got.transpose(0, 2, 3, 1, 4).reshape(B, side * side, KT)
    tokens = np.concatenate([np.zeros((B, 1, KT), np.float32), spots], axis=1).reshape(T, KT)
    tokens = np.pad(tokens, ((0, 2 * (PAIRS + 1) * R - T), (0, 0)))
    src = shift_sources()

    def by_spot(v):
        padded = np.concatenate([v, np.zeros_like(v[:1])])
        got = padded[src]
        return np.ascontiguousarray(got.reshape((5, TC, TP) + v.shape[1:]).swapaxes(1, 2).swapaxes(0, 1))

    def halves(v):
        return np.ascontiguousarray(v.reshape(2, KD).T)

    def by_heads(v, bias):
        padded = np.zeros((HC, QUADS, HP, D), v.dtype)
        padded[:, :, :HD] = v.reshape(HC, QUADS, HD, D)
        padded[0, 0, HD] = bias
        return np.ascontiguousarray(padded.reshape(HC, 128, D).swapaxes(0, 1))

    sinks = np.zeros((QUADS, HP, HC), np.float32)
    sinks[:, HD] = HD ** -0.5
    sinks[:, SINK_ROW] = f["L1_attn_sinks"].reshape(HC, QUADS).T
    a = {
        "x": np.ascontiguousarray(tokens), "cls_tok": f["cls_tok"].reshape(1, D),
        "wsh": by_spot(f["L0_tok_proj_weight"].T), "gsh": by_spot(f["L0_tok_ln_weight"]),
        "bsh": by_spot(f["L0_tok_ln_bias"]), "tok_bias": f["L0_tok_proj_bias"].reshape(1, D),
        "L0_attn_W_qkv": f["L0_attn_W_qkv"],
        "attn_bqk": np.ascontiguousarray(f["L0_attn_b_qkv"][:2 * D].reshape(4, KD).T),
        "attn_bv": np.ascontiguousarray(f["L0_attn_b_qkv"][2 * D:]),
        "qkv0": f["L0_ffn_qkv_w"], "bqkv0": f["L0_ffn_qkv_b"], "gain0": halves(f["L0_ffn_ln1_g"]),
        "shift0": halves(f["L0_ffn_ln1_b"]), "proj0": by_heads(f["L0_ffn_proj_w"], f["L0_ffn_proj_b"]),
        "gate0": f["L0_ffn_gate_w"], "w1_0": f["L0_ffn_w1"], "w2_0": f["L0_ffn_w2"], "b2_0": f["L0_ffn_b2"],
        "gain2": halves(f["L0_ffn_ln2_g"]), "shift2": halves(f["L0_ffn_ln2_b"]),
        "qkv1": f["L1_attn_W_attn"], "bqkv1": f["L1_attn_b_attn"], "gain1": halves(f["L1_attn_norm_scale"]),
        "shift1": halves(f["L1_attn_norm_bias"]), "proj1": by_heads(f["L1_attn_W_proj"], f["L1_attn_b_proj"]),
        "gate1": f["L1_ffn_Ws"], "w1_1": f["L1_ffn_W1"], "w2_1": f["L1_ffn_W2"], "b2_1": f["L1_ffn_b2"],
        "sinks": sinks.reshape(128, HC), "rezero": f["L1_attn_rezero"],
        "bs": np.stack([np.zeros(EXPERTS, np.float32), f["L1_ffn_bs"]]),
    }
    for l, b1 in enumerate((f["L0_ffn_b1"], f["L1_ffn_b1"])):
        a[f"b1_{l}"] = b1.reshape(1, EXPERTS, FF)
    return a


def kernel(**inputs):
    import concourse.bacc as bacc
    from concourse.bass_utils import run_bass_kernel_spmd

    nc = bacc.Bacc("TRN2", target_bir_lowering=False, num_devices=1)
    arrays = {**laid_out(inputs), **constants()}
    a = {k: nc.dram_tensor(f"in_{k}", v.shape, mybir.dt.from_np(v.dtype), kind="ExternalInput").ap()
         for k, v in arrays.items()}
    out = nc.dram_tensor("out", (T, D), F32, kind="ExternalOutput").ap()
    build(nc, a, out)
    r = run_bass_kernel_spmd(nc, [{f"in_{k}": v for k, v in arrays.items()}], core_ids=[0])
    return r.results[0]["out"].reshape(B, N, D)
```
